# Optimizing a Trainium2 kernel written in Bass

```python
import numpy as np
import jax
import jax.numpy as jnp

def _softmax(x, axis=-1):
    return jax.nn.softmax(x, axis=axis)

def _gelu(x):
    return jax.nn.gelu(x, approximate=True)

def _silu(x):
    return jax.nn.silu(x)

def _sigmoid(x):
    return jax.nn.sigmoid(x)

def _layernorm(x, axis=-1, eps=1e-05):
    m = jnp.mean(x, axis=axis, keepdims=True)
    v = jnp.var(x, axis=axis, keepdims=True)
    return (x - m) / jnp.sqrt(v + eps)

def _scatter_add(tgt, idx, src, axis=0):
    return tgt.at[idx].add(src)

def _segment_sum(src, seg, n):
    return jax.ops.segment_sum(src, seg, n)
kernel_name = 'mk_pixart_resid_d4_seqx_r4_f63876'

def setup_inputs(seed: int=0):
    np.random.seed(seed)
    _w = jnp.asarray

    def _rec_inputs():
        import jax
        import jax.numpy as jnp
        _rk = jax.random.key(seed)
        x = 7.22e-05 + 1 * jax.random.normal(jax.random.fold_in(_rk, 1), (8, 512, 256), jnp.float32)
        _lenS = 512 - jax.random.randint(jax.random.fold_in(_rk, 7), (8,), 0, max(1, 512 // 4) + 1, jnp.int32)
        _lenS2 = 64 - jax.random.randint(jax.random.fold_in(_rk, 8), (8,), 0, max(1, 64 // 4) + 1, jnp.int32)
        _ctx_1024P = jax.random.normal(jax.random.fold_in(_rk, 11), (8, 16, 256), jnp.float32)
        _ctx_1024c = jax.random.dirichlet(jax.random.fold_in(_rk, 511), 0.3 * jnp.ones((16,), jnp.float32), (8, 64))
        _ctx_1024t = jnp.einsum('bsk,bkd->bsd', _ctx_1024c, _ctx_1024P)
        _ctx_1024t = _ctx_1024t * jax.lax.rsqrt(jnp.mean(jnp.square(_ctx_1024t)) + 1e-12) * 0.953939
        ctx_1024 = 4.13588e-05 + 0.999923 * (_ctx_1024t + 0.3 * jax.random.normal(jax.random.fold_in(_rk, 611), (8, 64, 256), jnp.float32))
        condB_tau = jax.random.uniform(jax.random.fold_in(_rk, 12), (8,), jnp.float32, 0.0, 1.45372)
        fside_BxS2_0 = 0.0088954 + 1.00633 * jax.random.normal(jax.random.fold_in(_rk, 13), (8, 64), jnp.float32)
        condB_pt = jax.random.uniform(jax.random.fold_in(_rk, 15), (8,), jnp.float32, 0.0, 226.919)
        return (x, ctx_1024, condB_tau, fside_BxS2_0, condB_pt, _lenS2)
    x, ctx_1024, condB_tau, fside_BxS2_0, condB_pt, _lenS2 = _rec_inputs()

    def _L0_xcond_setup():
        import jax, jax.numpy as jnp
        import numpy as np
        D_MODEL = 256
        N_HEADS = 16
        key = jax.random.key(seed)
        ks = jax.random.split(key, 16)
        B, L, S, D = (4, 512, 512, D_MODEL)
        inp = {'q': jax.random.normal(ks[0], (B, L, D), jnp.float32), 'k': jax.random.normal(ks[1], (B, S, D), jnp.float32), 'v': jax.random.normal(ks[2], (B, S, D), jnp.float32), 'tau': jax.random.uniform(ks[3], (B, 1), jnp.float32, 0.5, 1.5), 'delta': jax.random.normal(ks[4], (B, S), jnp.float32)}
        s = 1.0 / np.sqrt(D)
        inp['Wq'] = jax.random.normal(ks[5], (D, D), jnp.float32) * s
        inp['bq'] = jnp.zeros((D,), jnp.float32)
        inp['Wk'] = jax.random.normal(ks[6], (D, D), jnp.float32) * s
        inp['bk'] = jnp.zeros((D,), jnp.float32)
        inp['Wv'] = jax.random.normal(ks[7], (D, D), jnp.float32) * s
        inp['bv'] = jnp.zeros((D,), jnp.float32)
        inp['Wo'] = jax.random.normal(ks[8], (D, D), jnp.float32) * s
        inp['bo'] = jnp.zeros((D,), jnp.float32)
        return inp
    _L0_xcond_all = _L0_xcond_setup()
    _L0_xcond_in = {k: v for k, v in _L0_xcond_all.items() if k in ('Wq', 'bq', 'Wk', 'bk', 'Wv', 'bv', 'Wo', 'bo')}
    del _L0_xcond_all

    def _L0_ffn_setup():
        import jax, jax.numpy as jnp
        import numpy as np
        DIM = 256
        E = 8
        K = 2
        EPS = 1e-05

        def _ln(x, g, b):
            mu = jnp.mean(x, axis=-1, keepdims=True)
            var = jnp.mean(jnp.square(x - mu), axis=-1, keepdims=True)
            return (x - mu) * jax.lax.rsqrt(var + EPS) * g + b
        key = jax.random.key(seed)
        ks = jax.random.split(key, 8)
        H = 2 * DIM
        s_in = 1.0 / np.sqrt(DIM)
        s_h = 1.0 / np.sqrt(H)
        return {'x': jax.random.normal(ks[0], (2, 512, DIM), dtype=jnp.float32), 'gate_w': jax.random.uniform(ks[1], (DIM, E), minval=-s_in, maxval=s_in, dtype=jnp.float32), 'w1': jax.random.uniform(ks[2], (E, DIM, H), minval=-s_in, maxval=s_in, dtype=jnp.float32), 'b1': jax.random.uniform(ks[3], (E, H), minval=-s_in, maxval=s_in, dtype=jnp.float32), 'ln1_g': jnp.ones((E, H), dtype=jnp.float32), 'ln1_b': jnp.zeros((E, H), dtype=jnp.float32), 'w2': jax.random.uniform(ks[4], (E, H, DIM), minval=-s_h, maxval=s_h, dtype=jnp.float32), 'b2': jax.random.uniform(ks[5], (E, DIM), minval=-s_h, maxval=s_h, dtype=jnp.float32), 'ln_g': jnp.ones((DIM,), dtype=jnp.float32), 'ln_b': jnp.zeros((DIM,), dtype=jnp.float32)}
    _L0_ffn_all = _L0_ffn_setup()
    _L0_ffn_in = {k: v for k, v in _L0_ffn_all.items() if k in ('gate_w', 'w1', 'b1', 'ln1_g', 'ln1_b', 'w2', 'b2', 'ln_g', 'ln_b')}
    del _L0_ffn_all

    def _L1_xcond_setup():
        import jax, jax.numpy as jnp
        import numpy as np
        B, S, D, H = (2, 512, 256, 16)
        DK = D // H

        def _split_heads(x):
            b, s, _ = x.shape
            return x.reshape(b, s, H, DK).transpose(0, 2, 1, 3)
        key = jax.random.key(seed)
        ks = jax.random.split(key, 14)
        inp = {'query': jax.random.normal(ks[0], (B, S, D), jnp.float32), 'key': jax.random.normal(ks[1], (B, S, D), jnp.float32), 'value': jax.random.normal(ks[2], (B, S, D), jnp.float32), 'tau': jax.random.uniform(ks[3], (B, 1), jnp.float32, 0.5, 1.5), 'delta': jax.random.normal(ks[4], (B, S), jnp.float32)}
        sc = 1.0 / np.sqrt(D)
        for i, name in enumerate(['q', 'k', 'v', 'o']):
            inp[f'W{name}'] = jax.random.normal(ks[5 + 2 * i], (D, D), jnp.float32) * sc
            inp[f'b{name}'] = jax.random.normal(ks[6 + 2 * i], (D,), jnp.float32) * 0.01
        return inp
    _L1_xcond_all = _L1_xcond_setup()
    _L1_xcond_in = {k: v for k, v in _L1_xcond_all.items() if k in ('Wq', 'bq', 'Wk', 'bk', 'Wv', 'bv', 'Wo', 'bo')}
    del _L1_xcond_all

    def _L1_ffn_setup():
        import jax, jax.numpy as jnp
        import numpy as np
        B, S, D_MODEL, D_FF = (4, 512, 256, 1024)

        def _quantum_transform(hidden, theta, w_real, w_imag):
            imag = w_imag * jnp.sin(theta + hidden * 0.1)
            quantum_phase = jnp.cos(theta) * w_real + jnp.sin(theta) * w_imag
            return hidden + quantum_phase * imag * 0.1
        key = jax.random.key(seed)
        ks = jax.random.split(key, 8)
        return {'x': jax.random.normal(ks[0], (B, S, D_MODEL), dtype=jnp.float32), 'W1': jax.random.normal(ks[1], (D_MODEL, D_FF), dtype=jnp.float32) * (1.0 / np.sqrt(D_MODEL)), 'b1': jnp.zeros((D_FF,), dtype=jnp.float32), 'quantum_phases': jax.random.normal(ks[2], (D_FF,), dtype=jnp.float32) * (2.0 * np.pi), 'quantum_weights_real': jax.random.normal(ks[3], (D_FF,), dtype=jnp.float32) * 0.1, 'quantum_weights_imag': jax.random.normal(ks[4], (D_FF,), dtype=jnp.float32) * 0.1, 'W2': jax.random.normal(ks[5], (D_FF, D_MODEL), dtype=jnp.float32) * (1.0 / np.sqrt(D_FF)), 'b2': jnp.zeros((D_MODEL,), dtype=jnp.float32)}
    _L1_ffn_all = _L1_ffn_setup()
    _L1_ffn_in = {k: v for k, v in _L1_ffn_all.items() if k in ('W1', 'b1', 'quantum_phases', 'quantum_weights_real', 'quantum_weights_imag', 'W2', 'b2')}
    del _L1_ffn_all

    def _L2_xcond_setup():
        import jax, jax.numpy as jnp
        import numpy as np
        N, L, H, Q = (64, 258, 256, 64)
        WINDOW = 16.0
        DEV_POW = 128.0
        key = jax.random.key(seed)
        k1, k2, k3, k4, k5, k6 = jax.random.split(key, 6)
        encoder_outputs = jax.random.normal(k1, (N, L, H), dtype=jnp.float32)
        decoder_h_t = jax.random.normal(k2, (N, Q, H), dtype=jnp.float32)
        src_len = jax.random.randint(k3, (N,), 32, L + 1).astype(jnp.int32)
        p_t = jax.random.uniform(k4, (N,), dtype=jnp.float32) * (src_len.astype(jnp.float32) - 1.0)
        W_a = jax.random.normal(k5, (H, H), dtype=jnp.float32) * (1.0 / np.sqrt(H))
        W_c = jax.random.normal(k6, (H, 2 * H), dtype=jnp.float32) * (1.0 / np.sqrt(2 * H))
        return {'encoder_outputs': encoder_outputs, 'decoder_h_t': decoder_h_t, 'src_len': src_len, 'p_t': p_t, 'W_a': W_a, 'W_c': W_c}
    _L2_xcond_all = _L2_xcond_setup()
    _L2_xcond_in = {k: v for k, v in _L2_xcond_all.items() if k in ('W_a', 'W_c')}
    del _L2_xcond_all

    def _L2_ffn_setup():
        import jax, jax.numpy as jnp
        import numpy as np
        TOP_K = 2
        key = jax.random.key(seed)
        ks = jax.random.split(key, 6)
        B, T, H, E, F = (2, 512, 256, 8, 1024)
        s = 0.02
        return {'hidden_states': jax.random.normal(ks[0], (B, T, H), dtype=jnp.float32), 'router_w': jax.random.normal(ks[1], (E, H), dtype=jnp.float32) * s, 'w1': jax.random.normal(ks[2], (E, F, H), dtype=jnp.float32) * s, 'b1': jax.random.normal(ks[3], (E, F), dtype=jnp.float32) * s, 'w2': jax.random.normal(ks[4], (E, H, F), dtype=jnp.float32) * s, 'b2': jax.random.normal(ks[5], (E, H), dtype=jnp.float32) * s}
    _L2_ffn_all = _L2_ffn_setup()
    _L2_ffn_in = {k: v for k, v in _L2_ffn_all.items() if k in ('router_w', 'w1', 'b1', 'w2', 'b2')}
    del _L2_ffn_all

    def _L3_xcond_setup():
        import jax, jax.numpy as jnp
        import numpy as np
        B, S, D, H = (2, 512, 256, 16)
        DK = D // H

        def _split_heads(x):
            b, s, _ = x.shape
            return x.reshape(b, s, H, DK).transpose(0, 2, 1, 3)
        key = jax.random.key(seed)
        ks = jax.random.split(key, 14)
        inp = {'query': jax.random.normal(ks[0], (B, S, D), jnp.float32), 'key': jax.random.normal(ks[1], (B, S, D), jnp.float32), 'value': jax.random.normal(ks[2], (B, S, D), jnp.float32), 'tau': jax.random.uniform(ks[3], (B, 1), jnp.float32, 0.5, 1.5), 'delta': jax.random.normal(ks[4], (B, S), jnp.float32)}
        sc = 1.0 / np.sqrt(D)
        for i, name in enumerate(['q', 'k', 'v', 'o']):
            inp[f'W{name}'] = jax.random.normal(ks[5 + 2 * i], (D, D), jnp.float32) * sc
            inp[f'b{name}'] = jax.random.normal(ks[6 + 2 * i], (D,), jnp.float32) * 0.01
        return inp
    _L3_xcond_all = _L3_xcond_setup()
    _L3_xcond_in = {k: v for k, v in _L3_xcond_all.items() if k in ('Wq', 'bq', 'Wk', 'bk', 'Wv', 'bv', 'Wo', 'bo')}
    del _L3_xcond_all

    def _L3_ffn_setup():
        import jax, jax.numpy as jnp
        import numpy as np
        HIDDEN = 256
        INNER = 1024

        def _weight_quant(w):
            scale = 1.0 / jnp.clip(jnp.mean(jnp.abs(w)), 1e-05)
            wq = jnp.clip(jnp.round(w * scale), -1.0, 1.0) / scale
            return w + jax.lax.stop_gradient(wq - w)

        def _act_quant(x):
            scale = 127.0 / jnp.clip(jnp.max(jnp.abs(x), axis=-1, keepdims=True), 1e-05)
            xq = jnp.clip(jnp.round(x * scale), -128.0, 127.0) / scale
            return x + jax.lax.stop_gradient(xq - x)

        def _bitlinear(x, w):
            return jnp.einsum('bsi,oi->bso', _act_quant(x), _weight_quant(w))
        key = jax.random.key(seed)
        k0, k1, k2, k3 = jax.random.split(key, 4)
        x = jax.random.normal(k0, (4, 512, HIDDEN), dtype=jnp.float32)
        w_gate = jax.random.normal(k1, (INNER, HIDDEN), dtype=jnp.float32) / np.sqrt(HIDDEN)
        w_up = jax.random.normal(k2, (INNER, HIDDEN), dtype=jnp.float32) / np.sqrt(HIDDEN)
        w_down = jax.random.normal(k3, (HIDDEN, INNER), dtype=jnp.float32) / np.sqrt(INNER)
        return {'x': x, 'w_gate': w_gate, 'w_up': w_up, 'w_down': w_down}
    _L3_ffn_all = _L3_ffn_setup()
    _L3_ffn_in = {k: v for k, v in _L3_ffn_all.items() if k in ('w_gate', 'w_up', 'w_down')}
    del _L3_ffn_all
    return {'x': x, 'ctx_1024': ctx_1024, 'condB_tau': condB_tau, 'fside_BxS2_0': fside_BxS2_0, 'condB_pt': condB_pt, '_lenS2': _lenS2, 'L0_xcond_Wq': _L0_xcond_in['Wq'], 'L0_xcond_bq': _L0_xcond_in['bq'], 'L0_xcond_Wk': _L0_xcond_in['Wk'], 'L0_xcond_bk': _L0_xcond_in['bk'], 'L0_xcond_Wv': _L0_xcond_in['Wv'], 'L0_xcond_bv': _L0_xcond_in['bv'], 'L0_xcond_Wo': _L0_xcond_in['Wo'], 'L0_xcond_bo': _L0_xcond_in['bo'], 'L0_ffn_gate_w': _L0_ffn_in['gate_w'], 'L0_ffn_w1': _L0_ffn_in['w1'], 'L0_ffn_b1': _L0_ffn_in['b1'], 'L0_ffn_ln1_g': _L0_ffn_in['ln1_g'], 'L0_ffn_ln1_b': _L0_ffn_in['ln1_b'], 'L0_ffn_w2': _L0_ffn_in['w2'], 'L0_ffn_b2': _L0_ffn_in['b2'], 'L0_ffn_ln_g': _L0_ffn_in['ln_g'], 'L0_ffn_ln_b': _L0_ffn_in['ln_b'], 'L1_xcond_Wq': _L1_xcond_in['Wq'], 'L1_xcond_bq': _L1_xcond_in['bq'], 'L1_xcond_Wk': _L1_xcond_in['Wk'], 'L1_xcond_bk': _L1_xcond_in['bk'], 'L1_xcond_Wv': _L1_xcond_in['Wv'], 'L1_xcond_bv': _L1_xcond_in['bv'], 'L1_xcond_Wo': _L1_xcond_in['Wo'], 'L1_xcond_bo': _L1_xcond_in['bo'], 'L1_ffn_W1': _L1_ffn_in['W1'], 'L1_ffn_b1': _L1_ffn_in['b1'], 'L1_ffn_quantum_phases': _L1_ffn_in['quantum_phases'], 'L1_ffn_quantum_weights_real': _L1_ffn_in['quantum_weights_real'], 'L1_ffn_quantum_weights_imag': _L1_ffn_in['quantum_weights_imag'], 'L1_ffn_W2': _L1_ffn_in['W2'], 'L1_ffn_b2': _L1_ffn_in['b2'], 'L2_xcond_W_a': _L2_xcond_in['W_a'], 'L2_xcond_W_c': _L2_xcond_in['W_c'], 'L2_ffn_router_w': _L2_ffn_in['router_w'], 'L2_ffn_w1': _L2_ffn_in['w1'], 'L2_ffn_b1': _L2_ffn_in['b1'], 'L2_ffn_w2': _L2_ffn_in['w2'], 'L2_ffn_b2': _L2_ffn_in['b2'], 'L3_xcond_Wq': _L3_xcond_in['Wq'], 'L3_xcond_bq': _L3_xcond_in['bq'], 'L3_xcond_Wk': _L3_xcond_in['Wk'], 'L3_xcond_bk': _L3_xcond_in['bk'], 'L3_xcond_Wv': _L3_xcond_in['Wv'], 'L3_xcond_bv': _L3_xcond_in['bv'], 'L3_xcond_Wo': _L3_xcond_in['Wo'], 'L3_xcond_bo': _L3_xcond_in['bo'], 'L3_ffn_w_gate': _L3_ffn_in['w_gate'], 'L3_ffn_w_up': _L3_ffn_in['w_up'], 'L3_ffn_w_down': _L3_ffn_in['w_down']}

def reference(x, ctx_1024, condB_tau, fside_BxS2_0, condB_pt, _lenS2, L0_xcond_Wq, L0_xcond_bq, L0_xcond_Wk, L0_xcond_bk, L0_xcond_Wv, L0_xcond_bv, L0_xcond_Wo, L0_xcond_bo, L0_ffn_gate_w, L0_ffn_w1, L0_ffn_b1, L0_ffn_ln1_g, L0_ffn_ln1_b, L0_ffn_w2, L0_ffn_b2, L0_ffn_ln_g, L0_ffn_ln_b, L1_xcond_Wq, L1_xcond_bq, L1_xcond_Wk, L1_xcond_bk, L1_xcond_Wv, L1_xcond_bv, L1_xcond_Wo, L1_xcond_bo, L1_ffn_W1, L1_ffn_b1, L1_ffn_quantum_phases, L1_ffn_quantum_weights_real, L1_ffn_quantum_weights_imag, L1_ffn_W2, L1_ffn_b2, L2_xcond_W_a, L2_xcond_W_c, L2_ffn_router_w, L2_ffn_w1, L2_ffn_b1, L2_ffn_w2, L2_ffn_b2, L3_xcond_Wq, L3_xcond_bq, L3_xcond_Wk, L3_xcond_bk, L3_xcond_Wv, L3_xcond_bv, L3_xcond_Wo, L3_xcond_bo, L3_ffn_w_gate, L3_ffn_w_up, L3_ffn_w_down):
    import jax
    import jax.numpy as jnp

    def _L0_xcond_ref(q, k, v, tau, delta, Wq, bq, Wk, bk, Wv, bv, Wo, bo):
        import jax, jax.numpy as jnp
        import numpy as np
        D_MODEL = 256
        N_HEADS = 16
        B, L, D = q.shape
        S = k.shape[1]
        H = N_HEADS
        E = D // H
        qh = (q @ Wq.T + bq).reshape(B, L, H, E)
        kh = (k @ Wk.T + bk).reshape(B, S, H, E)
        vh = (v @ Wv.T + bv).reshape(B, S, H, E)
        scale = 1.0 / np.sqrt(E).astype(np.float32)
        scores = jnp.einsum('blhe,bshe->bhls', qh, kh)
        scores = scores * tau[:, None, None, :] + delta[:, None, None, :]
        a = jax.nn.softmax(scale * scores, axis=-1)
        out = jnp.einsum('bhls,bshd->blhd', a, vh).reshape(B, L, D)
        return out @ Wo.T + bo

    def _L0_ffn_ref(x, gate_w, w1, b1, ln1_g, ln1_b, w2, b2, ln_g, ln_b):
        import jax, jax.numpy as jnp
        import numpy as np
        DIM = 256
        E = 8
        K = 2
        EPS = 1e-05

        def _ln(x, g, b):
            mu = jnp.mean(x, axis=-1, keepdims=True)
            var = jnp.mean(jnp.square(x - mu), axis=-1, keepdims=True)
            return (x - mu) * jax.lax.rsqrt(var + EPS) * g + b
        shape = x.shape
        xf = x.reshape(-1, shape[-1])
        gates = jax.nn.softmax(xf @ gate_w, axis=-1)
        topw, topi = jax.lax.top_k(gates, K)
        topw = topw / jnp.sum(topw, axis=-1, keepdims=True)
        combine = jnp.sum(topw[:, :, None] * jax.nn.one_hot(topi, E, dtype=xf.dtype), axis=1)
        h = jnp.einsum('td,edh->teh', xf, w1) + b1
        h = _ln(h, ln1_g, ln1_b)
        h = jax.nn.gelu(h, approximate=False)
        y = jnp.einsum('teh,ehd->ted', h, w2) + b2
        out = jnp.einsum('ted,te->td', y, combine)
        out = _ln(out + xf, ln_g, ln_b)
        return out.reshape(shape)

    def _L1_xcond_ref(query, key, value, tau, delta, Wq, bq, Wk, bk, Wv, bv, Wo, bo):
        import jax, jax.numpy as jnp
        import numpy as np
        B, S, D, H = (2, 512, 256, 16)
        DK = D // H

        def _split_heads(x):
            b, s, _ = x.shape
            return x.reshape(b, s, H, DK).transpose(0, 2, 1, 3)
        q = _split_heads(query @ Wq.T + bq)
        k = _split_heads(key @ Wk.T + bk)
        v = _split_heads(value @ Wv.T + bv)
        scores = jnp.einsum('bhqd,bhkd->bhqk', q, k)
        scores = scores * tau[:, :, None, None] + delta[:, None, None, :]
        scores = scores / jnp.sqrt(jnp.asarray(DK, scores.dtype))
        p_attn = jax.nn.softmax(scores, axis=-1)
        x = jnp.einsum('bhqk,bhkd->bhqd', p_attn, v)
        x = x.transpose(0, 2, 1, 3).reshape(query.shape[0], -1, H * DK)
        return x @ Wo.T + bo

    def _L1_ffn_ref(x, W1, b1, quantum_phases, quantum_weights_real, quantum_weights_imag, W2, b2):
        import jax, jax.numpy as jnp
        import numpy as np
        B, S, D_MODEL, D_FF = (4, 512, 256, 1024)

        def _quantum_transform(hidden, theta, w_real, w_imag):
            imag = w_imag * jnp.sin(theta + hidden * 0.1)
            quantum_phase = jnp.cos(theta) * w_real + jnp.sin(theta) * w_imag
            return hidden + quantum_phase * imag * 0.1
        hidden = jnp.einsum('bsd,df->bsf', x, W1) + b1
        q = _quantum_transform(hidden, quantum_phases, quantum_weights_real, quantum_weights_imag)
        act = jax.nn.relu(q)
        return jnp.einsum('bsf,fd->bsd', act, W2) + b2

    def _L2_xcond_ref(encoder_outputs, decoder_h_t, src_len, p_t, W_a, W_c):
        import jax, jax.numpy as jnp
        import numpy as np
        N, L, H, Q = (64, 258, 256, 64)
        WINDOW = 16.0
        DEV_POW = 128.0
        n, l, h = encoder_outputs.shape
        idx = jnp.arange(l, dtype=jnp.float32)
        src_end = src_len.astype(jnp.float32)
        attn_start = jnp.maximum(p_t - WINDOW, 0.0)
        attn_end = jnp.minimum(p_t + WINDOW, src_end)
        mask = (idx[None, :] < attn_start[:, None]) | (idx[None, :] > attn_end[:, None])
        score = jnp.einsum('nqh,hk,nlk->nql', decoder_h_t, W_a, encoder_outputs)
        score = jnp.where(mask[:, None, :], -1000000000.0, score)
        align = jax.nn.softmax(score, axis=2)
        gauss = jnp.exp(-(idx[None, :] - p_t[:, None]) ** 2 / DEV_POW)
        align = align * gauss[:, None, :]
        context = jnp.einsum('nql,nlh->nqh', align, encoder_outputs)
        cat = jnp.concatenate([context, decoder_h_t], axis=2)
        return jnp.tanh(cat @ W_c.T)

    def _L2_ffn_ref(hidden_states, router_w, w1, b1, w2, b2):
        import jax, jax.numpy as jnp
        import numpy as np
        TOP_K = 2
        x = hidden_states
        router_logits = jnp.einsum('bth,eh->bte', x, router_w)
        topk_values, topk_indices = jax.lax.top_k(router_logits, TOP_K)
        topk_weights = jax.nn.softmax(topk_values.astype(jnp.float32), axis=-1).astype(x.dtype)
        h1 = jnp.einsum('bth,efh->btef', x, w1) + b1
        h1 = jax.nn.gelu(h1, approximate=False)
        expert_outputs = jnp.einsum('btef,ehf->bteh', h1, w2) + b2
        gather_idx = topk_indices[..., None]
        topk_expert_outputs = jnp.take_along_axis(expert_outputs, gather_idx, axis=2)
        mixed_output = jnp.sum(topk_expert_outputs * topk_weights[..., None], axis=2)
        return mixed_output

    def _L3_xcond_ref(query, key, value, tau, delta, Wq, bq, Wk, bk, Wv, bv, Wo, bo):
        import jax, jax.numpy as jnp
        import numpy as np
        B, S, D, H = (2, 512, 256, 16)
        DK = D // H

        def _split_heads(x):
            b, s, _ = x.shape
            return x.reshape(b, s, H, DK).transpose(0, 2, 1, 3)
        q = _split_heads(query @ Wq.T + bq)
        k = _split_heads(key @ Wk.T + bk)
        v = _split_heads(value @ Wv.T + bv)
        scores = jnp.einsum('bhqd,bhkd->bhqk', q, k)
        scores = scores * tau[:, :, None, None] + delta[:, None, None, :]
        scores = scores / jnp.sqrt(jnp.asarray(DK, scores.dtype))
        p_attn = jax.nn.softmax(scores, axis=-1)
        x = jnp.einsum('bhqk,bhkd->bhqd', p_attn, v)
        x = x.transpose(0, 2, 1, 3).reshape(query.shape[0], -1, H * DK)
        return x @ Wo.T + bo

    def _L3_ffn_ref(x, w_gate, w_up, w_down):
        import jax, jax.numpy as jnp
        import numpy as np
        HIDDEN = 256
        INNER = 1024

        def _weight_quant(w):
            scale = 1.0 / jnp.clip(jnp.mean(jnp.abs(w)), 1e-05)
            wq = jnp.clip(jnp.round(w * scale), -1.0, 1.0) / scale
            return w + jax.lax.stop_gradient(wq - w)

        def _act_quant(x):
            scale = 127.0 / jnp.clip(jnp.max(jnp.abs(x), axis=-1, keepdims=True), 1e-05)
            xq = jnp.clip(jnp.round(x * scale), -128.0, 127.0) / scale
            return x + jax.lax.stop_gradient(xq - x)

        def _bitlinear(x, w):
            return jnp.einsum('bsi,oi->bso', _act_quant(x), _weight_quant(w))
        gate = jax.nn.silu(_bitlinear(x, w_gate))
        up = _bitlinear(x, w_up)
        return _bitlinear(gate * up, w_down)
    x = x + _L0_xcond_ref(_layernorm(x, axis=-1), ctx_1024, ctx_1024, condB_tau[:, None], fside_BxS2_0, L0_xcond_Wq, L0_xcond_bq, L0_xcond_Wk, L0_xcond_bk, L0_xcond_Wv, L0_xcond_bv, L0_xcond_Wo, L0_xcond_bo)
    x = x + _L0_ffn_ref(_layernorm(x, axis=-1), L0_ffn_gate_w, L0_ffn_w1, L0_ffn_b1, L0_ffn_ln1_g, L0_ffn_ln1_b, L0_ffn_w2, L0_ffn_b2, L0_ffn_ln_g, L0_ffn_ln_b)
    x = x + _L1_xcond_ref(_layernorm(x, axis=-1), ctx_1024, ctx_1024, condB_tau[:, None], fside_BxS2_0, L1_xcond_Wq, L1_xcond_bq, L1_xcond_Wk, L1_xcond_bk, L1_xcond_Wv, L1_xcond_bv, L1_xcond_Wo, L1_xcond_bo)
    x = x + _L1_ffn_ref(_layernorm(x, axis=-1), L1_ffn_W1, L1_ffn_b1, L1_ffn_quantum_phases, L1_ffn_quantum_weights_real, L1_ffn_quantum_weights_imag, L1_ffn_W2, L1_ffn_b2)
    x = x + _L2_xcond_ref(ctx_1024, _layernorm(x, axis=-1), _lenS2, condB_pt, L2_xcond_W_a, L2_xcond_W_c)
    x = x + _L2_ffn_ref(_layernorm(x, axis=-1), L2_ffn_router_w, L2_ffn_w1, L2_ffn_b1, L2_ffn_w2, L2_ffn_b2)
    x = x + _L3_xcond_ref(_layernorm(x, axis=-1), ctx_1024, ctx_1024, condB_tau[:, None], fside_BxS2_0, L3_xcond_Wq, L3_xcond_bq, L3_xcond_Wk, L3_xcond_bk, L3_xcond_Wv, L3_xcond_bv, L3_xcond_Wo, L3_xcond_bo)
    x = x + _L3_ffn_ref(_layernorm(x, axis=-1), L3_ffn_w_gate, L3_ffn_w_up, L3_ffn_w_down)
    return x

_drawn_inputs = setup_inputs


def setup_inputs(seed=0):
    import zlib

    import numpy as np

    out = dict(_drawn_inputs(seed))
    spreads = {'L0_xcond_bq': (0.0, 0.401),
     'L0_xcond_bk': (0.0, 2.0),
     'L0_xcond_bv': (0.0, 0.1),
     'L0_xcond_bo': (0.0, 0.1),
     'L0_ffn_ln1_g': (1.0, 0.568),
     'L0_ffn_ln1_b': (0.0, 0.628),
     'L0_ffn_ln_g': (1.0, 0.2),
     'L0_ffn_ln_b': (0.0, 0.1),
     'L1_ffn_b1': (0.0, 0.268),
     'L1_ffn_b2': (0.0, 0.1)}
    factors = {'L0_ffn_b1': 6.649,
     'L0_ffn_b2': 6.431,
     'L1_xcond_bq': 54.681,
     'L1_xcond_bk': 64.0,
     'L1_xcond_bv': 8.0,
     'L1_xcond_bo': 8.0,
     'L1_ffn_quantum_phases': 29.345,
     'L1_ffn_quantum_weights_real': 57.091,
     'L1_ffn_quantum_weights_imag': 24.681,
     'L2_ffn_b1': 28.022,
     'L2_ffn_b2': 8.0,
     'L3_xcond_bq': 64.0,
     'L3_xcond_bk': 64.0,
     'L3_xcond_bv': 8.0,
     'L3_xcond_bo': 8.0}
    for name, (base, spread) in spreads.items():
        noise = np.random.default_rng([zlib.crc32(name.encode()), seed]).standard_normal(out[name].shape)
        drawn = base * np.exp(spread * noise) if base else spread * noise
        out[name] = jnp.asarray(drawn.astype(out[name].dtype))
    for name, factor in factors.items():
        out[name] = (out[name] * factor).astype(out[name].dtype)
    return out
```

```python
from contextlib import ExitStack

import numpy as np

import concourse.bass as bass
from concourse import mybir

F32 = mybir.dt.float32
BF16 = mybir.dt.bfloat16
I32 = mybir.dt.int32
U32 = mybir.dt.uint32
ALU = mybir.AluOpType
ACT = mybir.ActivationFunctionType
AX = mybir.AxisListType

P = 128
NB, SEQ, D = 8, 512, 256
TPB = SEQ // P
NT = NB * TPB
DC = D // P
S = 64
H, DK = 16, 16
HPC = H // DC
VW = DK + 1
E, TOPK = 8, 2
F0, F1, F2, F3 = 512, 1024, 1024, 1024
NTILES = TOPK * NT + E
EPS = 1e-5
MAGIC = 1.5 * 2.0 ** 23
TWO_PI = 2.0 * np.pi
WINDOW, DEV_POW = 16.0, 128.0

C_ID, C_TRI, C_ONE = 0, P, 2 * P
C_HM = 3 * P
C_L = C_HM + HPC * S
C_P = C_L + S
C_E = C_P + 1
C_J = C_E + E
C_N = C_J + NTILES


def constants():
    c = np.zeros((P, C_N), np.float32)
    p = np.arange(P)
    c[:, C_ID:C_ID + P] = np.eye(P)
    c[:, C_TRI:C_TRI + P] = p[:, None] < p[None, :]
    c[:, C_ONE:C_ONE + P] = 1.0
    c[:, C_HM:C_HM + HPC * S] = np.repeat(p[:, None] // DK == np.arange(HPC)[None, :], S, axis=1)
    c[:, C_L:C_L + S] = np.arange(S)
    c[:, C_P] = p % S
    c[:, C_E:C_E + E] = E - np.arange(E)
    c[:, C_J:C_J + NTILES] = np.arange(NTILES)
    return c


def wait_pos(eng, sem, value):
    if not (isinstance(value, int) and value <= 0):
        eng.wait_ge(sem, value)


def over_batches(eng, step, count=NB):
    step(0, 0, True, False)
    with eng.Fori(0, (count - 2) // 2) as i:
        step(i * 2 + 1, 1, False, False)
        step(i * 2 + 2, 0, False, False)
    step(count - 1, 1, False, True)


class Core:

    def __init__(self, nc, ctx, a):
        self.nc, self.a = nc, a
        self.stale = []
        sem = lambda n: ctx.enter_context(nc.semaphore(n))
        self.zeroed, self.scattered = sem("zeroed"), sem("scattered")
        self.g_in = [sem(f"g_in{r}") for r in range(RING)]
        self.mixtures = 0
        self.w_in = sem("w_in")
        self.psum = ctx.enter_context(nc.psum_tensor("psum", [P, 8 * BANK], F32))
        sb = lambda n, s, d=F32: ctx.enter_context(nc.sbuf_tensor(n, s, d))
        self.x = sb("x_res", [P, NT * D])
        self.cst = sb("cst", [P, C_N])
        self.stats = sb("stats", [P, NT, 6])
        self.mean = sb("mean", [P, NT])
        self.rstd = sb("rstd", [P, NT])
        self.half = sb("half", [P, NT])
        self.lnt = sb("lnt", [P, 3, NT])
        self.tau = sb("tau", [P, NB])
        self.delta = sb("delta", [P, NB * S])
        self.xs = nc.dram_tensor("sorted_in", [NTILES * P, D], F32, kind="Internal").ap()
        self.ys = nc.dram_tensor("sorted_out", [NTILES * P, D], F32, kind="Internal").ap()
        self.ident = self.cst[:, C_ID:C_ID + P]

    def xt(self, n):
        return self.x[:, bass.ds(n * D, D)]


RING = 4
BANK = 512


def scoped(k):
    nc, taken = k.nc, [0]
    ctx = ExitStack()
    sb = lambda n, s, d=F32: ctx.enter_context(nc.sbuf_tensor(n, s, d))

    def ps(name, shape, dtype=F32):
        size = int(np.prod(shape[1:]))
        words = size // (2 if dtype == BF16 else 1)
        at, taken[0] = taken[0], taken[0] + -(-words // BANK)
        assert taken[0] <= 8, name
        ap = k.psum[:, at * BANK:at * BANK + words]
        if dtype == BF16:
            ap = ap.bitcast(BF16)
        return ap if len(shape) == 2 else ap.rearrange("p (a b) -> p a b", a=shape[1])


    def sem(name):
        handle = ctx.enter_context(nc.semaphore(name))
        k.stale.append(handle)
        return handle

    return ctx, sb, ps, sem


def clear_stale(k, pool, own):
    numbers = sorted({s.num for s in k.stale} - {s.num for s in own})
    k.stale = list(own)
    while numbers:
        n = 1
        while n < len(numbers) and numbers[n] == numbers[0] + n:
            n += 1
        pool.sem_clear(range(numbers[0], numbers[0] + n))
        numbers = numbers[n:]


def load_stage(nc, k):
    ctx, sb, ps, sem = scoped(k)
    a = k.a
    with ctx:
        loaded, x_loaded, half_set = sem("ld_small"), sem("ld_x"), sem("ld_half")
        zero_set = sem("ld_zero_set")
        zero = sb("ld_zero", [P, NTILES // E * D])
        with nc.Block() as block:
            @block.sync
            def _(sp):
                for b in range(NB):
                    sp.dma_start(k.x[:, b * TPB * D:(b + 1) * TPB * D].rearrange("p (t d) -> p t d", t=TPB),
                                 a["x"][b].rearrange("(t p) d -> p t d", p=P)).then_inc(x_loaded, 16)

            @block.scalar
            def _(act):
                act.dma_start(k.cst[:, :], a["cst"]).then_inc(loaded, 16)
                act.dma_start(k.tau[:, :], a["tau"].partition_broadcast(P)).then_inc(loaded, 16)
                act.dma_start(k.delta[:, :], a["delta"].partition_broadcast(P)).then_inc(loaded, 16)

            @block.gpsimd
            def _(pool):
                pool.memset(k.half[:, :], -0.5).then_inc(half_set, 1)
                pool.memset(zero[:, :], 0.0).then_inc(zero_set, 1)
                pool.wait_ge(zero_set, 1)
                for g in range(E):
                    pool.dma_start(k.xs.rearrange("(g p r) d -> g p (r d)", g=E, p=P)[g], zero[:, :]).then_inc(k.zeroed, 16)
                pool.wait_ge(k.zeroed, 16 * E)

            @block.vector
            def _(dve):
                dve.wait_ge(loaded, 48)
                dve.tensor_scalar(k.tau[:, :], k.tau[:, :], DK ** -0.5, None, ALU.mult)
                dve.tensor_scalar(k.delta[:, :], k.delta[:, :], DK ** -0.5, None, ALU.mult)
                for b in range(NB):
                    if b == 0:
                        dve.wait_ge(x_loaded, 16 * NB)
                    for t in range(TPB):
                        n = b * TPB + t
                        dve.bn_stats(k.stats[:, n, :], k.x[:, n * D:(n + 1) * D])


def ln_scalars(nc, k, name):
    ctx, sb, ps, sem = scoped(k)
    with ctx:
        dv, pw = sem(name + "_lnv"), sem(name + "_lnp")
        me, ve, mo, vo = (k.stats[:, :, j] for j in (1, 2, 4, 5))
        d, m2, v = (k.lnt[:, j, :] for j in range(3))
        with nc.Block() as block:
            @block.vector
            def _(dve):
                dve.tensor_tensor(d, me, mo, ALU.subtract).then_inc(dv, 1)
                dve.tensor_tensor(m2, ve, vo, ALU.add).then_inc(dv, 1)
                dve.tensor_tensor(k.mean[:, :], me, mo, ALU.add).then_inc(dv, 1)
                dve.wait_ge(dv, 3)
                dve.scalar_tensor_tensor(v, d, 0.25, d, ALU.mult, ALU.mult).then_inc(dv, 1)
                dve.tensor_scalar(k.mean[:, :], k.mean[:, :], 0.5, None, ALU.mult)
                dve.tensor_scalar(m2, m2, 1.0 / D, EPS, ALU.mult, ALU.add).then_inc(dv, 1)
                dve.wait_ge(dv, 5)
                dve.tensor_tensor(v, v, m2, ALU.add).then_inc(pw, 1)

            @block.gpsimd
            def _(pool):
                clear_stale(k, pool, (dv, pw))
                pool.wait_ge(pw, 1)
                pool.tensor_tensor(k.rstd[:, :], v, k.half[:, :], ALU.pow)



def attention(nc, k, L):
    ctx, sb, ps, sem = scoped(k)
    a = k.a
    nm = f"a{L}_"
    with ctx:
        w = {c: sb(nm + "w" + c, [P, DC, D]) for c in "qkvo"}
        bq, bk = sb(nm + "bq", [P, DC]), sb(nm + "bk", [P, DC])
        bv, bo = sb(nm + "bv", [P, D]), sb(nm + "bo", [P, D])
        cx = [sb(f"{nm}cx{s}", [P, DC, 2, S]) for s in range(2)]
        z = [sb(f"{nm}z{s}", [P, TPB, D]) for s in range(2)]
        zT = sb(nm + "zT", [P, DC, SEQ])
        qT = [sb(f"{nm}qT{s}", [P, DC, SEQ]) for s in range(2)]
        kb = [sb(f"{nm}kb{s}", [P, DC, HPC * S]) for s in range(2)]
        va = [sb(f"{nm}va{s}", [P, H // 2, 2, VW]) for s in range(2)]
        pr = [sb(f"{nm}pr{s}", [P, H * S]) for s in range(2)]
        pT = [sb(f"{nm}pT{s}", [P, H // 2, P]) for s in range(2)]
        mx = [sb(f"{nm}mx{s}", [P, H]) for s in range(2)]
        rec = [sb(f"{nm}rec{s}", [P, H]) for s in range(2)]
        on = [sb(f"{nm}on{s}", [P, D]) for s in range(2)]
        oT = [sb(f"{nm}oT{s}", [P, DC, P]) for s in range(2)]
        psS = [ps(f"{nm}psS{s}", [P, H * S]) for s in range(2)]
        psP = ps(nm + "psP", [P, H // 2, P])
        m0, m1 = ps(nm + "m0", [P, 512]), ps(nm + "m1", [P, 512])

        w_in = sem(nm + "w_in")
        cx_in = [sem(f"{nm}cx_in{s}") for s in range(2)]
        va_zero, va_init = sem(nm + "va_zero"), sem(nm + "va_init")
        z_done, xb_done = sem(nm + "z_done"), sem(nm + "xb_done")
        zT_ps, q_ps, k_ps, v_ps = (sem(nm + c) for c in ("zT_ps", "q_ps", "k_ps", "v_ps"))
        m0_drained, m1_drained = sem(nm + "m0_drained"), sem(nm + "m1_drained")
        s_ps, s_evac, s_max, s_sub, exp_done = (
            sem(nm + c) for c in ("s_ps", "s_evac", "s_max", "s_sub", "exp_done"))
        t_ps, t_evac, o_ps, o_rec, o_norm = (sem(nm + c) for c in ("t_ps", "t_evac", "o_ps", "o_rec", "o_norm"))
        oT_ps, oT_copied, y_ps, x_added = (sem(nm + c) for c in ("oT_ps", "oT_copied", "y_ps", "x_added"))

        def pieces(b, t, last): return 3 * b + 3 + (0 if last else t)

        with nc.Block() as block:
            @block.sync
            def _(sp):
                for c in "qkvo":
                    sp.dma_start(w[c][:, :, :], a[f"L{L}_xcond_W{c}"]).then_inc(w_in, 16)
                sp.dma_start(bq[:, :], a[f"L{L}_xcond_bq"]).then_inc(w_in, 16)
                sp.dma_start(bk[:, :], a[f"L{L}_xcond_bk"]).then_inc(w_in, 16)
                sp.dma_start(bv[:, :], a[f"L{L}_xcond_bv"].partition_broadcast(P)).then_inc(w_in, 16)
                sp.dma_start(bo[:, :], a[f"L{L}_xcond_bo"].partition_broadcast(P)).then_inc(w_in, 16)

                def step(b, s, first, last):
                    wait_pos(sp, v_ps, b - 1)
                    for j in range(2):
                        sp.dma_start(cx[s][:, :, j, :],
                                     a["ctxT"][bass.ds(b, 1)].rearrange("b p c l -> p (b c) l")).then_inc(cx_in[s], 16)
                over_batches(sp, step)

            @block.gpsimd
            def _(pool):
                for s in range(2):
                    pool.memset(va[s][:, :, :, :], 0.0).then_inc(va_zero, 1)
                pool.wait_ge(va_zero, 2)
                for s in range(2):
                    pool.memset(va[s][0:S, :, 0, DK:VW], 1.0).then_inc(va_init, 1)
                    pool.memset(va[s][S:P, :, 1, DK:VW], 1.0).then_inc(va_init, 1)
                pool.wait_ge(w_in, 16 * 8)

                def step(b, s, first, last):
                    pool.wait_ge(z_done, b + 1)
                    xs = k.x[:, bass.ds(b * (TPB * D), TPB * D)].rearrange("p (t d) -> p t d", t=TPB)
                    pool.tensor_tensor(xs, xs, bo[:, None, :].to_broadcast([P, TPB, D]), ALU.add).then_inc(xb_done, 1)
                over_batches(pool, step)

            @block.tensor
            def _(pe):
                def piece(b, s, t, u, n):
                    wait_pos(pe, o_norm, n + 1)
                    wait_pos(pe, x_added, n)
                    if t == 0:
                        pe.wait_ge(z_done, b + 1)
                        for c, (m, drained) in enumerate(((m0, m0_drained), (m1, m1_drained))):
                            wait_pos(pe, drained, u)
                            for i in range(TPB):
                                mm = pe.transpose(m[:, i * P:(i + 1) * P], z[s][:, i, c * P:(c + 1) * P], k.ident)
                            mm.then_inc(zT_ps, 1)
                    elif t == 1:
                        pe.wait_ge(m0_drained, u)
                        pe.wait_ge(m1_drained, u)
                        for c, m in enumerate((m0, m1)):
                            for kk in range(DC):
                                mm = pe.matmul(m[:, :], w["q"][:, kk, c * P:(c + 1) * P], zT[:, kk, :],
                                               start=(kk == 0), stop=(kk == DC - 1))
                            mm.then_inc(q_ps, 1)
                    else:
                        pe.wait_ge(cx_in[s], 16 * b + (16 if s else 32))
                        pe.wait_ge(m0_drained, u)
                        for c in range(DC):
                            for kk in range(DC):
                                mm = pe.matmul(m0[:, c * S:(c + 1) * S], w["k"][:, kk, c * P:(c + 1) * P],
                                               cx[s][:, kk, 0, :], start=(kk == 0), stop=(kk == DC - 1))
                        mm.then_inc(k_ps, 1)
                        pe.wait_ge(m1_drained, u)
                        for kk in range(DC):
                            mm = pe.matmul(m1[:, 0:D], cx[s][:, kk, :, :].rearrange("p j l -> p (j l)"),
                                           w["v"][:, kk, :], start=(kk == 0), stop=(kk == DC - 1))
                        mm.then_inc(v_ps, 1)

                def scores(n, s, t):
                    u = t % 2
                    wait_pos(pe, s_evac, n - 1)
                    for c in range(DC):
                        mm = pe.matmul(psS[u][:, c * 512:(c + 1) * 512], qT[s][:, c, t * P:(t + 1) * P],
                                       kb[s][:, c, :], start=True, stop=True)
                    mm.then_inc(s_ps, 1)

                def project_turn(n, t):
                    pe.wait_ge(o_norm, n + 1)
                    for c in range(DC):
                        mm = pe.transpose(m1[:, c * P:(c + 1) * P], on[t % 2][:, c * P:(c + 1) * P], k.ident)
                    mm.then_inc(oT_ps, 1)

                def project(n, t):
                    pe.wait_ge(oT_copied, n + 1)
                    for c in range(DC):
                        mm = pe.matmul(m1[:, D:2 * D], oT[t % 2][:, c, :], w["o"][:, c, :],
                                       start=(c == 0), stop=(c == DC - 1))
                    mm.then_inc(y_ps, 1)

                def step(b, s, first, last):
                    for t in range(TPB):
                        n = b * TPB + t
                        if t < TPB - 1:
                            scores(n + 1, s, t + 1)
                        elif not last:
                            pe.wait_ge(m1_drained, pieces(b, 3, last))
                            scores(n + 1, 1 - s, 0)
                        begins = first and t == 0
                        if not begins:
                            pe.wait_ge(m1_drained, pieces(b, t, last))
                            wait_pos(pe, x_added, n - 1)
                            project_turn(n - 1, t - 1)
                        pe.wait_ge(exp_done, n + 1)
                        wait_pos(pe, t_evac, n)
                        for c in range(H // 2):
                            mm = pe.transpose(psP[:, c, :], pr[t % 2][:, c * P:(c + 1) * P], k.ident)
                        mm.then_inc(t_ps, 1)
                        if not begins:
                            project(n - 1, t - 1)
                        pe.wait_ge(t_evac, n + 1)
                        pe.wait_ge(m0_drained, pieces(b, t, last))
                        wait_pos(pe, o_norm, n)
                        for c in range(H // 2):
                            mm = pe.matmul(m0[:, c * 2 * VW:(c + 1) * 2 * VW], pT[t % 2][:, c, :],
                                           va[s][:, c, :, :].rearrange("p j v -> p (j v)"), start=True, stop=True)
                        mm.then_inc(o_ps, 1)
                        if t < 3 and not last:
                            piece(b + 1, 1 - s, t, pieces(b, t, last), n)

                pe.wait_ge(w_in, 16 * 8)
                for t in range(3):
                    piece(0, 0, t, t, -1)
                pe.wait_ge(m1_drained, 3)
                scores(0, 0, 0)
                over_batches(pe, step)
                pe.wait_ge(x_added, NT - 1)
                project_turn(NT - 1, TPB - 1)
                project(NT - 1, TPB - 1)

            @block.scalar
            def _(act):
                def zT_copy(b):
                    for c, (m, drained) in enumerate(((m0, m0_drained), (m1, m1_drained))):
                        act.wait_ge(zT_ps, 2 * b + c + 1)
                        act.activation(zT[:, c, :], m[:, :], ACT.Copy).then_inc(drained, 1)

                def exponentials(n, t):
                    act.wait_ge(s_sub, n + 1)
                    act.activation(pr[t % 2][:, :], pr[t % 2][:, :], ACT.Exp).then_inc(exp_done, 1)

                def project_copy(n, t):
                    act.wait_ge(oT_ps, n + 1)
                    act.activation(oT[t % 2][:, :, :], m1[:, 0:D].rearrange("p (c q) -> p c q", c=DC),
                                   ACT.Copy).then_inc(oT_copied, 1)

                def step(b, s, first, last):
                    for t in range(TPB):
                        n = b * TPB + t
                        if not (first and t == 0):
                            project_copy(n - 1, t - 1)
                        act.wait_ge(t_ps, n + 1)
                        act.activation(pT[t % 2][:, :, :], psP[:, :, :], ACT.Copy).then_inc(t_evac, 1)
                        if not (last and t == TPB - 1):
                            exponentials(n + 1, t + 1)
                        if t == 0 and not last:
                            zT_copy(b + 1)

                zT_copy(0)
                act.wait_ge(w_in, 16 * 8)
                k.ahead(act)
                exponentials(0, 0)
                over_batches(act, step)
                project_copy(NT - 1, TPB - 1)

            @block.vector
            def _(dve):
                def normalise(b, s):
                    wait_pos(dve, zT_ps, 2 * (b - 1))
                    for t in range(TPB):
                        n = b * TPB + t
                        v = dve.tensor_scalar(z[s][:, t, :], k.xt(n), k.mean[:, bass.ds(n, 1)],
                                              k.rstd[:, bass.ds(n, 1)], ALU.subtract, ALU.mult)
                    v.then_inc(z_done, 1)

                def piece(b, s, t):
                    if t == 1:
                        for c, (m, drained) in enumerate(((m0, m0_drained), (m1, m1_drained))):
                            dve.wait_ge(q_ps, 2 * b + c + 1)
                            dve.tensor_scalar(qT[s][:, c, :], m[:, :], bq[:, c:c + 1],
                                              k.tau[:, bass.ds(b, 1)], ALU.add, ALU.mult).then_inc(drained, 1)
                    if t == 2:
                        dve.wait_ge(k_ps, b + 1)
                        for c in range(DC):
                            v = dve.scalar_tensor_tensor(
                                kb[s][:, c, :].rearrange("p (h l) -> p h l", h=HPC),
                                m0[:, None, c * S:(c + 1) * S].to_broadcast([P, HPC, S]), bk[:, c:c + 1],
                                k.cst[:, C_HM:C_HM + HPC * S].rearrange("p (h l) -> p h l", h=HPC),
                                ALU.add, ALU.mult)
                        v.then_inc(m0_drained, 1)
                        dve.wait_ge(v_ps, b + 1)
                        for j in range(2):
                            h = slice(j * S, (j + 1) * S)
                            v = dve.tensor_tensor(
                                va[s][h, :, j, 0:DK],
                                m1[h, 0:D].rearrange("p (c j e) -> p c j e", c=H // 2, j=2)[:, :, j, :],
                                bv[h, :].rearrange("p (c j e) -> p c j e", c=H // 2, j=2)[:, :, j, :], ALU.add)
                        v.then_inc(m1_drained, 1)

                def softmax(n, b, t):
                    p3 = pr[t % 2][:, :].rearrange("p (h l) -> p h l", h=H)
                    dve.wait_ge(s_ps, n + 1)
                    dve.tensor_tensor(p3, psS[t % 2][:, :].rearrange("p (h l) -> p h l", h=H),
                                      k.delta[:, None, bass.ds(b * S, S)].to_broadcast([P, H, S]),
                                      ALU.add).then_inc(s_evac, 1)
                    dve.wait_ge(s_evac, n + 1)
                    dve.tensor_reduce(mx[t % 2][:, :], p3, AX.X, ALU.max).then_inc(s_max, 1)
                    dve.wait_ge(s_max, n + 1)
                    dve.tensor_tensor(p3, p3, mx[t % 2][:, :, None].to_broadcast([P, H, S]),
                                      ALU.subtract).then_inc(s_sub, 1)

                def divide(n, t):
                    o3 = m0[:, 0:H * VW].rearrange("p (h v) -> p h v", h=H)
                    dve.wait_ge(o_ps, n + 1)
                    dve.reciprocal(rec[t % 2][:, :], o3[:, :, DK]).then_inc(o_rec, 1)
                    dve.wait_ge(o_rec, n + 1)
                    dve.tensor_tensor(on[t % 2][:, :].rearrange("p (h e) -> p h e", h=H), o3[:, :, 0:DK],
                                      rec[t % 2][:, :, None].to_broadcast([P, H, DK]), ALU.mult).then_inc(o_norm, 1)

                def residual(n):
                    dve.wait_ge(y_ps, n + 1)
                    dve.tensor_tensor(k.xt(n), m1[:, D:2 * D], k.xt(n), ALU.add).then_inc(x_added, 1)

                def statistics(n):
                    dve.wait_ge(x_added, n + 1)
                    dve.bn_stats(k.stats[:, bass.ds(n, 1), :], k.xt(n))

                def step(b, s, first, last):
                    for t in range(TPB):
                        n = b * TPB + t
                        if t == 0 and not last:
                            normalise(b + 1, 1 - s)
                        if t < TPB - 1:
                            softmax(n + 1, b, t + 1)
                        elif not last:
                            softmax(n + 1, b + 1, 0)
                        if not (first and t == 0):
                            if t == 1:
                                dve.wait_ge(xb_done, b + 1)
                            residual(n - 1)
                        divide(n, t)
                        if not (first and t == 0):
                            statistics(n - 1)
                        if t in (1, 2) and not last:
                            piece(b + 1, 1 - s, t)

                dve.wait_ge(w_in, 16 * 8)
                dve.wait_ge(va_init, 4)
                normalise(0, 0)
                for t in (1, 2):
                    piece(0, 0, t)
                softmax(0, 0, 0)
                over_batches(dve, step)
                residual(NT - 1)
                statistics(NT - 1)


def router(nc, k, L):
    ctx, sb, ps, sem = scoped(k)
    nm = f"r{L}_"
    with ctx:
        gate = sb(nm + "gate", [P, DC, E])
        z = [sb(f"{nm}z{s}", [P, TPB, D]) for s in range(2)]
        zT = [sb(f"{nm}zT{s}", [P, DC, SEQ]) for s in range(2)]
        bank = [ps(f"{nm}b{s}", [P, DC, SEQ]) for s in range(2)]
        lg = [ps(f"{nm}lg{s}", [P, 512]) for s in range(2)]
        w_in, z_done, z_kept, zT_ps, zT_copied, lg_ps, lg_read = (
            sem(nm + c) for c in ("w_in", "z_done", "z_kept", "zT_ps", "zT_copied", "lg_ps", "lg_read"))
        with nc.Block() as block:
            @block.sync
            def _(sp):
                sp.dma_start(gate[:, :, :], k.a[f"L{L}_gate"]).then_inc(w_in, 16)

            @block.vector
            def _(dve):
                def normalise(b, s):
                    wait_pos(dve, zT_ps, b - 1)
                    wait_pos(dve, z_kept, b - 1)
                    for t in range(TPB):
                        n = b * TPB + t
                        v = dve.tensor_scalar(z[s][:, t, :], k.xt(n), k.mean[:, bass.ds(n, 1)],
                                              k.rstd[:, bass.ds(n, 1)], ALU.subtract, ALU.mult)
                    v.then_inc(z_done, 1)

                def step(b, s, first, last):
                    if not last:
                        normalise(b + 1, 1 - s)
                    dve.wait_ge(lg_ps, b + 1)
                    dve.tensor_copy(k.logits[:, bass.ds(b * TPB, TPB), :],
                                    lg[s][:, 0:TPB * E].rearrange("p (t e) -> p t e", t=TPB)).then_inc(lg_read, 1)

                normalise(0, 0)
                over_batches(dve, step)

            @block.gpsimd
            def _(pool):
                def step(b, s, first, last):
                    pool.wait_ge(z_done, b + 1)
                    pool.tensor_copy(k.z[:, bass.ds(b * (TPB * D), TPB * D)],
                                     z[s][:, :, :].rearrange("p t d -> p (t d)")).then_inc(z_kept, 1)
                over_batches(pool, step)

            @block.tensor
            def _(pe):
                def turn(b, s):
                    pe.wait_ge(z_done, b + 1)
                    wait_pos(pe, zT_copied, b - 1)
                    for c in range(DC):
                        for t in range(TPB):
                            mm = pe.transpose(bank[s][:, c, t * P:(t + 1) * P], z[s][:, t, c * P:(c + 1) * P], k.ident)
                    mm.then_inc(zT_ps, 1)

                def step(b, s, first, last):
                    if not last:
                        turn(b + 1, 1 - s)
                    pe.wait_ge(zT_copied, b + 1)
                    wait_pos(pe, lg_read, b - 1)
                    for t in range(TPB):
                        for c in range(DC):
                            mm = pe.matmul(lg[s][:, t * E:(t + 1) * E], zT[s][:, c, t * P:(t + 1) * P],
                                           gate[:, c, :], start=(c == 0), stop=(c == DC - 1))
                    mm.then_inc(lg_ps, 1)

                pe.wait_ge(w_in, 16)
                turn(0, 0)
                over_batches(pe, step)

            @block.scalar
            def _(act):
                def step(b, s, first, last):
                    act.wait_ge(zT_ps, b + 1)
                    wait_pos(act, lg_ps, b - 1)
                    act.activation(zT[s][:, :, :], bank[s][:, :, :], ACT.Copy).then_inc(zT_copied, 1)
                over_batches(act, step)


def route(nc, k, L):
    ctx, sb, ps, sem = scoped(k)
    nm = f"q{L}_"
    with ctx:
        t3 = lambda n: sb(nm + n, [P, NT, E])
        t2 = lambda n: sb(nm + n, [P, NT])
        eq, cand, rest = t3("eq"), t3("cand"), t3("rest")
        hot = [t3("hot0"), t3("hot1")]
        top, code, pf = [t2("top0"), t2("top1")], t2("code"), t2("pf")
        chosen, place, prod = t3("chosen"), t3("place"), t3("prod")
        run = [t3("run0"), t3("run1")]
        gap, den = t2("gap"), t2("den")
        cnt = [sb(f"{nm}cnt{j}", [P, E]) for j in range(3)]
        owner = sb(nm + "owner", [1, NTILES, E])
        ownf = sb(nm + "ownf", [1, NTILES])
        pre, tot = ps(nm + "pre", [P, NT, E]), ps(nm + "tot", [P, NT, E])
        v, gap_done, gap_exp, chosen_done, pre_ps = (
            sem(nm + c) for c in ("v", "gap", "gap_exp", "chosen", "pre_ps"))
        bc = lambda t: t[:, :, None].to_broadcast([P, NT, E])
        code_e = k.cst[:, None, C_E:C_E + E].to_broadcast([P, NT, E])
        with nc.Block() as block:
            @block.vector
            def _(dve):
                n = [0]

                def then(op):
                    n[0] += 1
                    op.then_inc(v, 1)
                    dve.wait_ge(v, n[0])

                src = k.logits
                for j in range(TOPK):
                    then(dve.tensor_reduce(top[j][:, :], src[:, :, :], AX.X, ALU.max))
                    then(dve.tensor_tensor(eq[:, :, :], src[:, :, :], bc(top[j]), ALU.is_equal))
                    then(dve.tensor_tensor(cand[:, :, :], eq[:, :, :], code_e, ALU.mult))
                    then(dve.tensor_reduce(code[:, :], cand[:, :, :], AX.X, ALU.max))
                    then(dve.tensor_tensor(hot[j][:, :, :], cand[:, :, :], bc(code), ALU.is_equal))
                    if j == 0:
                        then(dve.scalar_tensor_tensor(rest[:, :, :], hot[0][:, :, :], -3e38, src[:, :, :],
                                                      ALU.mult, ALU.add))
                        src = rest
                dve.tensor_tensor(chosen[:, :, :], hot[0][:, :, :], hot[1][:, :, :], ALU.add).then_inc(chosen_done, 1)
                dve.tensor_tensor(gap[:, :], top[1][:, :], top[0][:, :], ALU.subtract).then_inc(gap_done, 1)
                dve.wait_ge(pre_ps, 2)
                then(dve.tensor_copy(run[0][:, :, :], tot[:, :, :]))
                cur = 0
                for sh in (1, 2, 4, 8, 16):
                    a, b = run[cur], run[1 - cur]
                    dve.tensor_copy(b[:, 0:sh, :], a[:, 0:sh, :])
                    then(dve.tensor_tensor(b[:, sh:NT, :], a[:, sh:NT, :], a[:, 0:NT - sh, :], ALU.add))
                    cur = 1 - cur
                upto = run[cur]
                then(dve.tensor_scalar(cnt[0][:, :], upto[:, NT - 1, :], P - 1.0, 1.0 / P, ALU.add, ALU.mult))
                then(dve.tensor_scalar(cnt[0][:, :], cnt[0][:, :], -(0.5 - 0.5 / P), MAGIC, ALU.add, ALU.add))
                then(dve.tensor_scalar(cnt[0][:, :], cnt[0][:, :], MAGIC, None, ALU.subtract))
                then(dve.tensor_copy(cnt[1][:, :], cnt[0][:, :]))
                c = 1
                for sh in (1, 2, 4):
                    a, b = cnt[c], cnt[3 - c]
                    dve.tensor_copy(b[:, 0:sh], a[:, 0:sh])
                    then(dve.tensor_tensor(b[:, sh:E], a[:, sh:E], a[:, 0:E - sh], ALU.add))
                    c = 3 - c
                end, start = cnt[c], cnt[3 - c]
                then(dve.tensor_tensor(start[:, :], end[:, :], cnt[0][:, :], ALU.subtract))
                then(dve.tensor_tensor(owner[:, :, :],
                                       k.cst[0:1, C_J:C_J + NTILES, None].to_broadcast([1, NTILES, E]),
                                       end[0:1, None, :].to_broadcast([1, NTILES, E]), ALU.is_ge))
                then(dve.tensor_reduce(ownf[:, :], owner[:, :, :], AX.X, ALU.add))
                dve.tensor_scalar(k.owner[:, :], ownf[:, :], E - 1.0, None, ALU.min)
                then(dve.tensor_scalar(start[:, :], start[:, :], float(P), None, ALU.mult))
                then(dve.tensor_tensor(place[:, :, :], upto[:, :, :], tot[:, :, :], ALU.subtract))
                then(dve.tensor_tensor(place[:, :, :], place[:, :, :], pre[:, :, :], ALU.add))
                then(dve.tensor_tensor(place[:, :, :], place[:, :, :],
                                       start[:, None, :].to_broadcast([P, NT, E]), ALU.add))
                for j in range(TOPK):
                    then(dve.tensor_tensor(prod[:, :, :], place[:, :, :], hot[j][:, :, :], ALU.mult))
                    then(dve.tensor_reduce(pf[:, :], prod[:, :, :], AX.X, ALU.add))
                    then(dve.tensor_copy(k.pos[j][:, :], pf[:, :]))
                dve.wait_ge(gap_exp, 1)
                then(dve.tensor_scalar(den[:, :], k.wt[1][:, :], 1.0, None, ALU.add))
                then(dve.reciprocal(k.wt[0][:, :], den[:, :]))
                then(dve.tensor_tensor(k.wt[1][:, :], k.wt[1][:, :], k.wt[0][:, :], ALU.mult))
                k.places_at = n[0]

            @block.scalar
            def _(act):
                act.wait_ge(gap_done, 1)
                act.activation(k.wt[1][:, :], gap[:, :], ACT.Exp).then_inc(gap_exp, 1)

            @block.tensor
            def _(pe):
                pe.wait_ge(chosen_done, 1)
                flat = lambda t: t[:, :, :].rearrange("p n e -> p (n e)")
                pe.matmul(flat(pre), k.cst[:, C_TRI:C_TRI + P], flat(chosen), start=True, stop=True).then_inc(pre_ps, 1)
                pe.matmul(flat(tot), k.cst[:, C_ONE:C_ONE + P], flat(chosen), start=True, stop=True).then_inc(pre_ps, 1)

        with nc.Block() as block:
            @block.gpsimd
            def _(pool):
                for n in range(NT):
                    for j in range(TOPK):
                        pool.indirect_dma_start(
                            out=k.xs[:, :], out_offset=bass.IndirectOffsetOnAxis(ap=k.pos[j][:, n:n + 1], axis=0),
                            in_=k.z[:, n * D:(n + 1) * D], in_offset=None).then_inc(k.scattered, 16)
                pool.wait_ge(k.scattered, 16 * NT * TOPK * (k.mixtures + 1))


def over_tiles(eng, step, ahead):
    loop = (NTILES - ahead) // 2
    step(0, 0, True, lambda d: True)
    step(1, 1, True, lambda d: True)
    with eng.Fori(1, loop) as i:
        step(i * 2, 0, False, lambda d: True)
        step(i * 2 + 1, 1, False, lambda d: True)
    for j in range(2 * loop, NTILES):
        step(j, j % 2, False, lambda d, j=j: j + d < NTILES)


def load_second_layers(sp, k, L):
    n2 = (F0 if L == 0 else F2) // P * D
    for e in range(E):
        sp.dma_start(k.w2[:, e * n2:(e + 1) * n2], k.a[f"L{L}_ffn_w2"][:, e, :]).then_inc(k.w_in, 16)


def load_first_layers(sp, k, L, es):
    n1 = DC * (F0 if L == 0 else F2)
    for e in es:
        sp.dma_start(k.w1[:, e * n1:(e + 1) * n1], k.a[f"L{L}_ffn_w1"][:, e, :]).then_inc(k.w_in, 16)


def experts(nc, k, L, late):
    ctx, sb, ps, sem = scoped(k)
    a = k.a
    nm = f"e{L}_"
    F = F0 if L == 0 else F2
    FC = F // P
    norm = L == 0
    A = 2 if norm else 1
    with ctx:
        w1, w2 = k.w1, k.w2
        b2 = sb(nm + "b2", [P, E * D])
        bt = sb(nm + "bt", [P, E * FC])
        if norm:
            b1 = sb(nm + "b1", [P, E * F])
            gt = sb(nm + "gt", [P, E * FC])
            st = [sb(f"{nm}st{s}", [P, 6]) for s in range(2)]
            mv = [sb(f"{nm}mv{s}", [P, 2]) for s in range(2)]
            ve = [sb(f"{nm}ve{s}", [P, 1]) for s in range(2)]
            rs = [sb(f"{nm}rs{s}", [P, 1]) for s in range(2)]
        xin = [sb(f"{nm}x{s}", [P, D]) for s in range(2)]
        xT = [sb(f"{nm}xT{s}", [P, DC, P]) for s in range(2)]
        h = [sb(f"{nm}h{s}", [P, F]) for s in range(2)]
        hT = [sb(f"{nm}hT{s}", [P, FC, P]) for s in range(2)]
        y = [sb(f"{nm}y{s}", [P, D]) for s in range(2)]
        xT_b = ps(nm + "pxT", [P, 512])
        h_b = [ps(f"{nm}ph{s}", [P, F]) for s in range(2)]
        hT_b = ps(nm + "phT", [P, FC, P])
        y_b = ps(nm + "py", [P, 512])
        c_in = sem(nm + "c_in")
        x_in = [sem(f"{nm}x_in{s}") for s in range(2)]
        y_out = [sem(f"{nm}y_out{s}") for s in range(2)]
        xT_ps, xT_copied, h_ps, h_read, h_ready, hT_ps, gelu_done, y_ps, y_done = (
            sem(nm + c) for c in ("xT_ps", "xT_copied", "h_ps", "h_read", "h_ready", "hT_ps", "gelu_done",
                                  "y_ps", "y_done"))
        aggr, var, rsq = (sem(nm + c) for c in ("aggr", "var", "rsq"))
        if not norm:
            h_read = h_ready
        with nc.Block() as block:
            @block.sync
            def _(sp):
                sp.dma_start(b2[:, :], a[f"L{L}_ffn_b2"].partition_broadcast(P)).then_inc(c_in, 16)
                sp.dma_start(bt[:, :], a[f"L{L}_ffn_bt"]).then_inc(c_in, 16)
                if norm:
                    sp.dma_start(b1[:, :], a[f"L{L}_ffn_b1"].partition_broadcast(P)).then_inc(c_in, 16)
                    sp.dma_start(gt[:, :], a[f"L{L}_ffn_gt"]).then_inc(c_in, 16)
                late(sp)

                def step(j, s, first, more):
                    wait_pos(sp, xT_ps, j - 1)
                    sp.dma_start(xin[s][:, :], k.xs[bass.ds(j * P, P), :]).then_inc(x_in[s], 16)
                over_tiles(sp, step, 0)
                for s in range(2):
                    sp.wait_ge(y_out[s], 16 * (NTILES // 2))

            @block.tensor
            def _(pe):
                def turn(j, s):
                    pe.wait_ge(x_in[s], 8 * j + (8 if s else 16))
                    wait_pos(pe, xT_copied, j)
                    for c in range(DC):
                        mm = pe.transpose(xT_b[:, c * P:(c + 1) * P], xin[s][:, c * P:(c + 1) * P], k.ident)
                    mm.then_inc(xT_ps, 1)

                def layer1(j, s):
                    e = pe.value_load(k.owner[0:1, bass.ds(j, 1)], min_val=0, max_val=E - 1)
                    pe.wait_ge(xT_copied, j + 1)
                    wait_pos(pe, h_read, j - 1)
                    for c in range(F // 512):
                        for kk in range(DC):
                            mm = pe.matmul(h_b[s][:, c * 512:(c + 1) * 512], xT[s][:, kk, :],
                                           w1[:, bass.ds(e * (DC * F) + (kk * F + c * 512), 512)],
                                           start=(kk == 0), stop=(kk == DC - 1))
                    mm.then_inc(h_ps, 1)

                def step(j, s, first, more):
                    sa = (s + A) % 2
                    if more(A):
                        turn(j + A, sa)
                    pe.wait_ge(h_ready, j + 1)
                    wait_pos(pe, gelu_done, j)
                    for f in range(FC):
                        mm = pe.transpose(hT_b[:, f, :], h[s][:, f * P:(f + 1) * P], k.ident)
                    mm.then_inc(hT_ps, 1)
                    if more(A):
                        layer1(j + A, sa)
                    e = pe.value_load(k.owner[0:1, bass.ds(j, 1)], min_val=0, max_val=E - 1)
                    pe.wait_ge(gelu_done, j + 1)
                    wait_pos(pe, y_done, j)
                    for f in range(FC):
                        mm = pe.matmul(y_b[:, 0:D], hT[s][:, f, :], w2[:, bass.ds(e * (FC * D) + f * D, D)],
                                       start=(f == 0), stop=(f == FC - 1))
                    mm.then_inc(y_ps, 1)

                pe.wait_ge(k.w_in, k.w_count)
                for j in range(A):
                    turn(j, j)
                    layer1(j, j)
                over_tiles(pe, step, A)

            @block.scalar
            def _(act):
                def copy(j, s):
                    act.wait_ge(xT_ps, j + 1)
                    act.activation(xT[s][:, :, :], xT_b[:, 0:D].rearrange("p (c q) -> p c q", c=DC),
                                   ACT.Copy).then_inc(xT_copied, 1)

                def store(j, s):
                    act.wait_ge(y_done, j + 1)
                    act.dma_start(k.ys[bass.ds(j * P, P), :], y[s][:, :]).then_inc(y_out[s], 16)

                def step(j, s, first, more):
                    if more(A):
                        copy(j + A, (s + A) % 2)
                    e = act.value_load(k.owner[0:1, bass.ds(j, 1)], min_val=0, max_val=E - 1)
                    act.wait_ge(hT_ps, j + 1)
                    for f in range(FC):
                        col = bass.ds(e * FC + f, 1)
                        g = act.activation(hT[s][:, f, :], hT_b[:, f, :], ACT.Gelu, bias=bt[:, col],
                                           scale=gt[:, col] if norm else 1.0)
                    g.then_inc(gelu_done, 1)
                    if not (isinstance(j, int) and j == 0):
                        store(j - 1, 1 - s)

                act.wait_ge(c_in, 64 if norm else 32)
                for j in range(A):
                    copy(j, j)
                over_tiles(act, step, A)
                store(NTILES - 1, 1)

            @block.vector
            def _(dve):
                def hidden(j, s):
                    if not norm:
                        dve.wait_ge(h_ps, j + 1)
                        dve.tensor_copy(h[s][:, :], h_b[s][:, :]).then_inc(h_ready, 1)
                        return
                    e = dve.value_load(k.owner[0:1, bass.ds(j, 1)], min_val=0, max_val=E - 1)
                    dve.wait_ge(h_ps, j + 1)
                    dve.tensor_tensor(h[s][:, :], h_b[s][:, :], b1[:, bass.ds(e * F, F)], ALU.add).then_inc(h_read, 1)
                    dve.wait_ge(h_read, j + 1)
                    dve.bn_stats(st[s][:, :], h[s][:, :])
                    dve.drain()
                    dve.bn_aggr(mv[s][:, :], st[s][:, :]).then_inc(aggr, 1)
                    dve.wait_ge(aggr, j + 1)
                    dve.tensor_scalar(ve[s][:, :], mv[s][:, 1:2], EPS, None, ALU.add).then_inc(var, 1)

                def centre(j, s):
                    dve.wait_ge(rsq, j + 1)
                    dve.tensor_scalar(h[s][:, :], h[s][:, :], mv[s][:, 0:1], rs[s][:, :],
                                      ALU.subtract, ALU.mult).then_inc(h_ready, 1)

                def step(j, s, first, more):
                    if more(A):
                        hidden(j + A, (s + A) % 2)
                    e = dve.value_load(k.owner[0:1, bass.ds(j, 1)], min_val=0, max_val=E - 1)
                    dve.wait_ge(y_ps, j + 1)
                    if not first:
                        wait_pos(dve, y_out[s], 8 * j - (8 if s else 0))
                    dve.tensor_tensor(y[s][:, :], y_b[:, 0:D], b2[:, bass.ds(e * D, D)], ALU.add).then_inc(y_done, 1)
                    if norm and more(A):
                        centre(j + A, (s + A) % 2)

                dve.wait_ge(c_in, 64 if norm else 32)
                for j in range(A):
                    hidden(j, j)
                    if norm:
                        centre(j, j)
                over_tiles(dve, step, A)

            if norm:
                @block.gpsimd
                def _(pool):
                    def step(j, s, first, more):
                        pool.wait_ge(var, j + 1)
                        pool.tensor_tensor(rs[s][:, :], ve[s][:, :], k.half[:, 0:1], ALU.pow).then_inc(rsq, 1)
                    over_tiles(pool, step, 0)


def combine(nc, k, L):
    ctx, sb, ps, sem = scoped(k)
    nm = f"c{L}_"
    with ctx:
        got = [[sb(f"{nm}g{j}_{r}", [P, D]) for r in range(RING)] for j in range(TOPK)]
        before = 32 * (NT // RING) * k.mixtures
        part, whole = sem(nm + "part"), sem(nm + "whole")
        with nc.Block() as block:
            @block.gpsimd
            def _(pool):
                for n in range(NT):
                    wait_pos(pool, whole, n - RING + 1)
                    for j in range(TOPK):
                        pool.indirect_dma_start(
                            out=got[j][n % RING][:, :], out_offset=None, in_=k.ys[:, :],
                            in_offset=bass.IndirectOffsetOnAxis(ap=k.pos[j][:, n:n + 1], axis=0)
                        ).then_inc(k.g_in[n % RING], 16)

            @block.vector
            def _(dve):
                acc = k.z if L == 0 else k.x
                with dve.Fori(0, NT // RING) as i:
                    for r in range(RING):
                        n = i * RING + r
                        at = acc[:, bass.ds(n * D, D)]
                        dve.wait_ge(k.g_in[r], i * 32 + (32 + before))
                        dve.scalar_tensor_tensor(at, got[0][r][:, :], k.wt[0][:, bass.ds(n, 1)], at,
                                                 ALU.mult, ALU.add).then_inc(part, 1)
                        dve.wait_ge(part, n + 1)
                        dve.scalar_tensor_tensor(at, got[1][r][:, :], k.wt[1][:, bass.ds(n, 1)], at,
                                                 ALU.mult, ALU.add).then_inc(whole, 1)
                        dve.wait_ge(whole, n + 1)
                        dve.bn_stats(k.stats[:, bass.ds(n, 1), :], at)


def post_norm(nc, k):
    ctx, sb, ps, sem = scoped(k)
    nm = "pn_"
    with ctx:
        g, b_ = sb(nm + "g", [P, D]), sb(nm + "b", [P, D])
        w_in, u_done, m_done, b_done, x_done = (sem(nm + c) for c in ("w_in", "u", "m", "b_done", "x"))
        span = lambda t, b: t[:, bass.ds(b * (TPB * D), TPB * D)].rearrange("p (t d) -> p t d", t=TPB)
        bc = lambda t: t[:, None, :].to_broadcast([P, TPB, D])
        with nc.Block() as block:
            @block.sync
            def _(sp):
                sp.dma_start(g[:, :], k.a["L0_ffn_ln_g"].partition_broadcast(P)).then_inc(w_in, 16)
                sp.dma_start(b_[:, :], k.a["L0_ffn_ln_b"].partition_broadcast(P)).then_inc(w_in, 16)

            @block.gpsimd
            def _(pool):
                pool.wait_ge(w_in, 32)
                with pool.Fori(0, NB) as b:
                    pool.tensor_tensor(span(k.x, b), span(k.x, b), bc(b_), ALU.add).then_inc(b_done, 1)

            @block.vector
            def _(dve):
                dve.wait_ge(w_in, 32)
                with dve.Fori(0, NB) as b:
                    for t in range(TPB):
                        n = b * TPB + t
                        at = k.z[:, bass.ds(n * D, D)]
                        v = dve.tensor_scalar(at, at, k.mean[:, bass.ds(n, 1)], k.rstd[:, bass.ds(n, 1)],
                                              ALU.subtract, ALU.mult)
                    v.then_inc(u_done, 1)
                    dve.wait_ge(u_done, b + 1)
                    dve.tensor_tensor(span(k.z, b), span(k.z, b), bc(g), ALU.mult).then_inc(m_done, 1)
                    dve.wait_ge(m_done, b + 1)
                    dve.wait_ge(b_done, b + 1)
                    dve.tensor_tensor(span(k.x, b), span(k.x, b), span(k.z, b), ALU.add).then_inc(x_done, 1)
                    dve.wait_ge(x_done, b + 1)
                    for t in range(TPB):
                        n = b * TPB + t
                        dve.bn_stats(k.stats[:, bass.ds(n, 1), :], k.xt(n))


def mixture(nc, k, L):
    ctx, sb, ps, sem = scoped(k)
    with ctx:
        k.logits = sb(f"x{L}_logits", [P, NT, E])
        k.pos = [sb(f"x{L}_pos{j}", [P, NT], U32) for j in range(TOPK)]
        k.wt = [sb(f"x{L}_wt{j}", [P, NT]) for j in range(TOPK)]
        k.owner = sb(f"x{L}_owner", [1, NTILES], I32)
        if L == 0:
            k.z = sb("x0_z", [P, NT * D])
        else:
            k.z = k.w1[:, NT * D:]
        router(nc, k, L)
        route(nc, k, L)
        experts(nc, k, L, k.late)
        combine(nc, k, L)
        k.mixtures += 1
        if L == 0:
            ln_scalars(nc, k, "pn")
            post_norm(nc, k)


def quantum_ffn(nc, k):
    ctx, sb, ps, sem = scoped(k)
    nm = "f1_"
    a = k.a
    FC = F1 // P
    with ctx:
        w1, w2 = sb(nm + "w1", [P, DC, F1]), sb(nm + "w2", [P, FC, D])
        par = sb(nm + "par", [P, 4, FC])
        b2 = sb(nm + "b2", [P, D])
        turn_t, half_t, cs, c_ = (sb(nm + n, [P, 2, FC]) for n in ("turn", "near", "cs", "c"))
        z = [sb(f"{nm}z{s}", [P, TPB, D]) for s in range(2)]
        zT = [sb(f"{nm}zT{s}", [P, DC, SEQ]) for s in range(2)]
        u = [sb(f"{nm}u{s}", [P, SEQ]) for s in range(2)]
        near = [sb(f"{nm}near{s}", [P, SEQ]) for s in range(2)]
        q = [sb(f"{nm}q{s}", [P, FC, SEQ]) for s in range(2)]
        bank = ps(nm + "bank", [P, DC, SEQ])
        hb = [ps(f"{nm}h{i}", [P, SEQ]) for i in range(2)]
        yb = [ps(f"{nm}y{s}", [P, 512]) for s in range(2)]
        w_in, v, sc = sem(nm + "w_in"), sem(nm + "v"), sem(nm + "sc")
        z_done, b_done, zT_ps, zT_copied, h_ps, u_done, near_done, frac, sine, mixed, q_done, y_ps, x_added = (
            sem(nm + n) for n in ("z", "b", "zT_ps", "zT_copied", "h_ps", "u", "near", "frac", "sine",
                                  "mixed", "q", "y_ps", "x"))
        with nc.Block() as block:
            @block.sync
            def _(sp):
                sp.dma_start(w1[:, :, :], a["L1_ffn_W1"]).then_inc(w_in, 16)
                sp.dma_start(w2[:, :, :], a["L1_ffn_W2"]).then_inc(w_in, 16)
                sp.dma_start(par[:, :, :], a["L1_ffn_par"]).then_inc(w_in, 16)
                sp.dma_start(b2[:, :], a["L1_ffn_b2"].partition_broadcast(P)).then_inc(w_in, 16)

            @block.gpsimd
            def _(pool):
                pool.wait_ge(w_in, 64)

                def step(b, s, first, last):
                    pool.wait_ge(z_done, b + 1)
                    xs = k.x[:, bass.ds(b * (TPB * D), TPB * D)].rearrange("p (t d) -> p t d", t=TPB)
                    pool.tensor_tensor(xs, xs, b2[:, None, :].to_broadcast([P, TPB, D]), ALU.add).then_inc(b_done, 1)
                over_batches(pool, step)

            @block.vector
            def _(dve):
                dve.wait_ge(w_in, 64)
                b1, th, wr, wi = (par[:, j, :] for j in range(4))
                tn, tc = turn_t[:, 0, :], turn_t[:, 1, :]
                n = [0]

                def then(op):
                    n[0] += 1
                    op.then_inc(v, 1)
                    dve.wait_ge(v, n[0])

                parts, rest = [], TWO_PI
                for _i in range(2):
                    hi = float(np.float32(np.round(rest * 2 ** (9 + 11 * _i)) / 2 ** (9 + 11 * _i)))
                    parts.append(hi)
                    rest -= hi
                parts.append(float(np.float32(rest)))
                kt = half_t[:, 0, :]
                then(dve.tensor_scalar(kt, th, 1.0 / TWO_PI, MAGIC, ALU.mult, ALU.add))
                then(dve.tensor_scalar(kt, kt, MAGIC, None, ALU.subtract))
                red = half_t[:, 1, :]
                then(dve.scalar_tensor_tensor(red, kt, -parts[0], th, ALU.mult, ALU.add))
                then(dve.scalar_tensor_tensor(red, kt, -parts[1], red, ALU.mult, ALU.add))
                then(dve.scalar_tensor_tensor(red, kt, -parts[2], red, ALU.mult, ALU.add))
                then(dve.tensor_scalar(tn, red, 1.0 / TWO_PI, None, ALU.mult))
                then(dve.tensor_scalar(tc, tn, 0.25, None, ALU.add))
                for j in range(2):
                    then(dve.tensor_scalar(half_t[:, j, :], turn_t[:, j, :], MAGIC, None, ALU.add))
                    then(dve.tensor_scalar(half_t[:, j, :], half_t[:, j, :], MAGIC, None, ALU.subtract))
                    then(dve.tensor_tensor(half_t[:, j, :], turn_t[:, j, :], half_t[:, j, :], ALU.subtract))
                dve.wait_ge(sc, 1)
                then(dve.tensor_tensor(c_[:, 0, :], cs[:, 1, :], wr, ALU.mult))
                then(dve.tensor_tensor(c_[:, 1, :], cs[:, 0, :], wi, ALU.mult))
                then(dve.tensor_tensor(c_[:, 0, :], c_[:, 0, :], c_[:, 1, :], ALU.add))
                then(dve.scalar_tensor_tensor(c_[:, 0, :], c_[:, 0, :], 0.1, wi, ALU.mult, ALU.mult))
                then(dve.scalar_tensor_tensor(c_[:, 1, :], b1, 0.1 / TWO_PI, tn, ALU.mult, ALU.add))
                assert n[0] == F1_CHAIN

                def normalise(b, s):
                    wait_pos(dve, zT_ps, b - 1)
                    for t in range(TPB):
                        m = b * TPB + t
                        o = dve.tensor_scalar(z[s][:, t, :], k.xt(m), k.mean[:, bass.ds(m, 1)],
                                              k.rstd[:, bass.ds(m, 1)], ALU.subtract, ALU.mult)
                    o.then_inc(z_done, 1)

                def fraction(m, f):
                    dve.wait_ge(u_done, m + 1)
                    dve.tensor_scalar(near[f % 2][:, :], u[f % 2][:, :], MAGIC, MAGIC, ALU.add,
                                      ALU.subtract).then_inc(near_done, 1)
                    dve.wait_ge(near_done, m + 1)
                    dve.tensor_tensor(u[f % 2][:, :], u[f % 2][:, :], near[f % 2][:, :], ALU.subtract).then_inc(frac, 1)

                def mix(m, f, s):
                    dve.wait_ge(sine, m + 1)
                    dve.scalar_tensor_tensor(q[s][:, f, :], u[f % 2][:, :], c_[:, 0, f:f + 1],
                                             hb[f % 2][:, :], ALU.mult, ALU.add).then_inc(mixed, 1)
                    dve.wait_ge(mixed, m + 1)
                    dve.tensor_scalar(q[s][:, f, :], q[s][:, f, :], par[:, 0, f:f + 1], 0.0,
                                      ALU.add, ALU.max).then_inc(q_done, 1)

                def hidden(b, s):
                    for f in range(FC):
                        fraction(b * FC + f, f)
                        if f > 0:
                            mix(b * FC + f - 1, f - 1, s)
                    mix(b * FC + FC - 1, FC - 1, s)

                def residual(b, t):
                    m = b * TPB + t
                    dve.wait_ge(y_ps, m + 1)
                    dve.tensor_tensor(k.xt(m), yb[t % 2][:, 0:D], k.xt(m), ALU.add).then_inc(x_added, 1)

                def statistics(b, t):
                    m = b * TPB + t
                    dve.wait_ge(x_added, m + 1)
                    dve.bn_stats(k.stats[:, bass.ds(m, 1), :], k.xt(m))

                def step(b, s, first, last):
                    dve.wait_ge(b_done, b + 1)
                    for f in range(FC):
                        if not last:
                            fraction((b + 1) * FC + f, f)
                            if f > 0:
                                mix((b + 1) * FC + f - 1, f - 1, 1 - s)
                        if f % 2 == 1:
                            residual(b, f // 2)
                        elif f > 0:
                            statistics(b, f // 2 - 1)
                    if not last:
                        mix((b + 1) * FC + FC - 1, FC - 1, 1 - s)
                    statistics(b, TPB - 1)

                normalise(0, 0)
                normalise(1, 1)
                hidden(0, 0)

                def body(b, s, first, last):
                    if not first and not last:
                        normalise(b + 1, 1 - s)
                    step(b, s, first, last)
                over_batches(dve, body)

            @block.scalar
            def _(act):
                act.wait_ge(v, F1_CHAIN - 5)
                act.activation(cs[:, :, :], half_t[:, :, :], ACT.Sin, scale=TWO_PI).then_inc(sc, 1)
                act.wait_ge(v, F1_CHAIN)

                def copy(b, s):
                    act.wait_ge(zT_ps, b + 1)
                    act.activation(zT[s][:, :, :], bank[:, :, :], ACT.Copy).then_inc(zT_copied, 1)

                def turns(m, f):
                    act.wait_ge(h_ps, m + 1)
                    act.activation(u[f % 2][:, :], hb[f % 2][:, :], ACT.Identity, bias=c_[:, 1, f:f + 1],
                                   scale=0.1 / TWO_PI).then_inc(u_done, 1)

                def sines(m, f):
                    act.wait_ge(frac, m + 1)
                    act.activation(u[f % 2][:, :], u[f % 2][:, :], ACT.Sin, scale=TWO_PI).then_inc(sine, 1)

                def hidden(b):
                    for f in range(FC):
                        wait_pos(act, mixed, b * FC + f - 1)
                        turns(b * FC + f, f)
                        if f > 0:
                            sines(b * FC + f - 1, f - 1)
                    sines(b * FC + FC - 1, FC - 1)

                copy(0, 0)
                copy(1, 1)
                hidden(0)

                def step(b, s, first, last):
                    if not first and not last:
                        copy(b + 1, 1 - s)
                    if not last:
                        hidden(b + 1)
                over_batches(act, step)

            @block.tensor
            def _(pe):
                pe.wait_ge(w_in, 64)

                def turn(b, s):
                    pe.wait_ge(z_done, b + 1)
                    wait_pos(pe, zT_copied, b)
                    for c in range(DC):
                        for t in range(TPB):
                            mm = pe.transpose(bank[:, c, t * P:(t + 1) * P], z[s][:, t, c * P:(c + 1) * P], k.ident)
                    mm.then_inc(zT_ps, 1)

                def hidden(b, s, f):
                    m = b * FC + f
                    wait_pos(pe, mixed, m - 1)
                    for kk in range(DC):
                        mm = pe.matmul(hb[f % 2][:, :], w1[:, kk, f * P:(f + 1) * P], zT[s][:, kk, :],
                                       start=(kk == 0), stop=(kk == DC - 1))
                    mm.then_inc(h_ps, 1)

                def second(b, s, f):
                    t, half = f // 2, f % 2
                    m = b * TPB + t
                    if half == 0:
                        if f == 0:
                            pe.wait_ge(q_done, (b + 1) * FC)
                        wait_pos(pe, x_added, m - 1)
                    for g in range(half * FC // 2, (half + 1) * FC // 2):
                        mm = pe.matmul(yb[t % 2][:, 0:D], q[s][:, g, t * P:(t + 1) * P], w2[:, g, :],
                                       start=(g == 0), stop=(g == FC - 1))
                    if half:
                        mm.then_inc(y_ps, 1)

                turn(0, 0)
                turn(1, 1)
                pe.wait_ge(zT_copied, 1)
                for f in range(FC):
                    hidden(0, 0, f)

                def step(b, s, first, last):
                    if not first and not last:
                        turn(b + 1, 1 - s)
                    if not last:
                        pe.wait_ge(zT_copied, b + 2)
                    for f in range(FC):
                        if not last:
                            hidden(b + 1, 1 - s, f)
                        second(b, s, f)
                over_batches(pe, step)


F1_CHAIN = 18


def window_attention(nc, k):
    ctx, sb, ps, sem = scoped(k)
    nm = "a2_"
    a = k.a
    with ctx:
        wa, wc = sb(nm + "wa", [P, DC, D]), sb(nm + "wc", [P, 2 * DC, D])
        pt, ln = sb(nm + "pt", [P, NB]), sb(nm + "ln", [P, NB], I32)
        lo, hi, lf = sb(nm + "lo", [P, NB]), sb(nm + "hi", [P, NB]), sb(nm + "lf", [P, NB])
        keep, k2, neg = (sb(nm + n, [P, NB, S]) for n in ("keep", "k2", "neg"))
        dist, gauss = sb(nm + "dist", [P, NB]), sb(nm + "gauss", [P, NB])
        cx = [sb(f"{nm}cx{s}", [P, DC, 2, S]) for s in range(2)]
        z = [sb(f"{nm}z{s}", [P, TPB, D]) for s in range(2)]
        zT = [sb(f"{nm}zT{s}", [P, DC, SEQ]) for s in range(2)]
        ac = [sb(f"{nm}ac{s}", [P, DC, S]) for s in range(2)]
        cc = [sb(f"{nm}cc{s}", [P, D]) for s in range(2)]
        pr = [sb(f"{nm}pr{s}", [P, TPB, S]) for s in range(2)]
        mx, sm, rc = (sb(nm + n, [P, TPB]) for n in ("mx", "sm", "rc"))
        pT = sb(nm + "pT", [P, TPB // 2 * P])
        th = [sb(f"{nm}th{s}", [P, D]) for s in range(2)]
        bank = ps(nm + "bank", [P, DC, SEQ])
        cb, sbk, tb = ps(nm + "cb", [P, 512]), ps(nm + "sb", [P, 512]), ps(nm + "tb", [P, 512])
        yb = [ps(f"{nm}yb{s}", [P, 512]) for s in range(2)]
        w_in, v, pv, ga = (sem(nm + n) for n in ("w_in", "v", "pv", "ga"))
        cx_in = [sem(f"{nm}cx_in{s}") for s in range(2)]
        (z_done, zT_ps, zT_copied, c_ps, c_read, s_ps, s_read, s_masked, s_max, s_sub, e_done, s_sum, s_rec,
         p_done, t_ps, t_copied, y_ps, t_done, x_added) = (
            sem(nm + n) for n in ("z", "zT_ps", "zT_copied", "c_ps", "c_read", "s_ps", "s_read", "s_masked",
                                  "s_max", "s_sub", "e", "s_sum", "s_rec", "p", "t_ps", "t_copied", "y_ps",
                                  "tanh", "x"))
        with nc.Block() as block:
            @block.sync
            def _(sp):
                sp.dma_start(wa[:, :, :], a["L2_Wa"]).then_inc(w_in, 16)
                sp.dma_start(wc[:, :, :], a["L2_Wc"]).then_inc(w_in, 16)
                sp.dma_start(pt[:, :], a["pt"].partition_broadcast(P)).then_inc(w_in, 16)
                sp.dma_start(ln[:, :], a["len"].partition_broadcast(P)).then_inc(w_in, 16)

                def step(b, s, first, last):
                    wait_pos(sp, c_ps, b - 1)
                    for j in range(2):
                        sp.dma_start(cx[s][:, :, j, :],
                                     a["ctxT"][bass.ds(b, 1)].rearrange("b p c l -> p (b c) l")).then_inc(cx_in[s], 16)
                over_batches(sp, step)

            @block.vector
            def _(dve):
                n = [0]

                def then(op):
                    n[0] += 1
                    op.then_inc(v, 1)
                    dve.wait_ge(v, n[0])

                dve.wait_ge(w_in, 64)
                idx = k.cst[:, None, C_L:C_L + S].to_broadcast([P, NB, S])
                bc = lambda t: t[:, :, None].to_broadcast([P, NB, S])
                then(dve.tensor_copy(lf[:, :], ln[:, :]))
                then(dve.tensor_scalar(lo[:, :], pt[:, :], WINDOW, 0.0, ALU.subtract, ALU.max))
                then(dve.scalar_tensor_tensor(hi[:, :], pt[:, :], WINDOW, lf[:, :], ALU.add, ALU.min))
                then(dve.tensor_tensor(keep[:, :, :], idx, bc(lo), ALU.is_ge))
                then(dve.tensor_tensor(k2[:, :, :], idx, bc(hi), ALU.is_le))
                then(dve.tensor_tensor(keep[:, :, :], keep[:, :, :], k2[:, :, :], ALU.mult))
                then(dve.tensor_scalar(neg[:, :, :], keep[:, :, :], 1.0, 1e9, ALU.subtract, ALU.mult))
                then(dve.tensor_scalar(dist[:, :], pt[:, :], k.cst[:, C_P:C_P + 1], None, ALU.subtract))
                then(dve.tensor_tensor(dist[:, :], dist[:, :], dist[:, :], ALU.mult))
                dve.wait_ge(ga, 1)

                def normalise(b, s):
                    wait_pos(dve, zT_ps, b - 1)
                    for t in range(TPB):
                        m = b * TPB + t
                        o = dve.tensor_scalar(z[s][:, t, :], k.xt(m), k.mean[:, bass.ds(m, 1)],
                                              k.rstd[:, bass.ds(m, 1)], ALU.subtract, ALU.mult)
                    o.then_inc(z_done, 1)

                def prepare(b, s):
                    dve.wait_ge(c_ps, b + 1)
                    dve.tensor_copy(ac[s][:, :, :], cb[:, 0:DC * S].rearrange("p (c l) -> p c l", c=DC))
                    dve.tensor_scalar(cc[s][:, :], cb[:, D:2 * D], gauss[:, bass.ds(b, 1)], None,
                                      ALU.mult).then_inc(c_read, 1)

                def softmax(b, s):
                    p = pr[s][:, :, :]
                    at = lambda t: t[:, bass.ds(b, 1), :].to_broadcast([P, TPB, S])
                    bt = lambda t: t[:, :, None].to_broadcast([P, TPB, S])
                    dve.wait_ge(s_ps, b + 1)
                    dve.tensor_tensor(p, sbk[:, 0:TPB * S].rearrange("p (t l) -> p t l", t=TPB), at(keep),
                                      ALU.mult).then_inc(s_read, 1)
                    dve.wait_ge(s_read, b + 1)
                    dve.tensor_tensor(p, p, at(neg), ALU.add).then_inc(s_masked, 1)
                    dve.wait_ge(s_masked, b + 1)
                    dve.tensor_reduce(mx[:, :], p, AX.X, ALU.max).then_inc(s_max, 1)
                    dve.wait_ge(s_max, b + 1)
                    dve.tensor_tensor(p, p, bt(mx), ALU.subtract).then_inc(s_sub, 1)
                    dve.wait_ge(e_done, b + 1)
                    dve.tensor_reduce(sm[:, :], p, AX.X, ALU.add).then_inc(s_sum, 1)
                    dve.wait_ge(s_sum, b + 1)
                    dve.reciprocal(rc[:, :], sm[:, :]).then_inc(s_rec, 1)
                    dve.wait_ge(s_rec, b + 1)
                    dve.tensor_tensor(p, p, bt(rc), ALU.mult).then_inc(p_done, 1)

                def residual(b, s):
                    for t in range(TPB):
                        m = b * TPB + t
                        dve.wait_ge(t_done, m + 1)
                        dve.tensor_tensor(k.xt(m), th[t % 2][:, :], k.xt(m), ALU.add).then_inc(x_added, 1)
                    for t in range(TPB):
                        m = b * TPB + t
                        dve.wait_ge(x_added, m + 1)
                        dve.bn_stats(k.stats[:, bass.ds(m, 1), :], k.xt(m))

                def step(b, s, first, last):
                    if not last:
                        normalise(b + 1, 1 - s)
                        prepare(b + 1, 1 - s)
                    softmax(b, s)
                    residual(b, s)

                normalise(0, 0)
                prepare(0, 0)
                over_batches(dve, step)

            @block.scalar
            def _(act):
                act.wait_ge(v, 9)
                act.activation(gauss[:, :], dist[:, :], ACT.Exp, scale=-1.0 / DEV_POW).then_inc(ga, 1)

                def copy(b, s):
                    act.wait_ge(zT_ps, b + 1)
                    wait_pos(act, y_ps, (b - 1) * TPB)
                    act.activation(zT[s][:, :, :], bank[:, :, :], ACT.Copy).then_inc(zT_copied, 1)

                def step(b, s, first, last):
                    if not last:
                        copy(b + 1, 1 - s)
                    act.wait_ge(s_sub, b + 1)
                    act.activation(pr[s][:, :, :], pr[s][:, :, :], ACT.Exp).then_inc(e_done, 1)
                    act.wait_ge(t_ps, b + 1)
                    act.activation(pT[:, :], tb[:, 0:TPB // 2 * P], ACT.Copy).then_inc(t_copied, 1)
                    for t in range(TPB):
                        m = b * TPB + t
                        act.wait_ge(y_ps, m + 1)
                        wait_pos(act, x_added, m - 1)
                        act.activation(th[t % 2][:, :], yb[t % 2][:, 0:D], ACT.Tanh).then_inc(t_done, 1)

                copy(0, 0)
                act.wait_ge(w_in, 64)
                k.ahead(act)
                over_batches(act, step)

            @block.tensor
            def _(pe):
                pe.wait_ge(w_in, 64)

                def turn(b, s):
                    pe.wait_ge(z_done, b + 1)
                    wait_pos(pe, zT_copied, b)
                    for c in range(DC):
                        for t in range(TPB):
                            mm = pe.transpose(bank[:, c, t * P:(t + 1) * P], z[s][:, t, c * P:(c + 1) * P], k.ident)
                    mm.then_inc(zT_ps, 1)

                def prepare(b, s):
                    pe.wait_ge(cx_in[s], 16 * b + (16 if s else 32))
                    wait_pos(pe, c_read, b)
                    for c in range(DC):
                        for kk in range(DC):
                            pe.matmul(cb[:, c * S:(c + 1) * S], wa[:, kk, c * P:(c + 1) * P], cx[s][:, kk, 0, :],
                                      start=(kk == 0), stop=(kk == DC - 1))
                    for kk in range(DC):
                        mm = pe.matmul(cb[:, D:2 * D], cx[s][:, kk, :, :].rearrange("p j l -> p (j l)"), wc[:, kk, :],
                                       start=(kk == 0), stop=(kk == DC - 1))
                    mm.then_inc(c_ps, 1)

                def step(b, s, first, last):
                    if not last:
                        turn(b + 1, 1 - s)
                        prepare(b + 1, 1 - s)
                    pe.wait_ge(zT_copied, b + 1)
                    pe.wait_ge(c_read, b + 1)
                    wait_pos(pe, s_read, b)
                    for t in range(TPB):
                        for kk in range(DC):
                            mm = pe.matmul(sbk[:, t * S:(t + 1) * S], zT[s][:, kk, t * P:(t + 1) * P], ac[s][:, kk, :],
                                           start=(kk == 0), stop=(kk == DC - 1))
                    mm.then_inc(s_ps, 1)
                    pe.wait_ge(p_done, b + 1)
                    for g in range(TPB // 2):
                        mm = pe.transpose(tb[:, g * P:(g + 1) * P],
                                          pr[s][:, 2 * g:2 * g + 2, :].rearrange("p t l -> p (t l)"), k.ident)
                    mm.then_inc(t_ps, 1)
                    pe.wait_ge(t_copied, b + 1)
                    for t in range(TPB):
                        m = b * TPB + t
                        wait_pos(pe, t_done, m - 1)
                        for kk in range(DC):
                            pe.matmul(yb[t % 2][:, 0:D], zT[s][:, kk, t * P:(t + 1) * P], wc[:, DC + kk, :],
                                      start=(kk == 0), stop=False)
                        half = slice(t % 2 * S, (t % 2 + 1) * S)
                        pe.matmul(yb[t % 2][:, 0:D], pT[half, t // 2 * P:(t // 2 + 1) * P], cc[s][half, :],
                                  start=False, stop=True).then_inc(y_ps, 1)

                turn(0, 0)
                prepare(0, 0)
                over_batches(pe, step)


def ternary_ffn(nc, k, out):
    ctx, sb, ps, sem = scoped(k)
    nm = "f3_"
    a = k.a
    FC = F3 // P
    with ctx:
        z = [sb(f"{nm}z{s}", [P, TPB, D]) for s in range(2)]
        xq = [sb(f"{nm}xq{s}", [P, TPB, D], BF16) for s in range(2)]
        xT = [sb(f"{nm}xT{s}", [P, DC, SEQ], BF16) for s in range(2)]
        am, sc, rc = (sb(nm + n, [P, TPB]) for n in ("am", "sc", "rc"))
        sg = [sb(f"{nm}sg{s}", [P, TPB]) for s in range(2)]
        su = [sb(f"{nm}su{s}", [P, TPB]) for s in range(2)]
        g_ = [sb(f"{nm}g{s}", [P, F3]) for s in range(2)]
        h = [sb(f"{nm}h{s}", [P, F3]) for s in range(2)]
        hq = [sb(f"{nm}hq{s}", [P, F3], BF16) for s in range(2)]
        hm, hr, hs, hd = ([sb(f"{nm}{n}{s}", [P, 1]) for s in range(2)] for n in ("hm", "hr", "hs", "hd"))
        hT = [sb(f"{nm}hT{s}", [P, FC, P], BF16) for s in range(2)]
        ident = sb(nm + "ident", [P, P], BF16)
        wq = {c: sb(nm + "wq" + c, [P, 2 * F3], BF16) for c in "gud"}
        wsum, wmean, wscale = (sb(nm + n, [P, 3]) for n in ("wsum", "wmean", "wscale"))
        xb = ps(nm + "xb", [P, DC, SEQ], BF16)
        gb, ub = ps(nm + "gb", [P, F3]), ps(nm + "ub", [P, F3])
        hb = ps(nm + "hb", [P, FC, P], BF16)
        yb = [ps(f"{nm}yb{s}", [P, 512]) for s in range(2)]
        w_in, v, tot_ps, ready = (sem(nm + n) for n in ("w_in", "v", "tot", "ready"))
        (z_done, z_max, z_clip, z_rec, z_scale, z_mul, xq_done, x_ps, x_copied, g_ps, g_done, h_done, h_max,
         h_clip, h_rec, h_scale, h_mul, hq_done, h_tp, h_copied, y_ps, x_added) = (
            sem(nm + n) for n in ("z", "z_max", "z_clip", "z_rec", "z_scale", "z_mul", "xq", "x_ps", "x_copied",
                                  "g_ps", "g_done", "h", "h_max", "h_clip", "h_rec", "h_scale", "h_mul", "hq",
                                  "h_tp", "h_copied", "y_ps", "x"))
        stored = sem(nm + "stored")
        N3 = 2 * F3
        with ExitStack() as wctx:
            raw = [wctx.enter_context(nc.sbuf_tensor(f"{nm}raw{c}", [P, N3], F32)) for c in "gud"]
            tb = yb[0]
            with nc.Block() as block:
                @block.sync
                def _(sp):
                    for j, c in enumerate(("gate", "up", "down")):
                        sp.dma_start(raw[j][:, :], a[f"L3_ffn_w_{c}"]).then_inc(w_in, 16)

                @block.vector
                def _(dve):
                    n = [0]

                    def then(op):
                        n[0] += 1
                        op.then_inc(v, 1)
                        dve.wait_ge(v, n[0])

                    dve.wait_ge(w_in, 48)
                    for j in range(3):
                        dve.tensor_reduce(wsum[:, j:j + 1], raw[j][:, :], AX.X, ALU.add,
                                          apply_absolute_value=True).then_inc(v, 1)
                    n[0] = 3
                    dve.wait_ge(tot_ps, 1)
                    then(dve.tensor_scalar(wmean[:, :], tb[:, 0:3], 1.0 / (D * F3), 1e-5, ALU.mult, ALU.max))
                    then(dve.reciprocal(wscale[:, :], wmean[:, :]))
                    for j, c in enumerate("gud"):
                        then(dve.tensor_scalar(raw[j][:, :], raw[j][:, :], wscale[:, j:j + 1], MAGIC,
                                               ALU.mult, ALU.add))
                        then(dve.tensor_scalar(raw[j][:, :], raw[j][:, :], MAGIC, 1.0, ALU.subtract, ALU.min))
                        dve.tensor_scalar(wq[c][:, :], raw[j][:, :], -1.0, None, ALU.max)
                    dve.tensor_copy(ident[:, :], k.ident)

                @block.tensor
                def _(pe):
                    pe.wait_ge(v, 3)
                    pe.matmul(tb[:, 0:3], k.cst[:, C_ONE:C_ONE + P], wsum[:, :], start=True, stop=True).then_inc(tot_ps, 1)

        wg = wq["g"][:, :].rearrange("p (c f) -> p c f", c=DC)
        wu = wq["u"][:, :].rearrange("p (c f) -> p c f", c=DC)
        wd = wq["d"][:, :].rearrange("p (c f) -> p c f", c=FC)
        with nc.Block() as block:
            @block.vector
            def _(dve):
                def quantise(b, s):
                    wait_pos(dve, x_ps, b - 1)
                    for t in range(TPB):
                        m = b * TPB + t
                        o = dve.tensor_scalar(z[s][:, t, :], k.xt(m), k.mean[:, bass.ds(m, 1)],
                                              k.rstd[:, bass.ds(m, 1)], ALU.subtract, ALU.mult)
                    o.then_inc(z_done, 1)
                    dve.wait_ge(z_done, b + 1)
                    dve.tensor_reduce(am[:, :], z[s][:, :, :], AX.X, ALU.max, apply_absolute_value=True).then_inc(z_max, 1)
                    dve.wait_ge(z_max, b + 1)
                    dve.tensor_scalar(am[:, :], am[:, :], 1e-5, None, ALU.max).then_inc(z_clip, 1)
                    dve.wait_ge(z_clip, b + 1)
                    dve.reciprocal(rc[:, :], am[:, :]).then_inc(z_rec, 1)
                    dve.tensor_scalar(sg[s][:, :], am[:, :], 1.0 / 127.0, wmean[:, 0:1], ALU.mult, ALU.mult)
                    dve.tensor_scalar(su[s][:, :], am[:, :], 1.0 / 127.0, wmean[:, 1:2], ALU.mult, ALU.mult)
                    dve.wait_ge(z_rec, b + 1)
                    dve.tensor_scalar(sc[:, :], rc[:, :], 127.0, None, ALU.mult).then_inc(z_scale, 1)
                    dve.wait_ge(z_scale, b + 1)
                    for t in range(TPB):
                        o = dve.tensor_scalar(z[s][:, t, :], z[s][:, t, :], sc[:, t:t + 1], MAGIC, ALU.mult, ALU.add)
                    o.then_inc(z_mul, 1)
                    dve.wait_ge(z_mul, b + 1)
                    dve.tensor_scalar(xq[s][:, :, :], z[s][:, :, :], MAGIC, 127.0, ALU.subtract, ALU.min).then_inc(xq_done, 1)

                def hidden(m, t, s):
                    u = t % 2
                    dve.wait_ge(g_done, m + 1)
                    dve.scalar_tensor_tensor(h[u][:, :], ub[:, :], su[s][:, t:t + 1], g_[u][:, :],
                                             ALU.mult, ALU.mult).then_inc(h_done, 1)
                    dve.wait_ge(h_done, m + 1)
                    dve.tensor_reduce(hm[u][:, :], h[u][:, :], AX.X, ALU.max, apply_absolute_value=True).then_inc(h_max, 1)
                    dve.wait_ge(h_max, m + 1)
                    dve.tensor_scalar(hm[u][:, :], hm[u][:, :], 1e-5, None, ALU.max).then_inc(h_clip, 1)
                    dve.wait_ge(h_clip, m + 1)
                    dve.reciprocal(hr[u][:, :], hm[u][:, :]).then_inc(h_rec, 1)
                    dve.tensor_scalar(hd[u][:, :], hm[u][:, :], 1.0 / 127.0, wmean[:, 2:3], ALU.mult, ALU.mult)
                    dve.wait_ge(h_rec, m + 1)
                    dve.tensor_scalar(hs[u][:, :], hr[u][:, :], 127.0, None, ALU.mult).then_inc(h_scale, 1)
                    dve.wait_ge(h_scale, m + 1)
                    dve.tensor_scalar(h[u][:, :], h[u][:, :], hs[u][:, :], MAGIC, ALU.mult, ALU.add).then_inc(h_mul, 1)
                    dve.wait_ge(h_mul, m + 1)
                    dve.tensor_scalar(hq[u][:, :], h[u][:, :], MAGIC, 127.0, ALU.subtract, ALU.min).then_inc(hq_done, 1)

                def residual(m, t):
                    dve.wait_ge(y_ps, m + 1)
                    dve.scalar_tensor_tensor(k.xt(m), yb[t % 2][:, 0:D], hd[t % 2][:, :], k.xt(m),
                                             ALU.mult, ALU.add).then_inc(x_added, 1)

                def step(b, s, first, last):
                    for t in range(TPB):
                        m = b * TPB + t
                        if t == 1 and not last:
                            quantise(b + 1, 1 - s)
                        hidden(m, t, s)
                        if not (first and t == 0):
                            residual(m - 1, t - 1)

                quantise(0, 0)
                over_batches(dve, step)
                residual(NT - 1, TPB - 1)

            @block.scalar
            def _(act):
                def copy(b, s):
                    act.wait_ge(x_ps, b + 1)
                    act.activation(xT[s][:, :, :], xb[:, :, :], ACT.Copy).then_inc(x_copied, 1)

                def silu(m, t, s):
                    act.wait_ge(g_ps, m + 1)
                    act.activation(g_[t % 2][:, :], gb[:, :], ACT.Silu, scale=sg[s][:, t:t + 1]).then_inc(g_done, 1)

                def step(b, s, first, last):
                    for t in range(TPB):
                        m = b * TPB + t
                        act.wait_ge(h_tp, m + 1)
                        act.activation(hT[t % 2][:, :, :], hb[:, :, :], ACT.Copy).then_inc(h_copied, 1)
                        if t == 2 and not last:
                            copy(b + 1, 1 - s)
                        if t < TPB - 1:
                            silu(m + 1, t + 1, s)
                        elif not last:
                            silu(m + 1, 0, 1 - s)

                copy(0, 0)
                silu(0, 0, 0)
                over_batches(act, step)

            @block.tensor
            def _(pe):
                def turn(b, s):
                    pe.wait_ge(xq_done, b + 1)
                    wait_pos(pe, x_copied, b)
                    for c in range(DC):
                        for t in range(TPB):
                            mm = pe.transpose(xb[:, c, t * P:(t + 1) * P], xq[s][:, t, c * P:(c + 1) * P], ident[:, :])
                    mm.then_inc(x_ps, 1)

                def first_layers(m, t, s):
                    wait_pos(pe, h_done, m)
                    for w, dst in ((wu, ub), (wg, gb)):
                        for j in range(F3 // 512):
                            for c in range(DC):
                                mm = pe.matmul(dst[:, j * 512:(j + 1) * 512], xT[s][:, c, t * P:(t + 1) * P],
                                               w[:, c, j * 512:(j + 1) * 512], start=(c == 0), stop=(c == DC - 1))
                    mm.then_inc(g_ps, 1)

                def step(b, s, first, last):
                    for t in range(TPB):
                        m = b * TPB + t
                        if t == 2 and not last:
                            turn(b + 1, 1 - s)
                        if t < TPB - 1:
                            first_layers(m + 1, t + 1, s)
                        elif not last:
                            pe.wait_ge(x_copied, b + 2)
                            first_layers(m + 1, 0, 1 - s)
                        pe.wait_ge(hq_done, m + 1)
                        for f in range(FC):
                            mm = pe.transpose(hb[:, f, :], hq[t % 2][:, f * P:(f + 1) * P], ident[:, :])
                        mm.then_inc(h_tp, 1)
                        pe.wait_ge(h_copied, m + 1)
                        wait_pos(pe, x_added, m - 1)
                        for f in range(FC):
                            mm = pe.matmul(yb[t % 2][:, 0:D], hT[t % 2][:, f, :], wd[:, f, :],
                                           start=(f == 0), stop=(f == FC - 1))
                        mm.then_inc(y_ps, 1)

                turn(0, 0)
                pe.wait_ge(x_copied, 1)
                first_layers(0, 0, 0)
                over_batches(pe, step)

            @block.sync
            def _(sp):
                def step(b, s, first, last):
                    sp.wait_ge(x_added, b * TPB + TPB)
                    xs = k.x[:, bass.ds(b * (TPB * D), TPB * D)].rearrange("p (t d) -> p t d", t=TPB)
                    sp.dma_start(out[bass.ds(b, 1)].rearrange("b (t p) d -> p (b t) d", p=P), xs).then_inc(stored, 16)
                over_batches(sp, step)
                sp.wait_ge(stored, 16 * NB)


def store_stage(nc, k, out):
    ctx, sb, ps, sem = scoped(k)
    with ctx:
        stored = sem("stored")
        with nc.Block() as block:
            @block.sync
            def _(sp):
                for b in range(NB):
                    sp.dma_start(out[b].rearrange("(t p) d -> p t d", p=P),
                                 k.x[:, b * TPB * D:(b + 1) * TPB * D].rearrange("p (t d) -> p t d", t=TPB)
                                 ).then_inc(stored, 16)
                sp.wait_ge(stored, 16 * NB)


def build(nc, a, out, stages="a0 m0 a1 f1 w2 m2 a3 f3"):
    nothing = lambda sp: None
    with ExitStack() as ctx:
        k = Core(nc, ctx, a)
        load_stage(nc, k)
        todo = stages.split()
        weights = ExitStack()
        room = lambda n, words: weights.enter_context(nc.sbuf_tensor(n, [P, words], F32))

        def run(st, ahead=nothing):
            k.ahead = ahead
            ln_scalars(nc, k, st)
            if st[0] == "a":
                if st in todo:
                    attention(nc, k, int(st[1]))
            elif st[0] == "m":
                mixture(nc, k, int(st[1]))
            elif st == "f1":
                quantum_ffn(nc, k)
            elif st == "w2":
                window_attention(nc, k)
            elif st == "f3":
                ternary_ffn(nc, k, out)

        if "m0" in todo:
            k.w1, k.w2 = room("m0_w1", E * DC * F0), room("m0_w2", E * F0 // P * D)
            k.w_count = 16 * 2 * E

            def m0_weights(sp):
                load_first_layers(sp, k, 0, range(E))
                load_second_layers(sp, k, 0)
            k.late = nothing if "a0" in todo else m0_weights
        if "a0" in todo:
            run("a0", m0_weights if "m0" in todo else nothing)
        if "m0" in todo:
            run("m0")
            weights.close()
        if "m2" in todo:
            before = k.w_count if "m0" in todo else 0
            k.w_count = before + 16 * 2 * E
            k.w2 = room("m2_w2", E * F2 // P * D)
        early = "m2" in todo and "a1" in todo
        if "a1" in todo:
            run("a1", (lambda sp: load_second_layers(sp, k, 2)) if early else nothing)
        if "f1" in todo:
            run("f1")
        if "m2" in todo:
            k.w1 = room("m2_w1", E * DC * F2)

            def m2_late(sp):
                if not early:
                    load_second_layers(sp, k, 2)
                load_first_layers(sp, k, 2, range(0 if "w2" not in todo else E // 2, E))
            k.late = m2_late
        if "w2" in todo:
            run("w2", (lambda sp: load_first_layers(sp, k, 2, range(E // 2))) if "m2" in todo else nothing)
        if "m2" in todo:
            run("m2")
            weights.close()
        for st in ("a3", "f3"):
            if st in todo:
                run(st)
        if "f3" not in todo:
            store_stage(nc, k, out)


def chunked(w):
    return np.ascontiguousarray(np.asarray(w).reshape(-1, P, w.shape[-1]).transpose(1, 0, 2))


def layout(inputs):
    i = {n: np.asarray(v) for n, v in inputs.items()}
    a = {"x": i["x"], "cst": constants(), "tau": i["condB_tau"], "delta": i["fside_BxS2_0"].reshape(-1)}
    a["ctxT"] = np.ascontiguousarray(i["ctx_1024"].reshape(NB, S, DC, P).transpose(0, 3, 2, 1))
    for L in (0, 1, 3):
        for c in "qkvo":
            a[f"L{L}_xcond_W{c}"] = chunked(i[f"L{L}_xcond_W{c}"].T)
        for c in "qk":
            a[f"L{L}_xcond_b{c}"] = np.ascontiguousarray(i[f"L{L}_xcond_b{c}"].reshape(DC, P).T)
        for c in "vo":
            a[f"L{L}_xcond_b{c}"] = i[f"L{L}_xcond_b{c}"]
    a["L0_gate"], a["L2_gate"] = chunked(i["L0_ffn_gate_w"]), chunked(i["L2_ffn_router_w"].T)
    for L, w1, w2 in ((0, i["L0_ffn_w1"], i["L0_ffn_w2"]),
                      (2, i["L2_ffn_w1"].transpose(0, 2, 1), i["L2_ffn_w2"].transpose(0, 2, 1))):
        for n, w in (("w1", w1), ("w2", w2)):
            w = w.reshape(E, -1, P, w.shape[-1]).transpose(2, 0, 1, 3)
            a[f"L{L}_ffn_{n}"] = np.ascontiguousarray(w.reshape(P, E, -1))
        a[f"L{L}_ffn_b2"] = i[f"L{L}_ffn_b2"].reshape(-1)
    for n, v in (("L0_ffn_bt", i["L0_ffn_ln1_b"]), ("L0_ffn_gt", i["L0_ffn_ln1_g"]), ("L2_ffn_bt", i["L2_ffn_b1"])):
        a[n] = np.ascontiguousarray(v.reshape(-1, P).T)
    a["L0_ffn_b1"] = i["L0_ffn_b1"].reshape(-1)
    a["L1_ffn_W1"], a["L1_ffn_W2"] = chunked(i["L1_ffn_W1"]), chunked(i["L1_ffn_W2"])
    a["L1_ffn_par"] = np.ascontiguousarray(np.stack([
        i["L1_ffn_" + n].reshape(-1, P) for n in ("b1", "quantum_phases", "quantum_weights_real",
                                                  "quantum_weights_imag")]).transpose(2, 0, 1))
    a["L1_ffn_b2"] = i["L1_ffn_b2"]
    a["L2_Wa"], a["L2_Wc"] = chunked(i["L2_xcond_W_a"].T), chunked(i["L2_xcond_W_c"].T)
    a["pt"], a["len"] = i["condB_pt"], i["_lenS2"]
    for n in ("gate", "up", "down"):
        a["L3_ffn_w_" + n] = chunked(i["L3_ffn_w_" + n].T).reshape(P, -1)
    a["L0_ffn_ln_g"], a["L0_ffn_ln_b"] = i["L0_ffn_ln_g"], i["L0_ffn_ln_b"]
    return a


def kernel(**inputs):
    import concourse.bacc as bacc
    from concourse.bass_utils import run_bass_kernel_spmd

    nc = bacc.Bacc("TRN2", target_bir_lowering=False, num_devices=1)
    arrays = {f"in_{n}": v for n, v in layout(inputs).items()}
    a = {n[3:]: nc.dram_tensor(n, v.shape, mybir.dt.from_np(v.dtype), kind="ExternalInput").ap()
         for n, v in arrays.items()}
    out = nc.dram_tensor("out_x", (NB, SEQ, D), F32, kind="ExternalOutput").ap()
    build(nc, a, out)
    r = run_bass_kernel_spmd(nc, [arrays], core_ids=[0])
    return r.results[0]["out_x"]
```

```python
from contextlib import ExitStack

import numpy as np

import concourse.bass as bass
from concourse import mybir

F32 = mybir.dt.float32
BF16 = mybir.dt.bfloat16
I32 = mybir.dt.int32
U32 = mybir.dt.uint32
ALU = mybir.AluOpType
ACT = mybir.ActivationFunctionType
AX = mybir.AxisListType

P = 128
NB, SEQ, D = 8, 512, 256
TPB = SEQ // P
NT = NB * TPB
DC = D // P
S = 64
H, DK = 16, 16
HPC = H // DC
VW = DK + 1
E, TOPK = 8, 2
F0, F1, F2, F3 = 512, 1024, 1024, 1024
NTILES = TOPK * NT + E
CAP = (NT + 1) * P
EPS = 1e-5
MAGIC = 1.5 * 2.0 ** 23
TWO_PI = 2.0 * np.pi
WINDOW, DEV_POW = 16.0, 128.0

C_ID, C_TRI, C_ONE = 0, P, 2 * P
C_HM = 3 * P
C_L = C_HM + HPC * S
C_P = C_L + S
C_E = C_P + 1
C_J = C_E + E
C_REGION = C_J + NTILES
C_PART = C_REGION + E
C_N = C_PART + 1


def constants():
    c = np.zeros((P, C_N), np.float32)
    p = np.arange(P)
    c[:, C_ID:C_ID + P] = np.eye(P)
    c[:, C_TRI:C_TRI + P] = p[:, None] < p[None, :]
    c[:, C_ONE:C_ONE + P] = 1.0
    c[:, C_HM:C_HM + HPC * S] = np.repeat(p[:, None] // DK == np.arange(HPC)[None, :], S, axis=1)
    c[:, C_L:C_L + S] = np.arange(S)
    c[:, C_P] = p % S
    c[:, C_E:C_E + E] = E - np.arange(E)
    c[:, C_J:C_J + NTILES] = np.arange(NTILES)
    c[:, C_REGION:C_REGION + E] = CAP * np.arange(E)
    c[:, C_PART] = p
    return c


def wait_pos(eng, sem, value):
    if not (isinstance(value, int) and value <= 0):
        eng.wait_ge(sem, value)


def over_batches(eng, step, count=NB):
    step(0, 0, True, False)
    with eng.Fori(0, (count - 2) // 2) as i:
        step(i * 2 + 1, 1, False, False)
        step(i * 2 + 2, 0, False, False)
    step(count - 1, 1, False, True)


def over_batches_ahead(eng, step):
    step(0, 0, lambda d: True)
    with eng.Fori(0, (NB - 4) // 2) as i:
        step(i * 2 + 1, 1, lambda d: True)
        step(i * 2 + 2, 0, lambda d: True)
    for b in range(NB - 3, NB):
        step(b, b % 2, lambda d, b=b: b + d < NB)


def is_first(b):
    return isinstance(b, int) and b == 0


class Core:

    def __init__(self, nc, ctx, a):
        self.nc, self.a = nc, a
        self.stale = []
        sem = lambda n: ctx.enter_context(nc.semaphore(n))
        self.zeroed, self.padded = sem("zeroed"), sem("padded")
        self.scattered = [sem(f"scattered{s}") for s in range(2)]
        self.g_in = [sem(f"g_in{r}") for r in range(RING)]
        self.mixtures = 0
        self.w_in = sem("w_in")
        self.psum = ctx.enter_context(nc.psum_tensor("psum", [P, 8 * BANK], F32))
        sb = lambda n, s, d=F32: ctx.enter_context(nc.sbuf_tensor(n, s, d))
        self.x = sb("x_res", [P, NT * D])
        self.cst = sb("cst", [P, C_N])
        self.stats = sb("stats", [P, NT, 6])
        self.mean = sb("mean", [P, NT])
        self.rstd = sb("rstd", [P, NT])
        self.half = sb("half", [P, NT])
        self.lnt = sb("lnt", [P, 3, NT])
        self.tau = sb("tau", [P, NB])
        self.delta = sb("delta", [P, NB * S])
        self.xs = nc.dram_tensor("sorted_in", [E * CAP + P, D], F32, kind="Internal").ap()
        self.ys = nc.dram_tensor("sorted_out", [NTILES * P, D], F32, kind="Internal").ap()
        self.att_w = {c: sb("att_w" + c, [P, DC, D]) for c in "qkvo"}
        self.att_b = [sb("att_b" + c, [P, DC if c in "qk" else D]) for c in "qkvo"]
        self.att_in, self.att_loads = sem("att_in"), 0
        self.f1_in, self.win_in, self.f3_in = sem("f1_in"), sem("win_in"), sem("f3_in")
        self.ident = self.cst[:, C_ID:C_ID + P]

    def xt(self, n):
        return self.x[:, bass.ds(n * D, D)]


RING = 4
BANK = 512


def scoped(k):
    nc, taken = k.nc, [0]
    ctx = ExitStack()
    sb = lambda n, s, d=F32: ctx.enter_context(nc.sbuf_tensor(n, s, d))

    def ps(name, shape, dtype=F32):
        size = int(np.prod(shape[1:]))
        words = size // (2 if dtype == BF16 else 1)
        at, taken[0] = taken[0], taken[0] + -(-words // BANK)
        assert taken[0] <= 8, name
        ap = k.psum[:, at * BANK:at * BANK + words]
        if dtype == BF16:
            ap = ap.bitcast(BF16)
        return ap if len(shape) == 2 else ap.rearrange("p (a b) -> p a b", a=shape[1])


    def sem(name):
        handle = ctx.enter_context(nc.semaphore(name))
        k.stale.append(handle)
        return handle

    return ctx, sb, ps, sem


def clear_stale(k, pool, own):
    numbers = sorted({s.num for s in k.stale} - {s.num for s in own})
    k.stale = list(own)
    while numbers:
        n = 1
        while n < len(numbers) and numbers[n] == numbers[0] + n:
            n += 1
        pool.sem_clear(range(numbers[0], numbers[0] + n))
        numbers = numbers[n:]


def load_stage(nc, k):
    ctx, sb, ps, sem = scoped(k)
    a = k.a
    with ctx:
        loaded, x_loaded, half_set = sem("ld_small"), sem("ld_x"), sem("ld_half")
        zero_set = sem("ld_zero_set")
        zero = sb("ld_zero", [P, D])
        with nc.Block() as block:
            @block.sync
            def _(sp):
                for b in range(NB):
                    sp.dma_start(k.x[:, b * TPB * D:(b + 1) * TPB * D].rearrange("p (t d) -> p t d", t=TPB),
                                 a["x"][b].rearrange("(t p) d -> p t d", p=P)).then_inc(x_loaded, 16)

            @block.scalar
            def _(act):
                act.dma_start(k.cst[:, :], a["cst"]).then_inc(loaded, 16)
                act.dma_start(k.tau[:, :], a["tau"].partition_broadcast(P)).then_inc(loaded, 16)
                act.dma_start(k.delta[:, :], a["delta"].partition_broadcast(P)).then_inc(loaded, 16)
                if k.first_att is not None:
                    load_attention(act, k, k.first_att)

            @block.gpsimd
            def _(pool):
                pool.memset(k.half[:, :], -0.5).then_inc(half_set, 1)
                pool.memset(zero[:, :], 0.0).then_inc(zero_set, 1)
                pool.wait_ge(zero_set, 1)
                pool.dma_start(k.xs[E * CAP:E * CAP + P, :], zero[:, :]).then_inc(k.zeroed, 16)
                pool.wait_ge(k.zeroed, 16)

            @block.vector
            def _(dve):
                dve.wait_ge(loaded, 48)
                dve.tensor_scalar(k.tau[:, :], k.tau[:, :], DK ** -0.5, None, ALU.mult)
                dve.tensor_scalar(k.delta[:, :], k.delta[:, :], DK ** -0.5, None, ALU.mult)
                for b in range(NB):
                    if b == 0:
                        dve.wait_ge(x_loaded, 16 * NB)
                    for t in range(TPB):
                        n = b * TPB + t
                        dve.bn_stats(k.stats[:, n, :], k.x[:, n * D:(n + 1) * D])


def ln_scalars(nc, k, name):
    ctx, sb, ps, sem = scoped(k)
    with ctx:
        dv, pw = sem(name + "_lnv"), sem(name + "_lnp")
        me, ve, mo, vo = (k.stats[:, :, j] for j in (1, 2, 4, 5))
        d, m2, v = (k.lnt[:, j, :] for j in range(3))
        with nc.Block() as block:
            @block.vector
            def _(dve):
                dve.tensor_tensor(d, me, mo, ALU.subtract).then_inc(dv, 1)
                dve.tensor_tensor(m2, ve, vo, ALU.add).then_inc(dv, 1)
                dve.tensor_tensor(k.mean[:, :], me, mo, ALU.add).then_inc(dv, 1)
                dve.wait_ge(dv, 3)
                dve.scalar_tensor_tensor(v, d, 0.25, d, ALU.mult, ALU.mult).then_inc(dv, 1)
                dve.tensor_scalar(k.mean[:, :], k.mean[:, :], 0.5, None, ALU.mult)
                dve.tensor_scalar(m2, m2, 1.0 / D, EPS, ALU.mult, ALU.add).then_inc(dv, 1)
                dve.wait_ge(dv, 5)
                dve.tensor_tensor(v, v, m2, ALU.add).then_inc(pw, 1)

            @block.gpsimd
            def _(pool):
                clear_stale(k, pool, (dv, pw))
                pool.wait_ge(pw, 1)
                pool.tensor_tensor(k.rstd[:, :], v, k.half[:, :], ALU.pow)



ATT_LOADS = 8


def load_attention(eng, k, L):
    for c in "qkvo":
        eng.dma_start(k.att_w[c][:, :, :], k.a[f"L{L}_xcond_W{c}"]).then_inc(k.att_in, 16)
    for c, t in zip("qkvo", k.att_b):
        src = k.a[f"L{L}_xcond_b{c}"]
        eng.dma_start(t[:, :], src if c in "qk" else src.partition_broadcast(P)).then_inc(k.att_in, 16)


def attention(nc, k, L):
    ctx, sb, ps, sem = scoped(k)
    a = k.a
    nm = f"a{L}_"
    W = HPC * S
    with ctx:
        w, (bq, bk, bv, bo) = k.att_w, k.att_b
        bqt = sb(nm + "bqt", [P, DC, NB])
        cx = [sb(f"{nm}cx{s}", [P, DC, 2, S]) for s in range(2)]
        z = [sb(f"{nm}z{s}", [P, TPB, D]) for s in range(2)]
        zT = sb(nm + "zT", [P, DC, SEQ])
        qT = [sb(f"{nm}qT{s}", [P, DC, SEQ]) for s in range(2)]
        kb = [sb(f"{nm}kb{s}", [P, H * S]) for s in range(2)]
        va = [sb(f"{nm}va{s}", [P, H // 2, 2, VW]) for s in range(2)]
        pr = [sb(f"{nm}pr{s}", [P, H * S]) for s in range(2)]
        pT = [sb(f"{nm}pT{s}", [P, H // 2, P]) for s in range(2)]
        mx = [sb(f"{nm}mx{s}", [P, HPC]) for s in range(2)]
        rec = [sb(f"{nm}rec{s}", [P, H]) for s in range(2)]
        on = [sb(f"{nm}on{s}", [P, D]) for s in range(2)]
        oT = [sb(f"{nm}oT{s}", [P, DC, P]) for s in range(2)]
        sc_b = [ps(f"{nm}sc{c}", [P, W]) for c in range(2)]
        tr_b = [ps(f"{nm}tr{c}", [P, HPC // 2, P]) for c in range(2)]
        val_b = ps(nm + "val", [P, 512])
        out_b = ps(nm + "out", [P, 512])
        pr0, pr1 = ps(nm + "pr0", [P, 512]), ps(nm + "pr1", [P, 512])

        k.att_loads += ATT_LOADS
        cx_in = [sem(f"{nm}cx_in{s}") for s in range(2)]
        va_zero, va_init, bq_done = sem(nm + "va_zero"), sem(nm + "va_init"), sem(nm + "bq_done")
        z_done, xb_done = sem(nm + "z_done"), sem(nm + "xb_done")
        prep_ps, pr0_read, pr1_read, k_done, v_done = (
            sem(nm + c) for c in ("prep_ps", "pr0_read", "pr1_read", "k_done", "v_done"))
        s_ps, s_read, s_max, s_sub, exp_done = (
            sem(nm + c) for c in ("s_ps", "s_read", "s_max", "s_sub", "exp_done"))
        t_ps, t_evac, o_ps, o_rec, o_norm = (sem(nm + c) for c in ("t_ps", "t_evac", "o_ps", "o_rec", "o_norm"))
        oT_ps, oT_copied, y_ps, x_added = (sem(nm + c) for c in ("oT_ps", "oT_copied", "y_ps", "x_added"))

        FILLS = 6

        with nc.Block() as block:
            @block.sync
            def _(sp):
                def step(b, s, first, last):
                    wait_pos(sp, prep_ps, FILLS * (b - 1))
                    for j in range(2):
                        sp.dma_start(cx[s][:, :, j, :],
                                     a["ctxT"][bass.ds(b, 1)].rearrange("b p c l -> p (b c) l")).then_inc(cx_in[s], 16)
                over_batches(sp, step)

            @block.gpsimd
            def _(pool):
                for s in range(2):
                    pool.memset(va[s][:, :, :, :], 0.0).then_inc(va_zero, 1)
                pool.wait_ge(va_zero, 2)
                for s in range(2):
                    pool.memset(va[s][0:S, :, 0, DK:VW], 1.0).then_inc(va_init, 1)
                    pool.memset(va[s][S:P, :, 1, DK:VW], 1.0).then_inc(va_init, 1)
                pool.wait_ge(k.att_in, 16 * k.att_loads)

                def step(b, s, first, last):
                    pool.wait_ge(z_done, b + 1)
                    xs = k.x[:, bass.ds(b * (TPB * D), TPB * D)].rearrange("p (t d) -> p t d", t=TPB)
                    pool.tensor_tensor(xs, xs, bo[:, None, :].to_broadcast([P, TPB, D]), ALU.add).then_inc(xb_done, 1)
                over_batches(pool, step)

            @block.tensor
            def _(pe):
                def piece(b, s, t):
                    if t == 0:
                        pe.wait_ge(z_done, b + 1)
                        for c, (bank, done) in enumerate(((pr0, k_done), (pr1, v_done))):
                            wait_pos(pe, done, b)
                            for i in range(TPB):
                                mm = pe.transpose(bank[:, i * P:(i + 1) * P], z[s][:, i, c * P:(c + 1) * P], k.ident)
                            mm.then_inc(prep_ps, 1)
                    elif t == 1:
                        pe.wait_ge(pr0_read, 2 * b + 1)
                        pe.wait_ge(pr1_read, 2 * b + 1)
                        for c, bank in enumerate((pr0, pr1)):
                            for kk in range(DC):
                                mm = pe.matmul(bank[:, :], w["q"][:, kk, c * P:(c + 1) * P], zT[:, kk, :],
                                               start=(kk == 0), stop=(kk == DC - 1))
                            mm.then_inc(prep_ps, 1)
                    else:
                        pe.wait_ge(cx_in[s], 16 * b + (16 if s else 32))
                        pe.wait_ge(pr0_read, 2 * b + 2)
                        for c in range(DC):
                            for kk in range(DC):
                                mm = pe.matmul(pr0[:, c * S:(c + 1) * S], w["k"][:, kk, c * P:(c + 1) * P],
                                               cx[s][:, kk, 0, :], start=(kk == 0), stop=(kk == DC - 1))
                        mm.then_inc(prep_ps, 1)
                        pe.wait_ge(pr1_read, 2 * b + 2)
                        for kk in range(DC):
                            mm = pe.matmul(pr1[:, 0:D], cx[s][:, kk, :, :].rearrange("p j l -> p (j l)"),
                                           w["v"][:, kk, :], start=(kk == 0), stop=(kk == DC - 1))
                        mm.then_inc(prep_ps, 1)

                def scores(n, s, t, c):
                    wait_pos(pe, s_read, 2 * n + c - 1)
                    pe.matmul(sc_b[c][:, :], qT[s][:, c, t * P:(t + 1) * P], kb[s][:, c * W:(c + 1) * W],
                              start=True, stop=True).then_inc(s_ps, 1)

                def project_turn(n, t):
                    pe.wait_ge(o_norm, n + 1)
                    wait_pos(pe, x_added, n)
                    for c in range(DC):
                        mm = pe.transpose(out_b[:, c * P:(c + 1) * P], on[t % 2][:, c * P:(c + 1) * P], k.ident)
                    mm.then_inc(oT_ps, 1)

                def project(n, t):
                    pe.wait_ge(oT_copied, n + 1)
                    for c in range(DC):
                        mm = pe.matmul(out_b[:, D:2 * D], oT[t % 2][:, c, :], w["o"][:, c, :],
                                       start=(c == 0), stop=(c == DC - 1))
                    mm.then_inc(y_ps, 1)

                def step(b, s, first, last):
                    for t in range(TPB):
                        n = b * TPB + t
                        ends, begins = last and t == TPB - 1, first and t == 0
                        nxt = (n + 1, s, t + 1) if t < TPB - 1 else (n + 1, 1 - s, 0)
                        if t < TPB - 1:
                            scores(*nxt, 0)
                        if not begins:
                            project_turn(n - 1, t - 1)
                        for c in range(2):
                            pe.wait_ge(exp_done, 2 * n + c + 1)
                            wait_pos(pe, t_evac, 2 * n + c - 1)
                            for i in range(HPC // 2):
                                at = (c * HPC // 2 + i) * P
                                mm = pe.transpose(tr_b[c][:, i, :], pr[t % 2][:, at:at + P], k.ident)
                            mm.then_inc(t_ps, 1)
                        if t == TPB - 1 and not last:
                            pe.wait_ge(pr1_read, 2 * b + 4)
                            pe.wait_ge(k_done, b + 2)
                            scores(*nxt, 0)
                        if not ends:
                            scores(*nxt, 1)
                        if not begins:
                            project(n - 1, t - 1)
                        pe.wait_ge(t_evac, 2 * n + 2)
                        wait_pos(pe, o_norm, n)
                        if t == 0:
                            pe.wait_ge(v_done, b + 1)
                        for c in range(H // 2):
                            mm = pe.matmul(val_b[:, c * 2 * VW:(c + 1) * 2 * VW], pT[t % 2][:, c, :],
                                           va[s][:, c, :, :].rearrange("p j v -> p (j v)"), start=True, stop=True)
                        mm.then_inc(o_ps, 1)
                        if t < 3 and not last:
                            piece(b + 1, 1 - s, t)

                pe.wait_ge(k.att_in, 16 * k.att_loads)
                for t in range(3):
                    piece(0, 0, t)
                pe.wait_ge(k_done, 1)
                for c in range(2):
                    scores(0, 0, 0, c)
                over_batches(pe, step)
                project_turn(NT - 1, TPB - 1)
                project(NT - 1, TPB - 1)

            @block.scalar
            def _(act):
                def drain(b, s, t):
                    for c, (bank, read) in enumerate(((pr0, pr0_read), (pr1, pr1_read))):
                        act.wait_ge(prep_ps, FILLS * b + 2 * t + c + 1)
                        if t == 0:
                            act.activation(zT[:, c, :], bank[:, :], ACT.Copy).then_inc(read, 1)
                        else:
                            act.activation(qT[s][:, c, :], bank[:, :], ACT.Identity, bias=bqt[:, c, bass.ds(b, 1)],
                                           scale=k.tau[:, bass.ds(b, 1)]).then_inc(read, 1)

                def exponentials(n, t, c):
                    act.wait_ge(s_sub, 2 * n + c + 1)
                    half = pr[t % 2][:, c * W:(c + 1) * W]
                    act.activation(half, half, ACT.Exp).then_inc(exp_done, 1)

                def project_copy(n, t):
                    act.wait_ge(oT_ps, n + 1)
                    act.activation(oT[t % 2][:, :, :], out_b[:, 0:D].rearrange("p (c q) -> p c q", c=DC),
                                   ACT.Copy).then_inc(oT_copied, 1)

                def step(b, s, first, last):
                    for t in range(TPB):
                        n = b * TPB + t
                        if not (first and t == 0):
                            project_copy(n - 1, t - 1)
                        for c in range(2):
                            act.wait_ge(t_ps, 2 * n + c + 1)
                            act.activation(pT[t % 2][:, c * HPC // 2:(c + 1) * HPC // 2, :], tr_b[c][:, :, :],
                                           ACT.Copy).then_inc(t_evac, 1)
                        if not (last and t == TPB - 1):
                            for c in range(2):
                                exponentials(n + 1, t + 1, c)
                        if t < 2 and not last:
                            drain(b + 1, 1 - s, t)

                drain(0, 0, 0)
                k.ahead(act)
                act.wait_ge(bq_done, 1)
                drain(0, 0, 1)
                for c in range(2):
                    exponentials(0, 0, c)
                over_batches(act, step)
                project_copy(NT - 1, TPB - 1)

            @block.vector
            def _(dve):
                def normalise(b, s):
                    wait_pos(dve, prep_ps, FILLS * (b - 1))
                    for t in range(TPB):
                        n = b * TPB + t
                        v = dve.tensor_scalar(z[s][:, t, :], k.xt(n), k.mean[:, bass.ds(n, 1)],
                                              k.rstd[:, bass.ds(n, 1)], ALU.subtract, ALU.mult)
                    v.then_inc(z_done, 1)

                def drain(b, s):
                    dve.wait_ge(prep_ps, FILLS * b + 5)
                    for c in range(DC):
                        v = dve.scalar_tensor_tensor(
                            kb[s][:, c * W:(c + 1) * W].rearrange("p (h l) -> p h l", h=HPC),
                            pr0[:, None, c * S:(c + 1) * S].to_broadcast([P, HPC, S]), bk[:, c:c + 1],
                            k.cst[:, C_HM:C_HM + W].rearrange("p (h l) -> p h l", h=HPC), ALU.add, ALU.mult)
                    v.then_inc(k_done, 1)
                    dve.wait_ge(prep_ps, FILLS * b + 6)
                    for j in range(2):
                        h = slice(j * S, (j + 1) * S)
                        v = dve.tensor_tensor(
                            va[s][h, :, j, 0:DK],
                            pr1[h, 0:D].rearrange("p (c j e) -> p c j e", c=H // 2, j=2)[:, :, j, :],
                            bv[h, :].rearrange("p (c j e) -> p c j e", c=H // 2, j=2)[:, :, j, :], ALU.add)
                    v.then_inc(v_done, 1)

                def softmax(n, b, t, c):
                    p3 = pr[t % 2][:, c * W:(c + 1) * W].rearrange("p (h l) -> p h l", h=HPC)
                    dve.wait_ge(s_ps, 2 * n + c + 1)
                    dve.tensor_tensor(p3, sc_b[c][:, :].rearrange("p (h l) -> p h l", h=HPC),
                                      k.delta[:, None, bass.ds(b * S, S)].to_broadcast([P, HPC, S]),
                                      ALU.add).then_inc(s_read, 1)
                    dve.wait_ge(s_read, 2 * n + c + 1)
                    dve.tensor_reduce(mx[c][:, :], p3, AX.X, ALU.max).then_inc(s_max, 1)
                    dve.wait_ge(s_max, 2 * n + c + 1)
                    dve.tensor_tensor(p3, p3, mx[c][:, :, None].to_broadcast([P, HPC, S]),
                                      ALU.subtract).then_inc(s_sub, 1)

                def divide(n, t):
                    o3 = val_b[:, 0:H * VW].rearrange("p (h v) -> p h v", h=H)
                    dve.wait_ge(o_ps, n + 1)
                    dve.reciprocal(rec[t % 2][:, :], o3[:, :, DK]).then_inc(o_rec, 1)
                    dve.wait_ge(o_rec, n + 1)
                    dve.tensor_tensor(on[t % 2][:, :].rearrange("p (h e) -> p h e", h=H), o3[:, :, 0:DK],
                                      rec[t % 2][:, :, None].to_broadcast([P, H, DK]), ALU.mult).then_inc(o_norm, 1)

                def residual(n):
                    dve.wait_ge(y_ps, n + 1)
                    dve.tensor_tensor(k.xt(n), out_b[:, D:2 * D], k.xt(n), ALU.add).then_inc(x_added, 1)

                def statistics(n):
                    dve.wait_ge(x_added, n + 1)
                    dve.bn_stats(k.stats[:, bass.ds(n, 1), :], k.xt(n))

                def step(b, s, first, last):
                    for t in range(TPB):
                        n = b * TPB + t
                        ends, begins = last and t == TPB - 1, first and t == 0
                        nxt = (n + 1, b, t + 1) if t < TPB - 1 else (n + 1, b + 1, 0)
                        if not ends:
                            softmax(*nxt, 0)
                        if t == 0 and not last:
                            normalise(b + 1, 1 - s)
                        if not ends:
                            softmax(*nxt, 1)
                        if not begins:
                            if t == 1:
                                dve.wait_ge(xb_done, b + 1)
                            residual(n - 1)
                        divide(n, t)
                        if not begins:
                            statistics(n - 1)
                        if t == 2 and not last:
                            drain(b + 1, 1 - s)

                dve.wait_ge(k.att_in, 16 * k.att_loads)
                for c in range(DC):
                    v = dve.tensor_scalar(bqt[:, c, :], k.tau[:, :], bq[:, c:c + 1], None, ALU.mult)
                v.then_inc(bq_done, 1)
                dve.wait_ge(va_init, 4)
                normalise(0, 0)
                drain(0, 0)
                for c in range(2):
                    softmax(0, 0, 0, c)
                over_batches(dve, step)
                residual(NT - 1)
                statistics(NT - 1)


def dispatch(nc, k, L):
    ctx, sb, ps, sem = scoped(k)
    nm = f"r{L}_"
    with ctx:
        gate = sb(nm + "gate", [P, DC, E])
        z = [sb(f"{nm}z{s}", [P, TPB * D]) for s in range(2)]
        if L:
            zk = [sb(f"{nm}zk{s}", [P, TPB * D]) for s in range(2)]
        else:
            zk = [k.z[:, b * (TPB * D):(b + 1) * (TPB * D)] for b in range(NB)]
        zT = sb(nm + "zT", [P, DC, SEQ])
        t3 = lambda n: sb(nm + n, [P, TPB, E])
        t2 = lambda n: sb(nm + n, [P, TPB])
        lgt, eq, cand, rest, place, prod = (t3(n) for n in ("lgt", "eq", "cand", "rest", "place", "prod"))
        hot = [sb(f"{nm}hot{j}", [P, NT, E]) for j in range(TOPK)]
        pf = [sb(f"{nm}pf{j}", [P, NT]) for j in range(TOPK)]
        sent_to = [sb(f"{nm}to{j}", [P, NT], U32) for j in range(TOPK)]
        shift, moved = sb(nm + "shift", [P, E]), sb(nm + "moved", [P, NT, E])
        chosen, before = ([t3(f"{n}{s}") for s in range(2)] for n in ("chosen", "before"))
        code = t2("code")
        top = [sb(f"{nm}top{j}", [P, NT]) for j in range(TOPK)]
        gap, den = sb(nm + "gap", [P, NT]), sb(nm + "den", [P, NT])
        pad, zero = sb(nm + "pad", [P, E], U32), sb(nm + "zero", [P, D])
        cnt = [sb(f"{nm}cnt{j}", [P, E]) for j in range(4)]
        base = sb(nm + "base", [1, E])
        tile2 = sb(nm + "tiles", [1, NTILES])
        bank = [ps(f"{nm}b{s}", [P, DC, SEQ]) for s in range(2)]
        lg = [ps(f"{nm}lg{s}", [P, 512]) for s in range(2)]
        pp = [ps(f"{nm}pp{s}", [P, 512]) for s in range(2)]
        (w_in, z_done, zT_ps, zT_copied, lg_ps, lg_read, v, chosen_done, place_ps, pos_done, gap_done, gap_exp,
         cnt_ps, pad_done, zero_set, z_kept) = (
            sem(nm + c) for c in ("w_in", "z_done", "zT_ps", "zT_copied", "lg_ps", "lg_read", "v", "chosen",
                                  "place_ps", "pos", "gap", "gap_exp", "cnt_ps", "pad", "zero_set", "z_kept"))
        sent = 16 * NT * k.mixtures
        padded = 16 * E * k.mixtures
        bc = lambda t: t.to_broadcast([P, TPB, E])
        code_e = bc(k.cst[:, None, C_E:C_E + E])
        region = bc(k.cst[:, None, C_REGION:C_REGION + E])
        with nc.Block() as block:
            @block.sync
            def _(sp):
                sp.dma_start(gate[:, :, :], k.a[f"L{L}_gate"]).then_inc(w_in, 16)
                k.late(sp)

            @block.tensor
            def _(pe):
                def turn(b, s):
                    pe.wait_ge(z_done, b + 1)
                    wait_pos(pe, zT_copied, b - 1)
                    for c in range(DC):
                        for t in range(TPB):
                            at = z[s][:, t * D + c * P:t * D + (c + 1) * P]
                            mm = pe.transpose(bank[s][:, c, t * P:(t + 1) * P], at, k.ident)
                    mm.then_inc(zT_ps, 1)

                def logits(b, s):
                    pe.wait_ge(zT_copied, b + 1)
                    wait_pos(pe, lg_read, b - 1)
                    for t in range(TPB):
                        for c in range(DC):
                            mm = pe.matmul(lg[s][:, t * E:(t + 1) * E], zT[:, c, t * P:(t + 1) * P],
                                           gate[:, c, :], start=(c == 0), stop=(c == DC - 1))
                    mm.then_inc(lg_ps, 1)

                def step(b, s, after):
                    pe.wait_ge(chosen_done, b + 1)
                    flat = lambda t: t[:, :, :].rearrange("p t e -> p (t e)")
                    pe.matmul(pp[s][:, 0:TPB * E], k.cst[:, C_TRI:C_TRI + P], flat(chosen[s]), start=True, stop=False)
                    pe.matmul(pp[s][:, 0:TPB * E], k.cst[:, C_ONE:C_ONE + P], flat(before[s]),
                              start=False, stop=True).then_inc(place_ps, 1)
                    if after(2):
                        turn(b + 2, s)
                        logits(b + 2, s)

                pe.wait_ge(w_in, 16)
                for b in range(2):
                    turn(b, b)
                    logits(b, b)
                over_batches_ahead(pe, step)
                pe.wait_ge(v, ROUTE_STEPS * NB + 1)
                pe.matmul(pp[0][:, 0:E], k.cst[:, C_ONE:C_ONE + P], cnt[3][:, :],
                          start=True, stop=True).then_inc(cnt_ps, 1)

            @block.scalar
            def _(act):
                def step(b, s, first, last):
                    act.wait_ge(zT_ps, b + 1)
                    wait_pos(act, lg_ps, b)
                    act.activation(zT[:, :, :], bank[s][:, :, :], ACT.Copy).then_inc(zT_copied, 1)
                    if L and (not isinstance(b, int) or b >= 2):
                        act.wait_ge(k.scattered[s], b * (8 * SCATTERS) + (sent - 8 * SCATTERS * s))
                    kept = zk[s][:, :] if L else k.z[:, bass.ds(b * (TPB * D), TPB * D)]
                    act.activation(kept, z[s][:, :], ACT.Copy).then_inc(z_kept, 1)
                over_batches(act, step)
                act.wait_ge(gap_done, 1)
                act.activation(k.wt[1][:, :], gap[:, :], ACT.Exp).then_inc(gap_exp, 1)

            @block.vector
            def _(dve):
                def normalise(b, s):
                    wait_pos(dve, z_kept, b - 1)
                    wait_pos(dve, zT_ps, b - 1)
                    for t in range(TPB):
                        n = b * TPB + t
                        o = dve.tensor_scalar(z[s][:, t * D:(t + 1) * D], k.xt(n), k.mean[:, bass.ds(n, 1)],
                                              k.rstd[:, bass.ds(n, 1)], ALU.subtract, ALU.mult)
                    o.then_inc(z_done, 1)

                def then(n, op):
                    op.then_inc(v, 1)
                    dve.wait_ge(v, n + 1)
                    return n + 1

                def route(b, s, first):
                    n = b * ROUTE_STEPS
                    tiles = bass.ds(b * TPB, TPB)
                    dve.wait_ge(lg_ps, b + 1)
                    dve.tensor_copy(lgt[:, :, :], lg[s][:, 0:TPB * E].rearrange("p (t e) -> p t e", t=TPB)
                                    ).then_inc(lg_read, 1)
                    dve.wait_ge(lg_read, b + 1)
                    src = lgt
                    for j in range(TOPK):
                        largest = top[j][:, tiles]
                        n = then(n, dve.tensor_reduce(largest, src[:, :, :], AX.X, ALU.max))
                        n = then(n, dve.tensor_tensor(eq[:, :, :], src[:, :, :], bc(largest[:, :, None]), ALU.is_equal))
                        n = then(n, dve.tensor_tensor(cand[:, :, :], eq[:, :, :], code_e, ALU.mult))
                        n = then(n, dve.tensor_reduce(code[:, :], cand[:, :, :], AX.X, ALU.max))
                        n = then(n, dve.tensor_tensor(hot[j][:, tiles, :], cand[:, :, :], bc(code[:, :, None]), ALU.is_equal))
                        if j == 0:
                            n = then(n, dve.scalar_tensor_tensor(rest[:, :, :], hot[0][:, tiles, :], -3e38, src[:, :, :],
                                                                 ALU.mult, ALU.add))
                            src = rest
                    n = then(n, dve.tensor_tensor(chosen[s][:, :, :], hot[0][:, tiles, :], hot[1][:, tiles, :], ALU.add))
                    if first:
                        n = then(n, dve.tensor_scalar(before[s][:, 0, :], chosen[s][:, 0, :], 0.0, None, ALU.mult))
                    else:
                        n = then(n, dve.tensor_tensor(before[s][:, 0, :], before[1 - s][:, TPB - 1, :],
                                                      chosen[1 - s][:, TPB - 1, :], ALU.add))
                    for t in range(1, TPB):
                        o = dve.tensor_tensor(before[s][:, t, :], before[s][:, t - 1, :], chosen[s][:, t - 1, :], ALU.add)
                        if t < TPB - 1:
                            n = then(n, o)
                    o.then_inc(chosen_done, 1)
                    dve.wait_ge(place_ps, b + 1)
                    n = then(n, dve.tensor_tensor(place[:, :, :], pp[s][:, 0:TPB * E].rearrange("p (t e) -> p t e", t=TPB),
                                                  region, ALU.add))
                    for j in range(TOPK):
                        n = then(n, dve.tensor_tensor(prod[:, :, :], place[:, :, :], hot[j][:, tiles, :], ALU.mult))
                        n = then(n, dve.tensor_reduce(pf[j][:, tiles], prod[:, :, :], AX.X, ALU.add))
                        o = dve.tensor_copy(sent_to[j][:, tiles], pf[j][:, tiles])
                        if j == 0:
                            n = then(n, o)
                    o.then_inc(pos_done, 1)
                    dve.wait_ge(pos_done, b + 1)
                    if isinstance(b, int):
                        assert n == (b + 1) * ROUTE_STEPS, n

                normalise(0, 0)
                normalise(1, 1)

                def ahead_step(b, s, after):
                    route(b, s, is_first(b))
                    if after(2):
                        normalise(b + 2, s)
                over_batches_ahead(dve, ahead_step)

                n = NB * ROUTE_STEPS
                last = (NB - 1) % 2
                n = then(n, dve.tensor_tensor(cnt[3][:, :], before[last][:, TPB - 1, :], chosen[last][:, TPB - 1, :], ALU.add))
                dve.tensor_tensor(gap[:, :], top[1][:, :], top[0][:, :], ALU.subtract).then_inc(gap_done, 1)
                dve.wait_ge(cnt_ps, 1)
                total = cnt[3]
                n = then(n, dve.tensor_copy(total[:, :], pp[0][:, 0:E]))
                n = then(n, dve.tensor_tensor(cnt[0][:, :], total[:, :], k.cst[:, C_REGION:C_REGION + E], ALU.add))
                dve.tensor_scalar(pad[:, :], cnt[0][:, :], k.cst[:, C_PART:C_PART + 1], None, ALU.add).then_inc(pad_done, 1)
                dve.wait_ge(pad_done, 1)
                n = then(n, dve.tensor_scalar(total[:, :], total[:, :], P - 1.0, 1.0 / P, ALU.add, ALU.mult))
                n = then(n, dve.tensor_scalar(total[:, :], total[:, :], -(0.5 - 0.5 / P), MAGIC, ALU.add, ALU.add))
                n = then(n, dve.tensor_scalar(total[:, :], total[:, :], MAGIC, None, ALU.subtract))
                n = then(n, dve.tensor_copy(cnt[1][:, :], total[:, :]))
                c = 1
                for sh in (1, 2, 4):
                    a, b = cnt[c], cnt[3 - c]
                    dve.tensor_copy(b[:, 0:sh], a[:, 0:sh])
                    n = then(n, dve.tensor_tensor(b[:, sh:E], a[:, sh:E], a[:, 0:E - sh], ALU.add))
                    c = 3 - c
                end, start = cnt[c], cnt[3 - c]
                n = then(n, dve.tensor_tensor(start[:, :], end[:, :], total[:, :], ALU.subtract))
                wide = lambda t: t.to_broadcast([1, NTILES, E])
                j_col = wide(k.cst[0:1, C_J:C_J + NTILES, None])
                member, ended = (t[0:1, 0:NTILES * E].rearrange("p (j e) -> p j e", j=NTILES) for t in z)
                dve.wait_ge(zT_ps, NB)
                dve.wait_ge(z_kept, NB)
                n = then(n, dve.tensor_tensor(member[:, :, :], j_col, wide(start[0:1, None, :]), ALU.is_ge))
                n = then(n, dve.tensor_tensor(ended[:, :, :], j_col, wide(end[0:1, None, :]), ALU.is_ge))
                n = then(n, dve.tensor_tensor(member[:, :, :], member[:, :, :], ended[:, :, :], ALU.subtract))
                n = then(n, dve.tensor_reduce(tile2[:, :], ended[:, :, :], AX.X, ALU.add))
                n = then(n, dve.tensor_scalar(k.owner[:, :], tile2[:, :], E - 1.0, None, ALU.min))
                n = then(n, dve.scalar_tensor_tensor(base[:, :], start[0:1, :], -float(P),
                                                     k.cst[0:1, C_REGION:C_REGION + E], ALU.mult, ALU.add))
                n = then(n, dve.tensor_scalar(base[:, :], base[:, :], float(E * CAP), None, ALU.subtract))
                n = then(n, dve.scalar_tensor_tensor(ended[:, :, :], j_col, float(P), wide(base[0:1, None, :]),
                                                     ALU.mult, ALU.add))
                n = then(n, dve.tensor_tensor(ended[:, :, :], ended[:, :, :], member[:, :, :], ALU.mult))
                n = then(n, dve.tensor_reduce(tile2[:, :], ended[:, :, :], AX.X, ALU.add))
                n = then(n, dve.tensor_scalar(k.rows[:, :], tile2[:, :], float(E * CAP), None, ALU.add))
                dve.wait_ge(gap_exp, 1)
                n = then(n, dve.scalar_tensor_tensor(shift[:, :], start[:, :], float(P),
                                                     k.cst[:, C_REGION:C_REGION + E], ALU.mult, ALU.subtract))
                for j in range(TOPK):
                    n = then(n, dve.tensor_tensor(moved[:, :, :], hot[j][:, :, :],
                                                  shift[:, None, :].to_broadcast([P, NT, E]), ALU.mult))
                    n = then(n, dve.tensor_reduce(gap[:, :], moved[:, :, :], AX.X, ALU.add))
                    n = then(n, dve.tensor_tensor(k.pos[j][:, :], pf[j][:, :], gap[:, :], ALU.add))
                n = then(n, dve.tensor_scalar(den[:, :], k.wt[1][:, :], 1.0, None, ALU.add))
                n = then(n, dve.reciprocal(k.wt[0][:, :], den[:, :]))
                n = then(n, dve.tensor_tensor(k.wt[1][:, :], k.wt[1][:, :], k.wt[0][:, :], ALU.mult))

            @block.gpsimd
            def _(pool):
                pool.memset(zero[:, :], 0.0).then_inc(zero_set, 1)
                for b in range(NB):
                    pool.wait_ge(pos_done, b + 1)
                    pool.wait_ge(z_kept, b + 1)
                    for t in range(TPB):
                        n = b * TPB + t
                        for j in range(TOPK):
                            pool.indirect_dma_start(
                                out=k.xs[:, :], out_offset=bass.IndirectOffsetOnAxis(ap=sent_to[j][:, n:n + 1], axis=0),
                                in_=zk[b % len(zk)][:, t * D:(t + 1) * D], in_offset=None).then_inc(k.scattered[b % 2], 16)
                pool.wait_ge(zero_set, 1)
                pool.wait_ge(pad_done, 1)
                for e in range(E):
                    pool.indirect_dma_start(
                        out=k.xs[:, :], out_offset=bass.IndirectOffsetOnAxis(ap=pad[:, e:e + 1], axis=0),
                        in_=zero[:, :], in_offset=None).then_inc(k.padded, 16)
                for s in range(2):
                    pool.wait_ge(k.scattered[s], sent + 16 * NT)
                pool.wait_ge(k.padded, padded + 16 * E)


ROUTE_STEPS = 21
SCATTERS = TOPK * TPB


def over_tiles(eng, step, ahead):
    loop = (NTILES - ahead) // 2
    step(0, 0, True, lambda d: True)
    step(1, 1, True, lambda d: True)
    with eng.Fori(1, loop) as i:
        step(i * 2, 0, False, lambda d: True)
        step(i * 2 + 1, 1, False, lambda d: True)
    for j in range(2 * loop, NTILES):
        step(j, j % 2, False, lambda d, j=j: j + d < NTILES)


def load_second_layers(sp, k, L):
    n2 = (F0 if L == 0 else F2) // P * D
    for e in range(E):
        sp.dma_start(k.w2[:, e * n2:(e + 1) * n2], k.a[f"L{L}_ffn_w2"][:, e, :]).then_inc(k.w_in, 16)


def load_first_layers(sp, k, L, es):
    n1 = DC * (F0 if L == 0 else F2)
    for e in es:
        sp.dma_start(k.w1[:, e * n1:(e + 1) * n1], k.a[f"L{L}_ffn_w1"][:, e, :]).then_inc(k.w_in, 16)


def experts(nc, k, L):
    ctx, sb, ps, sem = scoped(k)
    a = k.a
    nm = f"e{L}_"
    F = F0 if L == 0 else F2
    FC = F // P
    norm = L == 0
    A = 2 if norm else 1
    with ctx:
        w1, w2 = k.w1, k.w2
        b2 = sb(nm + "b2", [P, E * D])
        bt = sb(nm + "bt", [P, E * FC])
        if norm:
            b1 = sb(nm + "b1", [P, E * F])
            gt = sb(nm + "gt", [P, E * FC])
            st = [sb(f"{nm}st{s}", [P, 6]) for s in range(2)]
            mv = [sb(f"{nm}mv{s}", [P, 2]) for s in range(2)]
            ve = [sb(f"{nm}ve{s}", [P, 1]) for s in range(2)]
            rs = [sb(f"{nm}rs{s}", [P, 1]) for s in range(2)]
        xin = [sb(f"{nm}x{s}", [P, D]) for s in range(2)]
        xT = [sb(f"{nm}xT{s}", [P, DC, P]) for s in range(2)]
        h = [sb(f"{nm}h{s}", [P, F]) for s in range(A)]
        h = [h[0], h[A - 1]]
        hT = [sb(f"{nm}hT{s}", [P, FC, P]) for s in range(2)]
        y = [sb(f"{nm}y{s}", [P, D]) for s in range(2)]
        xT_b = ps(nm + "pxT", [P, 512])
        h_b = [ps(f"{nm}ph{s}", [P, F]) for s in range(2)]
        hT_b = ps(nm + "phT", [P, FC, P])
        y_b = ps(nm + "py", [P, 512])
        c_in = sem(nm + "c_in")
        x_in = [sem(f"{nm}x_in{s}") for s in range(2)]
        y_out = [sem(f"{nm}y_out{s}") for s in range(2)]
        xT_ps, xT_copied, h_ps, h_read, h_ready, hT_ps, gelu_done, y_ps, y_done = (
            sem(nm + c) for c in ("xT_ps", "xT_copied", "h_ps", "h_read", "h_ready", "hT_ps", "gelu_done",
                                  "y_ps", "y_done"))
        aggr, var, rsq = (sem(nm + c) for c in ("aggr", "var", "rsq"))
        if not norm:
            h_read = h_ready
        with nc.Block() as block:
            @block.sync
            def _(sp):
                sp.dma_start(b2[:, :], a[f"L{L}_ffn_b2"].partition_broadcast(P)).then_inc(c_in, 16)
                sp.dma_start(bt[:, :], a[f"L{L}_ffn_bt"]).then_inc(c_in, 16)
                if norm:
                    sp.dma_start(b1[:, :], a[f"L{L}_ffn_b1"].partition_broadcast(P)).then_inc(c_in, 16)
                    sp.dma_start(gt[:, :], a[f"L{L}_ffn_gt"]).then_inc(c_in, 16)
                if k.next_att is not None:
                    load_attention(sp, k, k.next_att)

                def step(j, s, first, more):
                    wait_pos(sp, xT_ps, j - 1)
                    row = sp.value_load(k.rows[0:1, bass.ds(j, 1)], min_val=0, max_val=E * CAP)
                    sp.dma_start(xin[s][:, :], k.xs[bass.ds(row, P), :]).then_inc(x_in[s], 16)
                over_tiles(sp, step, 0)
                for s in range(2):
                    sp.wait_ge(y_out[s], 16 * (NTILES // 2))

            @block.tensor
            def _(pe):
                def turn(j, s):
                    pe.wait_ge(x_in[s], 8 * j + (8 if s else 16))
                    wait_pos(pe, xT_copied, j)
                    for c in range(DC):
                        mm = pe.transpose(xT_b[:, c * P:(c + 1) * P], xin[s][:, c * P:(c + 1) * P], k.ident)
                    mm.then_inc(xT_ps, 1)

                def layer1(j, s):
                    e = pe.value_load(k.owner[0:1, bass.ds(j, 1)], min_val=0, max_val=E - 1)
                    pe.wait_ge(xT_copied, j + 1)
                    wait_pos(pe, h_read, j - 1)
                    for c in range(F // 512):
                        for kk in range(DC):
                            mm = pe.matmul(h_b[s][:, c * 512:(c + 1) * 512], xT[s][:, kk, :],
                                           w1[:, bass.ds(e * (DC * F) + (kk * F + c * 512), 512)],
                                           start=(kk == 0), stop=(kk == DC - 1))
                    mm.then_inc(h_ps, 1)

                def step(j, s, first, more):
                    sa = (s + A) % 2
                    if more(A):
                        turn(j + A, sa)
                    pe.wait_ge(h_ready, j + 1)
                    wait_pos(pe, gelu_done, j)
                    for f in range(FC):
                        mm = pe.transpose(hT_b[:, f, :], h[s][:, f * P:(f + 1) * P], k.ident)
                    mm.then_inc(hT_ps, 1)
                    if more(A):
                        layer1(j + A, sa)
                    e = pe.value_load(k.owner[0:1, bass.ds(j, 1)], min_val=0, max_val=E - 1)
                    pe.wait_ge(gelu_done, j + 1)
                    wait_pos(pe, y_done, j)
                    for f in range(FC):
                        mm = pe.matmul(y_b[:, 0:D], hT[s][:, f, :], w2[:, bass.ds(e * (FC * D) + f * D, D)],
                                       start=(f == 0), stop=(f == FC - 1))
                    mm.then_inc(y_ps, 1)

                pe.wait_ge(k.w_in, k.w_count)
                for j in range(A):
                    turn(j, j)
                    layer1(j, j)
                over_tiles(pe, step, A)

            @block.scalar
            def _(act):
                def copy(j, s):
                    act.wait_ge(xT_ps, j + 1)
                    act.activation(xT[s][:, :, :], xT_b[:, 0:D].rearrange("p (c q) -> p c q", c=DC),
                                   ACT.Copy).then_inc(xT_copied, 1)

                def store(j, s):
                    act.wait_ge(y_done, j + 1)
                    act.dma_start(k.ys[bass.ds(j * P, P), :], y[s][:, :]).then_inc(y_out[s], 16)

                def step(j, s, first, more):
                    if more(A):
                        copy(j + A, (s + A) % 2)
                    e = act.value_load(k.owner[0:1, bass.ds(j, 1)], min_val=0, max_val=E - 1)
                    act.wait_ge(hT_ps, j + 1)
                    for f in range(FC):
                        col = bass.ds(e * FC + f, 1)
                        g = act.activation(hT[s][:, f, :], hT_b[:, f, :], ACT.Gelu, bias=bt[:, col],
                                           scale=gt[:, col] if norm else 1.0)
                    g.then_inc(gelu_done, 1)
                    if not (isinstance(j, int) and j == 0):
                        store(j - 1, 1 - s)

                act.wait_ge(c_in, 64 if norm else 32)
                for j in range(A):
                    copy(j, j)
                over_tiles(act, step, A)
                store(NTILES - 1, 1)

            @block.vector
            def _(dve):
                def hidden(j, s):
                    if not norm:
                        dve.wait_ge(h_ps, j + 1)
                        dve.tensor_copy(h[s][:, :], h_b[s][:, :]).then_inc(h_ready, 1)
                        return
                    e = dve.value_load(k.owner[0:1, bass.ds(j, 1)], min_val=0, max_val=E - 1)
                    dve.wait_ge(h_ps, j + 1)
                    dve.tensor_tensor(h[s][:, :], h_b[s][:, :], b1[:, bass.ds(e * F, F)], ALU.add).then_inc(h_read, 1)
                    dve.wait_ge(h_read, j + 1)
                    dve.bn_stats(st[s][:, :], h[s][:, :])
                    dve.drain()
                    dve.bn_aggr(mv[s][:, :], st[s][:, :]).then_inc(aggr, 1)
                    dve.wait_ge(aggr, j + 1)
                    dve.tensor_scalar(ve[s][:, :], mv[s][:, 1:2], EPS, None, ALU.add).then_inc(var, 1)

                def centre(j, s):
                    dve.wait_ge(rsq, j + 1)
                    dve.tensor_scalar(h[s][:, :], h[s][:, :], mv[s][:, 0:1], rs[s][:, :],
                                      ALU.subtract, ALU.mult).then_inc(h_ready, 1)

                def step(j, s, first, more):
                    if more(A):
                        hidden(j + A, (s + A) % 2)
                    e = dve.value_load(k.owner[0:1, bass.ds(j, 1)], min_val=0, max_val=E - 1)
                    dve.wait_ge(y_ps, j + 1)
                    if not first:
                        wait_pos(dve, y_out[s], 8 * j - (8 if s else 0))
                    dve.tensor_tensor(y[s][:, :], y_b[:, 0:D], b2[:, bass.ds(e * D, D)], ALU.add).then_inc(y_done, 1)
                    if norm and more(A):
                        centre(j + A, (s + A) % 2)

                dve.wait_ge(c_in, 64 if norm else 32)
                for j in range(A):
                    hidden(j, j)
                    if norm:
                        centre(j, j)
                over_tiles(dve, step, A)

            if norm:
                @block.gpsimd
                def _(pool):
                    def step(j, s, first, more):
                        pool.wait_ge(var, j + 1)
                        pool.tensor_tensor(rs[s][:, :], ve[s][:, :], k.half[:, 0:1], ALU.pow).then_inc(rsq, 1)
                    over_tiles(pool, step, 0)


def combine(nc, k, L):
    ctx, sb, ps, sem = scoped(k)
    nm = f"c{L}_"
    with ctx:
        got = [[sb(f"{nm}g{j}_{r}", [P, D]) for r in range(RING)] for j in range(TOPK)]
        before = 32 * (NT // RING) * k.mixtures
        part, whole = sem(nm + "part"), sem(nm + "whole")
        with nc.Block() as block:
            @block.gpsimd
            def _(pool):
                for n in range(NT):
                    wait_pos(pool, whole, n - RING + 1)
                    for j in range(TOPK):
                        pool.indirect_dma_start(
                            out=got[j][n % RING][:, :], out_offset=None, in_=k.ys[:, :],
                            in_offset=bass.IndirectOffsetOnAxis(ap=k.pos[j][:, n:n + 1], axis=0)
                        ).then_inc(k.g_in[n % RING], 16)

            @block.vector
            def _(dve):
                acc = k.z if L == 0 else k.x
                with dve.Fori(0, NT // RING) as i:
                    for r in range(RING):
                        n = i * RING + r
                        at = acc[:, bass.ds(n * D, D)]
                        dve.wait_ge(k.g_in[r], i * 32 + (32 + before))
                        dve.scalar_tensor_tensor(at, got[0][r][:, :], k.wt[0][:, bass.ds(n, 1)], at,
                                                 ALU.mult, ALU.add).then_inc(part, 1)
                        dve.wait_ge(part, n + 1)
                        dve.scalar_tensor_tensor(at, got[1][r][:, :], k.wt[1][:, bass.ds(n, 1)], at,
                                                 ALU.mult, ALU.add).then_inc(whole, 1)
                        dve.wait_ge(whole, n + 1)
                        dve.bn_stats(k.stats[:, bass.ds(n, 1), :], at)


def post_norm(nc, k):
    ctx, sb, ps, sem = scoped(k)
    nm = "pn_"
    with ctx:
        g, b_ = sb(nm + "g", [P, D]), sb(nm + "b", [P, D])
        w_in, u_done, m_done, b_done, x_done = (sem(nm + c) for c in ("w_in", "u", "m", "b_done", "x"))
        span = lambda t, b: t[:, bass.ds(b * (TPB * D), TPB * D)].rearrange("p (t d) -> p t d", t=TPB)
        bc = lambda t: t[:, None, :].to_broadcast([P, TPB, D])
        with nc.Block() as block:
            @block.sync
            def _(sp):
                sp.dma_start(g[:, :], k.a["L0_ffn_ln_g"].partition_broadcast(P)).then_inc(w_in, 16)
                sp.dma_start(b_[:, :], k.a["L0_ffn_ln_b"].partition_broadcast(P)).then_inc(w_in, 16)

            @block.gpsimd
            def _(pool):
                pool.wait_ge(w_in, 32)
                with pool.Fori(0, NB) as b:
                    pool.tensor_tensor(span(k.x, b), span(k.x, b), bc(b_), ALU.add).then_inc(b_done, 1)

            @block.vector
            def _(dve):
                dve.wait_ge(w_in, 32)
                with dve.Fori(0, NB) as b:
                    for t in range(TPB):
                        n = b * TPB + t
                        at = k.z[:, bass.ds(n * D, D)]
                        v = dve.tensor_scalar(at, at, k.mean[:, bass.ds(n, 1)], k.rstd[:, bass.ds(n, 1)],
                                              ALU.subtract, ALU.mult)
                    v.then_inc(u_done, 1)
                    dve.wait_ge(u_done, b + 1)
                    dve.tensor_tensor(span(k.z, b), span(k.z, b), bc(g), ALU.mult).then_inc(m_done, 1)
                    dve.wait_ge(m_done, b + 1)
                    dve.wait_ge(b_done, b + 1)
                    dve.tensor_tensor(span(k.x, b), span(k.x, b), span(k.z, b), ALU.add).then_inc(x_done, 1)
                    dve.wait_ge(x_done, b + 1)
                    for t in range(TPB):
                        n = b * TPB + t
                        dve.bn_stats(k.stats[:, bass.ds(n, 1), :], k.xt(n))


def mixture(nc, k, L):
    ctx, sb, ps, sem = scoped(k)
    with ctx:
        k.pos = [sb(f"x{L}_pos{j}", [P, NT], U32) for j in range(TOPK)]
        k.wt = [sb(f"x{L}_wt{j}", [P, NT]) for j in range(TOPK)]
        k.owner, k.rows = (sb(f"x{L}_{n}", [1, NTILES], I32) for n in ("owner", "rows"))
        if L == 0:
            k.z = sb("x0_z", [P, NT * D])
        dispatch(nc, k, L)
        experts(nc, k, L)
        combine(nc, k, L)
        k.mixtures += 1
        if L == 0:
            ln_scalars(nc, k, "pn")
            post_norm(nc, k)


def load_quantum(eng, k):
    for t, src in zip(k.f1, ("L1_ffn_W1", "L1_ffn_W2", "L1_ffn_par")):
        eng.dma_start(t[:, :, :], k.a[src]).then_inc(k.f1_in, 16)
    eng.dma_start(k.f1[3][:, :], k.a["L1_ffn_b2"].partition_broadcast(P)).then_inc(k.f1_in, 16)


def load_window(eng, k):
    wa, wc, pt, ln = k.win
    for t, src in ((wa, "L2_Wa"), (wc, "L2_Wc")):
        eng.dma_start(t[:, :, :], k.a[src]).then_inc(k.win_in, 16)
    for t, src in ((pt, "pt"), (ln, "len")):
        eng.dma_start(t[:, :], k.a[src].partition_broadcast(P)).then_inc(k.win_in, 16)


def load_ternary(eng, k):
    for t, c in zip(k.f3_raw, ("gate", "up", "down")):
        eng.dma_start(t[:, :], k.a[f"L3_ffn_w_{c}"]).then_inc(k.f3_in, 16)


def quantum_ffn(nc, k):
    ctx, sb, ps, sem = scoped(k)
    nm = "f1_"
    a = k.a
    HS = 4
    FC = F1 // P
    with ctx:
        w1, w2, par, b2 = k.f1
        turn_t, half_t, cs, c_ = (sb(nm + n, [P, 2, FC]) for n in ("turn", "near", "cs", "c"))
        z = [sb(f"{nm}z{s}", [P, TPB, D]) for s in range(2)]
        zT = [sb(f"{nm}zT{s}", [P, DC, SEQ]) for s in range(2)]
        u = [sb(f"{nm}u{s}", [P, SEQ]) for s in range(HS)]
        near = [sb(f"{nm}near{s}", [P, SEQ]) for s in range(2)]
        q = [sb(f"{nm}q{s}", [P, FC, SEQ]) for s in range(2)]
        bank = ps(nm + "bank", [P, DC, SEQ])
        hb = [ps(f"{nm}h{i}", [P, SEQ]) for i in range(HS)]
        yb = [ps(f"{nm}y{s}", [P, 512]) for s in range(2)]
        w_in, v, sc = k.f1_in, sem(nm + "v"), sem(nm + "sc")
        z_done, b_done, zT_ps, zT_copied, h_ps, u_done, near_done, frac, sine, mixed, q_done, y_ps, x_added = (
            sem(nm + n) for n in ("z", "b", "zT_ps", "zT_copied", "h_ps", "u", "near", "frac", "sine",
                                  "mixed", "q", "y_ps", "x"))
        with nc.Block() as block:
            @block.gpsimd
            def _(pool):
                pool.wait_ge(w_in, 64)

                def step(b, s, first, last):
                    pool.wait_ge(z_done, b + 1)
                    xs = k.x[:, bass.ds(b * (TPB * D), TPB * D)].rearrange("p (t d) -> p t d", t=TPB)
                    pool.tensor_tensor(xs, xs, b2[:, None, :].to_broadcast([P, TPB, D]), ALU.add).then_inc(b_done, 1)
                over_batches(pool, step)

            @block.vector
            def _(dve):
                dve.wait_ge(w_in, 64)
                b1, th, wr, wi = (par[:, j, :] for j in range(4))
                tn, tc = turn_t[:, 0, :], turn_t[:, 1, :]
                n = [0]

                def then(op):
                    n[0] += 1
                    op.then_inc(v, 1)
                    dve.wait_ge(v, n[0])

                parts, rest = [], TWO_PI
                for _i in range(2):
                    hi = float(np.float32(np.round(rest * 2 ** (9 + 11 * _i)) / 2 ** (9 + 11 * _i)))
                    parts.append(hi)
                    rest -= hi
                parts.append(float(np.float32(rest)))
                kt = half_t[:, 0, :]
                then(dve.tensor_scalar(kt, th, 1.0 / TWO_PI, MAGIC, ALU.mult, ALU.add))
                then(dve.tensor_scalar(kt, kt, MAGIC, None, ALU.subtract))
                red = half_t[:, 1, :]
                then(dve.scalar_tensor_tensor(red, kt, -parts[0], th, ALU.mult, ALU.add))
                then(dve.scalar_tensor_tensor(red, kt, -parts[1], red, ALU.mult, ALU.add))
                then(dve.scalar_tensor_tensor(red, kt, -parts[2], red, ALU.mult, ALU.add))
                then(dve.tensor_scalar(tn, red, 1.0 / TWO_PI, None, ALU.mult))
                then(dve.tensor_scalar(tc, tn, 0.25, None, ALU.add))
                for j in range(2):
                    then(dve.tensor_scalar(half_t[:, j, :], turn_t[:, j, :], MAGIC, None, ALU.add))
                    then(dve.tensor_scalar(half_t[:, j, :], half_t[:, j, :], MAGIC, None, ALU.subtract))
                    then(dve.tensor_tensor(half_t[:, j, :], turn_t[:, j, :], half_t[:, j, :], ALU.subtract))
                dve.wait_ge(sc, 1)
                then(dve.tensor_tensor(c_[:, 0, :], cs[:, 1, :], wr, ALU.mult))
                then(dve.tensor_tensor(c_[:, 1, :], cs[:, 0, :], wi, ALU.mult))
                then(dve.tensor_tensor(c_[:, 0, :], c_[:, 0, :], c_[:, 1, :], ALU.add))
                then(dve.scalar_tensor_tensor(c_[:, 0, :], c_[:, 0, :], 0.1, wi, ALU.mult, ALU.mult))
                then(dve.scalar_tensor_tensor(c_[:, 1, :], b1, 0.1 / TWO_PI, tn, ALU.mult, ALU.add))
                assert n[0] == F1_CHAIN

                def normalise(b, s, t):
                    m = b * TPB + t
                    if t == 0:
                        wait_pos(dve, zT_ps, b - 1)
                    o = dve.tensor_scalar(z[s][:, t, :], k.xt(m), k.mean[:, bass.ds(m, 1)],
                                          k.rstd[:, bass.ds(m, 1)], ALU.subtract, ALU.mult)
                    if t == TPB - 1:
                        o.then_inc(z_done, 1)

                def fraction(m, f):
                    r = f % HS
                    dve.wait_ge(u_done, m + 1)
                    dve.tensor_scalar(near[f % 2][:, :], u[r][:, :], MAGIC, MAGIC, ALU.add,
                                      ALU.subtract).then_inc(near_done, 1)
                    dve.wait_ge(near_done, m + 1)
                    dve.tensor_tensor(u[r][:, :], u[r][:, :], near[f % 2][:, :], ALU.subtract).then_inc(frac, 1)

                def mix(m, f, s):
                    r = f % HS
                    dve.wait_ge(sine, m + 1)
                    dve.scalar_tensor_tensor(q[s][:, f, :], u[r][:, :], c_[:, 0, f:f + 1],
                                             hb[r][:, :], ALU.mult, ALU.add).then_inc(mixed, 1)
                    dve.wait_ge(mixed, m + 1)
                    dve.tensor_scalar(q[s][:, f, :], q[s][:, f, :], par[:, 0, f:f + 1], 0.0,
                                      ALU.add, ALU.max).then_inc(q_done, 1)

                def hidden(b, s, between=lambda f: None):
                    for f in range(FC):
                        fraction(b * FC + f, f)
                        if f > 0:
                            mix(b * FC + f - 1, f - 1, s)
                        between(f)
                    mix(b * FC + FC - 1, FC - 1, s)

                def residual(b, t):
                    m = b * TPB + t
                    dve.wait_ge(y_ps, m + 1)
                    dve.tensor_tensor(k.xt(m), yb[t % 2][:, 0:D], k.xt(m), ALU.add).then_inc(x_added, 1)

                def statistics(b, t):
                    m = b * TPB + t
                    dve.wait_ge(x_added, m + 1)
                    dve.bn_stats(k.stats[:, bass.ds(m, 1), :], k.xt(m))

                def step(b, s, after):
                    dve.wait_ge(b_done, b + 1)

                    def between(f):
                        if f < TPB and after(2):
                            normalise(b + 2, s, f)
                        if f % 2 == 1:
                            residual(b, f // 2)
                        elif f > 0:
                            statistics(b, f // 2 - 1)
                    if after(1):
                        hidden(b + 1, 1 - s, between)
                    else:
                        for f in range(FC):
                            between(f)
                    statistics(b, TPB - 1)

                for b in range(2):
                    for t in range(TPB):
                        normalise(b, b, t)
                hidden(0, 0)
                over_batches_ahead(dve, step)

            @block.scalar
            def _(act):
                act.wait_ge(v, F1_CHAIN - 5)
                act.activation(cs[:, :, :], half_t[:, :, :], ACT.Sin, scale=TWO_PI).then_inc(sc, 1)
                act.wait_ge(v, F1_CHAIN)

                def copy(b, s):
                    act.wait_ge(zT_ps, b + 1)
                    act.activation(zT[s][:, :, :], bank[:, :, :], ACT.Copy).then_inc(zT_copied, 1)

                def turns(m, f):
                    act.wait_ge(h_ps, m + 1)
                    act.activation(u[f % HS][:, :], hb[f % HS][:, :], ACT.Identity, bias=c_[:, 1, f:f + 1],
                                   scale=0.1 / TWO_PI).then_inc(u_done, 1)

                def sines(m, f):
                    act.wait_ge(frac, m + 1)
                    act.activation(u[f % HS][:, :], u[f % HS][:, :], ACT.Sin, scale=TWO_PI).then_inc(sine, 1)

                def hidden(b, between=lambda f: None):
                    for f in range(FC):
                        turns(b * FC + f, f)
                        if f > 0:
                            sines(b * FC + f - 1, f - 1)
                        between(f)
                    sines(b * FC + FC - 1, FC - 1)

                copy(0, 0)
                copy(1, 1)
                k.ahead(act)
                hidden(0)

                def step(b, s, after):
                    if after(1):
                        hidden(b + 1, lambda f: copy(b + 2, s) if f == 6 and after(2) else None)
                over_batches_ahead(act, step)

            @block.tensor
            def _(pe):
                pe.wait_ge(w_in, 64)

                def turn(b, s):
                    pe.wait_ge(z_done, b + 1)
                    wait_pos(pe, zT_copied, b)
                    for c in range(DC):
                        for t in range(TPB):
                            mm = pe.transpose(bank[:, c, t * P:(t + 1) * P], z[s][:, t, c * P:(c + 1) * P], k.ident)
                    mm.then_inc(zT_ps, 1)

                def hidden(b, s, f):
                    m = b * FC + f
                    wait_pos(pe, mixed, m - HS + 1)
                    for kk in range(DC):
                        mm = pe.matmul(hb[f % HS][:, :], w1[:, kk, f * P:(f + 1) * P], zT[s][:, kk, :],
                                       start=(kk == 0), stop=(kk == DC - 1))
                    mm.then_inc(h_ps, 1)

                def second(b, s, f):
                    t, half = f // 2, f % 2
                    m = b * TPB + t
                    if half == 0:
                        if f == 0:
                            pe.wait_ge(q_done, (b + 1) * FC)
                        wait_pos(pe, x_added, m - 1)
                    for g in range(half * FC // 2, (half + 1) * FC // 2):
                        mm = pe.matmul(yb[t % 2][:, 0:D], q[s][:, g, t * P:(t + 1) * P], w2[:, g, :],
                                       start=(g == 0), stop=(g == FC - 1))
                    if half:
                        mm.then_inc(y_ps, 1)

                turn(0, 0)
                turn(1, 1)
                pe.wait_ge(zT_copied, 1)
                for f in range(FC):
                    hidden(0, 0, f)

                def step(b, s, after):
                    if after(1):
                        pe.wait_ge(zT_copied, b + 2)
                    for f in range(FC):
                        if after(1):
                            hidden(b + 1, 1 - s, f)
                        second(b, s, f)
                        if f == 5 and after(2):
                            turn(b + 2, s)
                over_batches_ahead(pe, step)


F1_CHAIN = 18


def window_attention(nc, k):
    ctx, sb, ps, sem = scoped(k)
    nm = "a2_"
    a = k.a
    with ctx:
        wa, wc, pt, ln = k.win
        lo, hi, lf = sb(nm + "lo", [P, NB]), sb(nm + "hi", [P, NB]), sb(nm + "lf", [P, NB])
        keep, k2, neg = (sb(nm + n, [P, NB, S]) for n in ("keep", "k2", "neg"))
        dist, gauss = sb(nm + "dist", [P, NB]), sb(nm + "gauss", [P, NB])
        cx = [sb(f"{nm}cx{s}", [P, DC, 2, S]) for s in range(2)]
        z = [sb(f"{nm}z{s}", [P, TPB, D]) for s in range(2)]
        zT = [sb(f"{nm}zT{s}", [P, DC, SEQ]) for s in range(2)]
        ac = [sb(f"{nm}ac{s}", [P, DC, S]) for s in range(2)]
        cc = [sb(f"{nm}cc{s}", [P, D]) for s in range(2)]
        pr = [sb(f"{nm}pr{s}", [P, TPB, S]) for s in range(2)]
        mx, sm, rc = (sb(nm + n, [P, TPB]) for n in ("mx", "sm", "rc"))
        pT = sb(nm + "pT", [P, TPB // 2 * P])
        th = [sb(f"{nm}th{s}", [P, TPB, D]) for s in range(2)]
        bank = ps(nm + "bank", [P, DC, SEQ])
        cb, sbk, tb = ps(nm + "cb", [P, 512]), ps(nm + "sb", [P, 512]), ps(nm + "tb", [P, 512])
        yb = [ps(f"{nm}yb{s}", [P, 512]) for s in range(2)]
        w_in, v, ga = k.win_in, sem(nm + "v"), sem(nm + "ga")
        cx_in = [sem(f"{nm}cx_in{s}") for s in range(2)]
        (z_done, zT_ps, zT_copied, c_ps, c_read, s_ps, s_read, s_masked, s_max, s_sub, e_done, s_sum, s_rec,
         p_done, t_ps, t_copied, y_ps, t_done, x_added) = (
            sem(nm + n) for n in ("z", "zT_ps", "zT_copied", "c_ps", "c_read", "s_ps", "s_read", "s_masked",
                                  "s_max", "s_sub", "e", "s_sum", "s_rec", "p", "t_ps", "t_copied", "y_ps",
                                  "tanh", "x"))
        with nc.Block() as block:
            @block.sync
            def _(sp):
                def step(b, s, first, last):
                    wait_pos(sp, c_ps, b - 1)
                    for j in range(2):
                        sp.dma_start(cx[s][:, :, j, :],
                                     a["ctxT"][bass.ds(b, 1)].rearrange("b p c l -> p (b c) l")).then_inc(cx_in[s], 16)
                over_batches(sp, step)

            @block.vector
            def _(dve):
                n = [0]

                def then(op):
                    n[0] += 1
                    op.then_inc(v, 1)
                    dve.wait_ge(v, n[0])

                dve.wait_ge(w_in, 64)
                idx = k.cst[:, None, C_L:C_L + S].to_broadcast([P, NB, S])
                bc = lambda t: t[:, :, None].to_broadcast([P, NB, S])
                then(dve.tensor_copy(lf[:, :], ln[:, :]))
                then(dve.tensor_scalar(lo[:, :], pt[:, :], WINDOW, 0.0, ALU.subtract, ALU.max))
                then(dve.scalar_tensor_tensor(hi[:, :], pt[:, :], WINDOW, lf[:, :], ALU.add, ALU.min))
                then(dve.tensor_tensor(keep[:, :, :], idx, bc(lo), ALU.is_ge))
                then(dve.tensor_tensor(k2[:, :, :], idx, bc(hi), ALU.is_le))
                then(dve.tensor_tensor(keep[:, :, :], keep[:, :, :], k2[:, :, :], ALU.mult))
                then(dve.tensor_scalar(neg[:, :, :], keep[:, :, :], 1.0, 1e9, ALU.subtract, ALU.mult))
                then(dve.tensor_scalar(dist[:, :], pt[:, :], k.cst[:, C_P:C_P + 1], None, ALU.subtract))
                then(dve.tensor_tensor(dist[:, :], dist[:, :], dist[:, :], ALU.mult))
                dve.wait_ge(ga, 1)

                def normalise(b, s):
                    wait_pos(dve, zT_ps, b - 1)
                    for t in range(TPB):
                        m = b * TPB + t
                        o = dve.tensor_scalar(z[s][:, t, :], k.xt(m), k.mean[:, bass.ds(m, 1)],
                                              k.rstd[:, bass.ds(m, 1)], ALU.subtract, ALU.mult)
                    o.then_inc(z_done, 1)

                def prepare(b, s):
                    dve.wait_ge(c_ps, b + 1)
                    dve.tensor_copy(ac[s][:, :, :], cb[:, 0:DC * S].rearrange("p (c l) -> p c l", c=DC))
                    dve.tensor_scalar(cc[s][:, :], cb[:, D:2 * D], gauss[:, bass.ds(b, 1)], None,
                                      ALU.mult).then_inc(c_read, 1)

                def softmax(b, s, between):
                    p = pr[s][:, :, :]
                    at = lambda t: t[:, bass.ds(b, 1), :].to_broadcast([P, TPB, S])
                    bt = lambda t: t[:, :, None].to_broadcast([P, TPB, S])
                    dve.wait_ge(s_ps, b + 1)
                    dve.tensor_tensor(p, sbk[:, 0:TPB * S].rearrange("p (t l) -> p t l", t=TPB), at(keep),
                                      ALU.mult).then_inc(s_read, 1)
                    dve.wait_ge(s_read, b + 1)
                    dve.tensor_tensor(p, p, at(neg), ALU.add).then_inc(s_masked, 1)
                    dve.wait_ge(s_masked, b + 1)
                    dve.tensor_reduce(mx[:, :], p, AX.X, ALU.max).then_inc(s_max, 1)
                    dve.wait_ge(s_max, b + 1)
                    dve.tensor_tensor(p, p, bt(mx), ALU.subtract).then_inc(s_sub, 1)
                    between()
                    dve.wait_ge(e_done, b + 1)
                    dve.tensor_reduce(sm[:, :], p, AX.X, ALU.add).then_inc(s_sum, 1)
                    dve.wait_ge(s_sum, b + 1)
                    dve.reciprocal(rc[:, :], sm[:, :]).then_inc(s_rec, 1)
                    dve.wait_ge(s_rec, b + 1)
                    dve.tensor_tensor(p, p, bt(rc), ALU.mult).then_inc(p_done, 1)

                def residual(b, s):
                    dve.wait_ge(t_done, (b + 1) * TPB)
                    xs = k.x[:, bass.ds(b * (TPB * D), TPB * D)].rearrange("p (t d) -> p t d", t=TPB)
                    dve.tensor_tensor(xs, th[s][:, :, :], xs, ALU.add).then_inc(x_added, 1)

                def statistics(b):
                    dve.wait_ge(x_added, b + 1)
                    for t in range(TPB):
                        m = b * TPB + t
                        dve.bn_stats(k.stats[:, bass.ds(m, 1), :], k.xt(m))

                def step(b, s, after):
                    softmax(b, s, lambda: None if is_first(b) else residual(b - 1, 1 - s))
                    if after(1):
                        prepare(b + 1, 1 - s)
                    if after(2):
                        normalise(b + 2, s)
                    if not is_first(b):
                        statistics(b - 1)

                normalise(0, 0)
                normalise(1, 1)
                prepare(0, 0)
                over_batches_ahead(dve, step)
                residual(NB - 1, 1)
                statistics(NB - 1)

            @block.scalar
            def _(act):
                act.wait_ge(v, 9)
                act.activation(gauss[:, :], dist[:, :], ACT.Exp, scale=-1.0 / DEV_POW).then_inc(ga, 1)

                def copy(b, s):
                    act.wait_ge(zT_ps, b + 1)
                    wait_pos(act, y_ps, (b - 1) * TPB)
                    act.activation(zT[s][:, :, :], bank[:, :, :], ACT.Copy).then_inc(zT_copied, 1)

                def step(b, s, after):
                    act.wait_ge(s_sub, b + 1)
                    act.activation(pr[s][:, :, :], pr[s][:, :, :], ACT.Exp).then_inc(e_done, 1)
                    if after(1):
                        copy(b + 1, 1 - s)
                    act.wait_ge(t_ps, b + 1)
                    act.activation(pT[:, :], tb[:, 0:TPB // 2 * P], ACT.Copy).then_inc(t_copied, 1)
                    wait_pos(act, x_added, b - 1)
                    for t in range(TPB):
                        m = b * TPB + t
                        act.wait_ge(y_ps, m + 1)
                        act.activation(th[s][:, t, :], yb[t % 2][:, 0:D], ACT.Tanh).then_inc(t_done, 1)

                copy(0, 0)
                k.ahead(act)
                over_batches_ahead(act, step)

            @block.tensor
            def _(pe):
                pe.wait_ge(w_in, 64)

                def turn(b, s):
                    pe.wait_ge(z_done, b + 1)
                    wait_pos(pe, zT_copied, b)
                    for c in range(DC):
                        for t in range(TPB):
                            mm = pe.transpose(bank[:, c, t * P:(t + 1) * P], z[s][:, t, c * P:(c + 1) * P], k.ident)
                    mm.then_inc(zT_ps, 1)

                def prepare(b, s):
                    pe.wait_ge(cx_in[s], 16 * b + (16 if s else 32))
                    wait_pos(pe, c_read, b)
                    for c in range(DC):
                        for kk in range(DC):
                            pe.matmul(cb[:, c * S:(c + 1) * S], wa[:, kk, c * P:(c + 1) * P], cx[s][:, kk, 0, :],
                                      start=(kk == 0), stop=(kk == DC - 1))
                    for kk in range(DC):
                        mm = pe.matmul(cb[:, D:2 * D], cx[s][:, kk, :, :].rearrange("p j l -> p (j l)"), wc[:, kk, :],
                                       start=(kk == 0), stop=(kk == DC - 1))
                    mm.then_inc(c_ps, 1)

                def scores(b, s):
                    pe.wait_ge(zT_copied, b + 1)
                    pe.wait_ge(c_read, b + 1)
                    wait_pos(pe, s_read, b)
                    for t in range(TPB):
                        for kk in range(DC):
                            mm = pe.matmul(sbk[:, t * S:(t + 1) * S], zT[s][:, kk, t * P:(t + 1) * P], ac[s][:, kk, :],
                                           start=(kk == 0), stop=(kk == DC - 1))
                    mm.then_inc(s_ps, 1)

                def step(b, s, after):
                    if after(1):
                        turn(b + 1, 1 - s)
                        prepare(b + 1, 1 - s)
                    pe.wait_ge(p_done, b + 1)
                    for g in range(TPB // 2):
                        mm = pe.transpose(tb[:, g * P:(g + 1) * P],
                                          pr[s][:, 2 * g:2 * g + 2, :].rearrange("p t l -> p (t l)"), k.ident)
                    mm.then_inc(t_ps, 1)
                    if after(1):
                        scores(b + 1, 1 - s)
                    pe.wait_ge(t_copied, b + 1)
                    for t in range(TPB):
                        m = b * TPB + t
                        wait_pos(pe, t_done, m - 1)
                        for kk in range(DC):
                            pe.matmul(yb[t % 2][:, 0:D], zT[s][:, kk, t * P:(t + 1) * P], wc[:, DC + kk, :],
                                      start=(kk == 0), stop=False)
                        half = slice(t % 2 * S, (t % 2 + 1) * S)
                        pe.matmul(yb[t % 2][:, 0:D], pT[half, t // 2 * P:(t // 2 + 1) * P], cc[s][half, :],
                                  start=False, stop=True).then_inc(y_ps, 1)

                turn(0, 0)
                prepare(0, 0)
                scores(0, 0)
                over_batches_ahead(pe, step)


def ternary_ffn(nc, k, out):
    ctx, sb, ps, sem = scoped(k)
    nm = "f3_"
    a = k.a
    FC = F3 // P
    with ctx:
        z = [sb(f"{nm}z{s}", [P, TPB, D]) for s in range(2)]
        xq = [sb(f"{nm}xq{s}", [P, TPB, D], BF16) for s in range(2)]
        xT = [sb(f"{nm}xT{s}", [P, DC, SEQ], BF16) for s in range(2)]
        am, sc, rc = (sb(nm + n, [P, TPB]) for n in ("am", "sc", "rc"))
        sg = [sb(f"{nm}sg{s}", [P, TPB]) for s in range(2)]
        su = [sb(f"{nm}su{s}", [P, TPB]) for s in range(2)]
        g_ = [sb(f"{nm}g{s}", [P, F3]) for s in range(2)]
        h = [sb(f"{nm}h{s}", [P, F3]) for s in range(2)]
        hq = [sb(f"{nm}hq{s}", [P, F3], BF16) for s in range(2)]
        hm, hr, hs, hd = ([sb(f"{nm}{n}{s}", [P, 1]) for s in range(2)] for n in ("hm", "hr", "hs", "hd"))
        hT = [sb(f"{nm}hT{s}", [P, FC, P], BF16) for s in range(2)]
        ident = sb(nm + "ident", [P, P], BF16)
        wq = {c: sb(nm + "wq" + c, [P, 2 * F3], BF16) for c in "gud"}
        wsum, wmean, wscale = (sb(nm + n, [P, 3]) for n in ("wsum", "wmean", "wscale"))
        xb = ps(nm + "xb", [P, DC, SEQ], BF16)
        gb, ub = ps(nm + "gb", [P, F3]), ps(nm + "ub", [P, F3])
        hb = ps(nm + "hb", [P, FC, P], BF16)
        yb = [ps(f"{nm}yb{s}", [P, 512]) for s in range(2)]
        w_in, v, tot_ps = k.f3_in, sem(nm + "v"), sem(nm + "tot")
        (z_done, z_max, z_clip, z_rec, z_scale, z_mul, xq_done, x_ps, x_copied, g_ps, g_done, h_done, h_max,
         h_clip, h_rec, h_scale, h_mul, hq_done, h_tp, h_copied, y_ps, x_added) = (
            sem(nm + n) for n in ("z", "z_max", "z_clip", "z_rec", "z_scale", "z_mul", "xq", "x_ps", "x_copied",
                                  "g_ps", "g_done", "h", "h_max", "h_clip", "h_rec", "h_scale", "h_mul", "hq",
                                  "h_tp", "h_copied", "y_ps", "x"))
        stored, u_ps = sem(nm + "stored"), sem(nm + "u_ps")
        N3 = 2 * F3
        with ExitStack() as wctx:
            raw = k.f3_raw
            tb = yb[0]
            with nc.Block() as block:
                @block.vector
                def _(dve):
                    n = [0]

                    def then(op):
                        n[0] += 1
                        op.then_inc(v, 1)
                        dve.wait_ge(v, n[0])

                    dve.wait_ge(w_in, 48)
                    for j in range(3):
                        dve.tensor_reduce(wsum[:, j:j + 1], raw[j][:, :], AX.X, ALU.add,
                                          apply_absolute_value=True).then_inc(v, 1)
                    n[0] = 3
                    dve.wait_ge(tot_ps, 1)
                    then(dve.tensor_scalar(wmean[:, :], tb[:, 0:3], 1.0 / (D * F3), 1e-5, ALU.mult, ALU.max))
                    then(dve.reciprocal(wscale[:, :], wmean[:, :]))
                    for j, c in enumerate("gud"):
                        then(dve.tensor_scalar(raw[j][:, :], raw[j][:, :], wscale[:, j:j + 1], MAGIC,
                                               ALU.mult, ALU.add))
                        then(dve.tensor_scalar(raw[j][:, :], raw[j][:, :], MAGIC, 1.0, ALU.subtract, ALU.min))
                        dve.tensor_scalar(wq[c][:, :], raw[j][:, :], -1.0, None, ALU.max)
                    dve.tensor_copy(ident[:, :], k.ident)

                @block.tensor
                def _(pe):
                    pe.wait_ge(v, 3)
                    pe.matmul(tb[:, 0:3], k.cst[:, C_ONE:C_ONE + P], wsum[:, :], start=True, stop=True).then_inc(tot_ps, 1)

        wg = wq["g"][:, :].rearrange("p (c f) -> p c f", c=DC)
        wu = wq["u"][:, :].rearrange("p (c f) -> p c f", c=DC)
        wd = wq["d"][:, :].rearrange("p (c f) -> p c f", c=FC)
        with nc.Block() as block:
            @block.vector
            def _(dve):
                def quantise(b, s):
                    wait_pos(dve, x_ps, b - 1)
                    for t in range(TPB):
                        m = b * TPB + t
                        o = dve.tensor_scalar(z[s][:, t, :], k.xt(m), k.mean[:, bass.ds(m, 1)],
                                              k.rstd[:, bass.ds(m, 1)], ALU.subtract, ALU.mult)
                    o.then_inc(z_done, 1)
                    dve.wait_ge(z_done, b + 1)
                    dve.tensor_reduce(am[:, :], z[s][:, :, :], AX.X, ALU.max, apply_absolute_value=True).then_inc(z_max, 1)
                    dve.wait_ge(z_max, b + 1)
                    dve.tensor_scalar(am[:, :], am[:, :], 1e-5, None, ALU.max).then_inc(z_clip, 1)
                    dve.wait_ge(z_clip, b + 1)
                    dve.reciprocal(rc[:, :], am[:, :]).then_inc(z_rec, 1)
                    dve.tensor_scalar(sg[s][:, :], am[:, :], 1.0 / 127.0, wmean[:, 0:1], ALU.mult, ALU.mult)
                    dve.tensor_scalar(su[s][:, :], am[:, :], 1.0 / 127.0, wmean[:, 1:2], ALU.mult, ALU.mult)
                    dve.wait_ge(z_rec, b + 1)
                    dve.tensor_scalar(sc[:, :], rc[:, :], 127.0, None, ALU.mult).then_inc(z_scale, 1)
                    dve.wait_ge(z_scale, b + 1)
                    for t in range(TPB):
                        o = dve.tensor_scalar(z[s][:, t, :], z[s][:, t, :], sc[:, t:t + 1], MAGIC, ALU.mult, ALU.add)
                    o.then_inc(z_mul, 1)
                    dve.wait_ge(z_mul, b + 1)
                    dve.tensor_scalar(xq[s][:, :, :], z[s][:, :, :], MAGIC, 127.0, ALU.subtract, ALU.min).then_inc(xq_done, 1)

                def hidden(m, t, s):
                    u = t % 2
                    dve.wait_ge(g_done, m + 1)
                    dve.wait_ge(u_ps, m + 1)
                    dve.scalar_tensor_tensor(h[u][:, :], ub[:, :], su[s][:, t:t + 1], g_[u][:, :],
                                             ALU.mult, ALU.mult).then_inc(h_done, 1)
                    dve.wait_ge(h_done, m + 1)
                    dve.tensor_reduce(hm[u][:, :], h[u][:, :], AX.X, ALU.max, apply_absolute_value=True).then_inc(h_max, 1)
                    dve.wait_ge(h_max, m + 1)
                    dve.tensor_scalar(hm[u][:, :], hm[u][:, :], 1e-5, None, ALU.max).then_inc(h_clip, 1)
                    dve.wait_ge(h_clip, m + 1)
                    dve.reciprocal(hr[u][:, :], hm[u][:, :]).then_inc(h_rec, 1)
                    dve.tensor_scalar(hd[u][:, :], hm[u][:, :], 1.0 / 127.0, wmean[:, 2:3], ALU.mult, ALU.mult)
                    dve.wait_ge(h_rec, m + 1)
                    dve.tensor_scalar(hs[u][:, :], hr[u][:, :], 127.0, None, ALU.mult).then_inc(h_scale, 1)
                    dve.wait_ge(h_scale, m + 1)
                    dve.tensor_scalar(h[u][:, :], h[u][:, :], hs[u][:, :], MAGIC, ALU.mult, ALU.add).then_inc(h_mul, 1)
                    dve.wait_ge(h_mul, m + 1)
                    dve.tensor_scalar(hq[u][:, :], h[u][:, :], MAGIC, 127.0, ALU.subtract, ALU.min).then_inc(hq_done, 1)

                def residual(m, t):
                    dve.wait_ge(y_ps, m + 1)
                    dve.scalar_tensor_tensor(k.xt(m), yb[t % 2][:, 0:D], hd[t % 2][:, :], k.xt(m),
                                             ALU.mult, ALU.add).then_inc(x_added, 1)

                def step(b, s, first, last):
                    for t in range(TPB):
                        m = b * TPB + t
                        if t == 0 and not last:
                            quantise(b + 1, 1 - s)
                        hidden(m, t, s)
                        if not (first and t == 0):
                            residual(m - 1, t - 1)

                quantise(0, 0)
                over_batches(dve, step)
                residual(NT - 1, TPB - 1)

            @block.scalar
            def _(act):
                def copy(b, s):
                    act.wait_ge(x_ps, b + 1)
                    act.activation(xT[s][:, :, :], xb[:, :, :], ACT.Copy).then_inc(x_copied, 1)

                def silu(m, t, s):
                    act.wait_ge(g_ps, m + 1)
                    act.activation(g_[t % 2][:, :], gb[:, :], ACT.Silu, scale=sg[s][:, t:t + 1]).then_inc(g_done, 1)

                def step(b, s, first, last):
                    for t in range(TPB):
                        m = b * TPB + t
                        act.wait_ge(h_tp, m + 1)
                        act.activation(hT[t % 2][:, :, :], hb[:, :, :], ACT.Copy).then_inc(h_copied, 1)
                        if t < TPB - 2:
                            silu(m + 2, t + 2, s)
                        elif not last:
                            silu(m + 2, t + 2 - TPB, 1 - s)
                        if t == 1 and not last:
                            copy(b + 1, 1 - s)

                copy(0, 0)
                silu(0, 0, 0)
                silu(1, 1, 0)
                over_batches(act, step)

            @block.tensor
            def _(pe):
                def turn(b, s):
                    pe.wait_ge(xq_done, b + 1)
                    wait_pos(pe, x_copied, b)
                    for c in range(DC):
                        for t in range(TPB):
                            mm = pe.transpose(xb[:, c, t * P:(t + 1) * P], xq[s][:, t, c * P:(c + 1) * P], ident[:, :])
                    mm.then_inc(x_ps, 1)

                def first_layers(m, t, s):
                    for w, dst, left, filled in ((wg, gb, g_done, g_ps), (wu, ub, h_done, u_ps)):
                        wait_pos(pe, left, m)
                        for j in range(F3 // 512):
                            for c in range(DC):
                                mm = pe.matmul(dst[:, j * 512:(j + 1) * 512], xT[s][:, c, t * P:(t + 1) * P],
                                               w[:, c, j * 512:(j + 1) * 512], start=(c == 0), stop=(c == DC - 1))
                        mm.then_inc(filled, 1)

                def step(b, s, first, last):
                    for t in range(TPB):
                        m = b * TPB + t
                        pe.wait_ge(hq_done, m + 1)
                        wait_pos(pe, h_copied, m)
                        for f in range(FC):
                            mm = pe.transpose(hb[:, f, :], hq[t % 2][:, f * P:(f + 1) * P], ident[:, :])
                        mm.then_inc(h_tp, 1)
                        if t < TPB - 2:
                            first_layers(m + 2, t + 2, s)
                        elif not last:
                            if t == 2:
                                pe.wait_ge(x_copied, b + 2)
                            first_layers(m + 2, t + 2 - TPB, 1 - s)
                        if t == 1 and not last:
                            turn(b + 1, 1 - s)
                        pe.wait_ge(h_copied, m + 1)
                        wait_pos(pe, x_added, m - 1)
                        for f in range(FC):
                            mm = pe.matmul(yb[t % 2][:, 0:D], hT[t % 2][:, f, :], wd[:, f, :],
                                           start=(f == 0), stop=(f == FC - 1))
                        mm.then_inc(y_ps, 1)

                turn(0, 0)
                pe.wait_ge(x_copied, 1)
                first_layers(0, 0, 0)
                first_layers(1, 1, 0)
                over_batches(pe, step)

            @block.sync
            def _(sp):
                def step(b, s, first, last):
                    sp.wait_ge(x_added, b * TPB + TPB)
                    xs = k.x[:, bass.ds(b * (TPB * D), TPB * D)].rearrange("p (t d) -> p t d", t=TPB)
                    sp.dma_start(out[bass.ds(b, 1)].rearrange("b (t p) d -> p (b t) d", p=P), xs).then_inc(stored, 16)
                over_batches(sp, step)
                sp.wait_ge(stored, 16 * NB)


def load_early(nc, k, load):
    with nc.Block() as block:
        @block.sync
        def _(sp):
            load(sp, k)


def store_stage(nc, k, out):
    ctx, sb, ps, sem = scoped(k)
    with ctx:
        stored = sem("stored")
        with nc.Block() as block:
            @block.sync
            def _(sp):
                for b in range(NB):
                    sp.dma_start(out[b].rearrange("(t p) d -> p t d", p=P),
                                 k.x[:, b * TPB * D:(b + 1) * TPB * D].rearrange("p (t d) -> p t d", t=TPB)
                                 ).then_inc(stored, 16)
                sp.wait_ge(stored, 16 * NB)


def build(nc, a, out, stages="a0 m0 a1 f1 w2 m2 a3 f3"):
    nothing = lambda sp: None
    with ExitStack() as ctx:
        k = Core(nc, ctx, a)
        todo = stages.split()
        layers = [int(st[1]) for st in todo if st[0] == "a"]
        k.first_att = layers[0] if layers else None
        load_stage(nc, k)
        weights = ExitStack()
        room = lambda n, words: weights.enter_context(nc.sbuf_tensor(n, [P, words], F32))

        def run(st, ahead=nothing):
            k.ahead = ahead
            ln_scalars(nc, k, st)
            if st[0] == "a":
                attention(nc, k, int(st[1]))
            elif st[0] == "m":
                after = [L for L in layers if L > int(st[1])]
                k.next_att = after[0] if after and layers[0] <= int(st[1]) else None
                mixture(nc, k, int(st[1]))
            elif st == "f1":
                quantum_ffn(nc, k)
            elif st == "w2":
                window_attention(nc, k)
            elif st == "f3":
                ternary_ffn(nc, k, out)

        def m0_weights(eng):
            load_first_layers(eng, k, 0, range(E))
            load_second_layers(eng, k, 0)

        def first_stage(st):
            return todo[0] == st

        if "m0" in todo:
            k.w1, k.w2 = room("m0_w1", E * DC * F0), room("m0_w2", E * F0 // P * D)
            k.w_count = 16 * 2 * E
            k.late = m0_weights if first_stage("m0") else nothing
        if "a0" in todo:
            run("a0", m0_weights if "m0" in todo else nothing)
        if "m0" in todo:
            run("m0")
            weights.close()
        if "m2" in todo:
            before = k.w_count if "m0" in todo else 0
            k.w_count = before + 16 * 2 * E
            k.w2 = room("m2_w2", E * F2 // P * D)
        with ExitStack() as small:
            sb = lambda n, s, d=F32: small.enter_context(nc.sbuf_tensor(n, s, d))
            k.f1 = (sb("f1_w1", [P, DC, F1]), sb("f1_w2", [P, F1 // P, D]), sb("f1_par", [P, 4, F1 // P]),
                    sb("f1_b2", [P, D]))
            k.win = (sb("a2_wa", [P, DC, D]), sb("a2_wc", [P, 2 * DC, D]), sb("a2_pt", [P, NB]),
                     sb("a2_ln", [P, NB], I32))
            if todo[0] in ("f1", "w2"):
                load_early(nc, k, (load_quantum if todo[0] == "f1" else load_window))

            def a1_ahead(eng):
                load_quantum(eng, k)
                if "m2" in todo:
                    load_second_layers(eng, k, 2)
            if "a1" in todo:
                run("a1", a1_ahead)
            if "f1" in todo:
                run("f1", (lambda eng: load_window(eng, k)) if "w2" in todo else nothing)
            if "w2" in todo:
                run("w2")
        if "m2" in todo:
            k.w1 = room("m2_w1", E * DC * F2)

            def m2_late(eng):
                if "a1" not in todo:
                    load_second_layers(eng, k, 2)
                load_first_layers(eng, k, 2, range(E))
            k.late = m2_late
            run("m2")
            weights.close()
        with ExitStack() as small:
            k.f3_raw = [small.enter_context(nc.sbuf_tensor("f3_raw" + c, [P, 2 * F3], F32)) for c in "gud"]
            if todo[0] == "f3":
                load_early(nc, k, load_ternary)
            if "a3" in todo:
                run("a3", lambda eng: load_ternary(eng, k))
            if "f3" in todo:
                run("f3")
        if "f3" not in todo:
            store_stage(nc, k, out)


def chunked(w):
    return np.ascontiguousarray(np.asarray(w).reshape(-1, P, w.shape[-1]).transpose(1, 0, 2))


def layout(inputs):
    i = {n: np.asarray(v) for n, v in inputs.items()}
    a = {"x": i["x"], "cst": constants(), "tau": i["condB_tau"], "delta": i["fside_BxS2_0"].reshape(-1)}
    a["ctxT"] = np.ascontiguousarray(i["ctx_1024"].reshape(NB, S, DC, P).transpose(0, 3, 2, 1))
    for L in (0, 1, 3):
        for c in "qkvo":
            a[f"L{L}_xcond_W{c}"] = chunked(i[f"L{L}_xcond_W{c}"].T)
        for c in "qk":
            a[f"L{L}_xcond_b{c}"] = np.ascontiguousarray(i[f"L{L}_xcond_b{c}"].reshape(DC, P).T)
        for c in "vo":
            a[f"L{L}_xcond_b{c}"] = i[f"L{L}_xcond_b{c}"]
    a["L0_gate"], a["L2_gate"] = chunked(i["L0_ffn_gate_w"]), chunked(i["L2_ffn_router_w"].T)
    for L, w1, w2 in ((0, i["L0_ffn_w1"], i["L0_ffn_w2"]),
                      (2, i["L2_ffn_w1"].transpose(0, 2, 1), i["L2_ffn_w2"].transpose(0, 2, 1))):
        for n, w in (("w1", w1), ("w2", w2)):
            w = w.reshape(E, -1, P, w.shape[-1]).transpose(2, 0, 1, 3)
            a[f"L{L}_ffn_{n}"] = np.ascontiguousarray(w.reshape(P, E, -1))
        a[f"L{L}_ffn_b2"] = i[f"L{L}_ffn_b2"].reshape(-1)
    for n, v in (("L0_ffn_bt", i["L0_ffn_ln1_b"]), ("L0_ffn_gt", i["L0_ffn_ln1_g"]), ("L2_ffn_bt", i["L2_ffn_b1"])):
        a[n] = np.ascontiguousarray(v.reshape(-1, P).T)
    a["L0_ffn_b1"] = i["L0_ffn_b1"].reshape(-1)
    a["L1_ffn_W1"], a["L1_ffn_W2"] = chunked(i["L1_ffn_W1"]), chunked(i["L1_ffn_W2"])
    a["L1_ffn_par"] = np.ascontiguousarray(np.stack([
        i["L1_ffn_" + n].reshape(-1, P) for n in ("b1", "quantum_phases", "quantum_weights_real",
                                                  "quantum_weights_imag")]).transpose(2, 0, 1))
    a["L1_ffn_b2"] = i["L1_ffn_b2"]
    a["L2_Wa"], a["L2_Wc"] = chunked(i["L2_xcond_W_a"].T), chunked(i["L2_xcond_W_c"].T)
    a["pt"], a["len"] = i["condB_pt"], i["_lenS2"]
    for n in ("gate", "up", "down"):
        a["L3_ffn_w_" + n] = chunked(i["L3_ffn_w_" + n].T).reshape(P, -1)
    a["L0_ffn_ln_g"], a["L0_ffn_ln_b"] = i["L0_ffn_ln_g"], i["L0_ffn_ln_b"]
    return a


def kernel(**inputs):
    import concourse.bacc as bacc
    from concourse.bass_utils import run_bass_kernel_spmd

    nc = bacc.Bacc("TRN2", target_bir_lowering=False, num_devices=1)
    arrays = {f"in_{n}": v for n, v in layout(inputs).items()}
    a = {n[3:]: nc.dram_tensor(n, v.shape, mybir.dt.from_np(v.dtype), kind="ExternalInput").ap()
         for n, v in arrays.items()}
    out = nc.dram_tensor("out_x", (NB, SEQ, D), F32, kind="ExternalOutput").ap()
    build(nc, a, out)
    r = run_bass_kernel_spmd(nc, [arrays], core_ids=[0])
    return r.results[0]["out_x"]
```

```python
from contextlib import ExitStack

import numpy as np

import concourse.bass as bass
from concourse import mybir

F32 = mybir.dt.float32
BF16 = mybir.dt.bfloat16
I32 = mybir.dt.int32
U32 = mybir.dt.uint32
ALU = mybir.AluOpType
ACT = mybir.ActivationFunctionType
AX = mybir.AxisListType

P = 128
NB, SEQ, D = 8, 512, 256
TPB = SEQ // P
NT = NB * TPB
DC = D // P
S = 64
H, DK = 16, 16
HPC = H // DC
VW = DK + 1
E, TOPK = 8, 2
F0, F1, F2, F3 = 512, 1024, 1024, 1024
NTILES = TOPK * NT + E
CAP = (NT + 1) * P
EPS = 1e-5
MAGIC = 1.5 * 2.0 ** 23
TWO_PI = 2.0 * np.pi
WINDOW, DEV_POW = 16.0, 128.0

C_ID, C_TRI, C_ONE = 0, P, 2 * P
C_HM = 3 * P
C_L = C_HM + HPC
C_P = C_L + S
C_E = C_P + 1
C_J = C_E + E
C_REGION = C_J + NTILES
C_PART = C_REGION + E
C_N = C_PART + 1


def constants():
    c = np.zeros((P, C_N), np.float32)
    p = np.arange(P)
    c[:, C_ID:C_ID + P] = np.eye(P)
    c[:, C_TRI:C_TRI + P] = p[:, None] < p[None, :]
    c[:, C_ONE:C_ONE + P] = 1.0
    c[:, C_HM:C_HM + HPC] = p[:, None] // DK == np.arange(HPC)[None, :]
    c[:, C_L:C_L + S] = np.arange(S)
    c[:, C_P] = p % S
    c[:, C_E:C_E + E] = E - np.arange(E)
    c[:, C_J:C_J + NTILES] = np.arange(NTILES)
    c[:, C_REGION:C_REGION + E] = CAP * np.arange(E)
    c[:, C_PART] = p
    return c


def wait_pos(eng, sem, value):
    if not (isinstance(value, int) and value <= 0):
        eng.wait_ge(sem, value)


def over_batches(eng, step, count=NB):
    step(0, 0, True, False)
    with eng.Fori(0, (count - 2) // 2) as i:
        step(i * 2 + 1, 1, False, False)
        step(i * 2 + 2, 0, False, False)
    step(count - 1, 1, False, True)


def over_batches_ahead(eng, step):
    step(0, 0, lambda d: True)
    with eng.Fori(0, (NB - 4) // 2) as i:
        step(i * 2 + 1, 1, lambda d: True)
        step(i * 2 + 2, 0, lambda d: True)
    for b in range(NB - 3, NB):
        step(b, b % 2, lambda d, b=b: b + d < NB)


def is_first(b):
    return isinstance(b, int) and b == 0


class Core:

    def __init__(self, nc, ctx, a):
        self.nc, self.a = nc, a
        self.stale = []
        sem = lambda n: ctx.enter_context(nc.semaphore(n))
        self.zeroed, self.padded = sem("zeroed"), sem("padded")
        self.scattered = [sem(f"scattered{s}") for s in range(2)]
        self.g_in = [sem(f"g_in{r}") for r in range(RING)]
        self.mixtures, self.gathers = 0, 0
        self.w_in = sem("w_in")
        self.psum = ctx.enter_context(nc.psum_tensor("psum", [P, 8 * BANK], F32))
        sb = lambda n, s, d=F32: ctx.enter_context(nc.sbuf_tensor(n, s, d))
        self.x = sb("x_res", [P, NT * D])
        self.cst = sb("cst", [P, C_N])
        self.stats = sb("stats", [P, NT, 6])
        self.mean = sb("mean", [P, NT])
        self.rstd = sb("rstd", [P, NT])
        self.half = sb("half", [P, NT])
        self.lnt = sb("lnt", [P, 3, NT])
        self.tau = sb("tau", [P, NB])
        self.delta = sb("delta", [P, NB * S])
        self.xs = nc.dram_tensor("sorted_in", [E * CAP + P, D], F32, kind="Internal").ap()
        self.ys = nc.dram_tensor("sorted_out", [NTILES * P, D], F32, kind="Internal").ap()
        self.pos = [sb(f"pos{j}", [P, NT], U32) for j in range(TOPK)]
        self.wt = [sb(f"wt{j}", [P, NT]) for j in range(TOPK)]
        self.att_w = {c: sb("att_w" + c, [P, DC, D]) for c in "qkvo"}
        self.att_b = [sb("att_b" + c, [P, DC if c in "qk" else D]) for c in "qkvo"]
        self.att_in, self.att_loads = sem("att_in"), 0
        self.arriving = self.normed = False
        self.f1_in, self.win_in, self.f3_in = sem("f1_in"), sem("win_in"), sem("f3_in")
        self.ident = self.cst[:, C_ID:C_ID + P]

    def xt(self, n):
        return self.x[:, bass.ds(n * D, D)]


RING = 4
BANK = 512


def scoped(k):
    nc, taken = k.nc, [0]
    ctx = ExitStack()
    sb = lambda n, s, d=F32: ctx.enter_context(nc.sbuf_tensor(n, s, d))

    def ps(name, shape, dtype=F32):
        size = int(np.prod(shape[1:]))
        words = size // (2 if dtype == BF16 else 1)
        at, taken[0] = taken[0], taken[0] + -(-words // BANK)
        assert taken[0] <= 8, name
        ap = k.psum[:, at * BANK:at * BANK + words]
        if dtype == BF16:
            ap = ap.bitcast(BF16)
        return ap if len(shape) == 2 else ap.rearrange("p (a b) -> p a b", a=shape[1])


    def sem(name):
        handle = ctx.enter_context(nc.semaphore(name))
        k.stale.append(handle)
        return handle

    return ctx, sb, ps, sem


def clear_stale(k, pool, own):
    numbers = sorted({s.num for s in k.stale} - {s.num for s in own})
    k.stale = list(own)
    while numbers:
        n = 1
        while n < len(numbers) and numbers[n] == numbers[0] + n:
            n += 1
        pool.sem_clear(range(numbers[0], numbers[0] + n))
        numbers = numbers[n:]


def load_stage(nc, k):
    ctx, sb, ps, sem = scoped(k)
    a = k.a
    with ctx:
        loaded, x_loaded, half_set = sem("ld_small"), sem("ld_x"), sem("ld_half")
        zero_set = sem("ld_zero_set")
        zero = sb("ld_zero", [P, D])
        with nc.Block() as block:
            @block.sync
            def _(sp):
                for b in range(NB):
                    sp.dma_start(k.x[:, b * TPB * D:(b + 1) * TPB * D].rearrange("p (t d) -> p t d", t=TPB),
                                 a["x"][b].rearrange("(t p) d -> p t d", p=P)).then_inc(x_loaded, 16)

            @block.scalar
            def _(act):
                act.dma_start(k.cst[:, :], a["cst"]).then_inc(loaded, 16)
                act.dma_start(k.tau[:, :], a["tau"].partition_broadcast(P)).then_inc(loaded, 16)
                act.dma_start(k.delta[:, :], a["delta"].partition_broadcast(P)).then_inc(loaded, 16)
                if k.first_att is not None:
                    load_attention(act, k, k.first_att)

            @block.gpsimd
            def _(pool):
                pool.memset(k.half[:, :], -0.5).then_inc(half_set, 1)
                pool.memset(zero[:, :], 0.0).then_inc(zero_set, 1)
                pool.wait_ge(zero_set, 1)
                pool.dma_start(k.xs[E * CAP:E * CAP + P, :], zero[:, :]).then_inc(k.zeroed, 16)
                pool.wait_ge(k.zeroed, 16)

            @block.vector
            def _(dve):
                dve.wait_ge(loaded, 48)
                dve.tensor_scalar(k.tau[:, :], k.tau[:, :], DK ** -0.5, None, ALU.mult)
                dve.tensor_scalar(k.delta[:, :], k.delta[:, :], DK ** -0.5, None, ALU.mult)
                for b in range(NB):
                    if b == 0:
                        dve.wait_ge(x_loaded, 16 * NB)
                    for t in range(TPB):
                        n = b * TPB + t
                        dve.bn_stats(k.stats[:, n, :], k.x[:, n * D:(n + 1) * D])


def clean_stage(nc, k):
    with nc.Block() as block:
        @block.gpsimd
        def _(pool):
            clear_stale(k, pool, ())


def ln_scalars(nc, k, name):
    ctx, sb, ps, sem = scoped(k)
    with ctx:
        dv, pw = sem(name + "_lnv"), sem(name + "_lnp")
        me, ve, mo, vo = (k.stats[:, :, j] for j in (1, 2, 4, 5))
        d, m2, v = (k.lnt[:, j, :] for j in range(3))
        with nc.Block() as block:
            @block.vector
            def _(dve):
                dve.tensor_tensor(d, me, mo, ALU.subtract).then_inc(dv, 1)
                dve.tensor_tensor(m2, ve, vo, ALU.add).then_inc(dv, 1)
                dve.tensor_tensor(k.mean[:, :], me, mo, ALU.add).then_inc(dv, 1)
                dve.wait_ge(dv, 3)
                dve.scalar_tensor_tensor(v, d, 0.25, d, ALU.mult, ALU.mult).then_inc(dv, 1)
                dve.tensor_scalar(k.mean[:, :], k.mean[:, :], 0.5, None, ALU.mult)
                dve.tensor_scalar(m2, m2, 1.0 / D, EPS, ALU.mult, ALU.add).then_inc(dv, 1)
                dve.wait_ge(dv, 5)
                dve.tensor_tensor(v, v, m2, ALU.add).then_inc(pw, 1)

            @block.gpsimd
            def _(pool):
                clear_stale(k, pool, (dv, pw))
                pool.wait_ge(pw, 1)
                pool.tensor_tensor(k.rstd[:, :], v, k.half[:, :], ALU.pow)



class Norm:

    def __init__(self, k, sem, name):
        self.k = k
        self.taken, self.chain, self.var, self.done = (sem(name + n) for n in ("_st", "_ch", "_var", "_rstd"))

    def statistics(self, dve, n, at=None):
        at = self.k.xt(n) if at is None else at
        dve.bn_stats(self.k.stats[:, bass.ds(n, 1), :], at).then_inc(self.taken, 1)

    def moments(self, dve, b):
        k, ch = self.k, self.chain
        tiles = bass.ds(b * TPB, TPB)
        me, ve, mo, vo = (k.stats[:, tiles, j] for j in (1, 2, 4, 5))
        d, m2, v = (k.lnt[:, j, tiles] for j in range(3))
        mean = k.mean[:, tiles]
        dve.wait_ge(self.taken, (b + 1) * TPB)
        dve.tensor_tensor(d, me, mo, ALU.subtract).then_inc(ch, 1)
        dve.tensor_tensor(m2, ve, vo, ALU.add).then_inc(ch, 1)
        dve.tensor_tensor(mean, me, mo, ALU.add).then_inc(ch, 1)
        dve.wait_ge(ch, 5 * b + 3)
        dve.scalar_tensor_tensor(v, d, 0.25, d, ALU.mult, ALU.mult).then_inc(ch, 1)
        dve.tensor_scalar(mean, mean, 0.5, None, ALU.mult)
        dve.tensor_scalar(m2, m2, 1.0 / D, EPS, ALU.mult, ALU.add).then_inc(ch, 1)
        dve.wait_ge(ch, 5 * b + 5)
        dve.tensor_tensor(v, v, m2, ALU.add).then_inc(self.var, 1)

    def root(self, pool, b):
        k, tiles = self.k, bass.ds(b * TPB, TPB)
        pool.wait_ge(self.var, b + 1)
        pool.tensor_tensor(k.rstd[:, tiles], k.lnt[:, 2, tiles], k.half[:, tiles], ALU.pow).then_inc(self.done, 1)


class Arrival:

    EARLY = 2

    def __init__(self, k, sb, sem, nm):
        self.k = k
        self.got = [[sb(f"{nm}g{j}_{r}", [P, D]) for r in range(RING)] for j in range(TOPK)]
        self.before = 32 * (NT // RING) * k.gathers
        self.scaled, self.part, self.whole = (sem(nm + c) for c in ("scaled", "part", "whole"))
        self.norm = Norm(k, sem, nm + "in")
        k.gathers += 1

    def fetch(self, pool, b):
        for t in range(TPB):
            n = b * TPB + t
            wait_pos(pool, self.whole, n - RING + 1)
            for j in range(TOPK):
                pool.indirect_dma_start(
                    out=self.got[j][t][:, :], out_offset=None, in_=self.k.ys[:, :],
                    in_offset=bass.IndirectOffsetOnAxis(ap=self.k.pos[j][:, n:n + 1], axis=0)
                ).then_inc(self.k.g_in[t], 16)

    def add(self, dve, b):
        k = self.k
        for t in range(TPB):
            n = b * TPB + t
            dve.wait_ge(k.g_in[t], b * 32 + (32 + self.before))
            for j, added in enumerate((self.part, self.whole)):
                dve.scalar_tensor_tensor(k.xt(n), self.got[j][t][:, :], k.wt[j][:, n:n + 1], k.xt(n),
                                         ALU.mult, ALU.add).then_inc(added, 1)
                dve.wait_ge(added, n + 1)

    def add_later(self, pool, b):
        k = self.k
        for t in range(TPB):
            n = b * TPB + t
            pool.wait_ge(k.g_in[t], b * 32 + (32 + self.before))
            for j in range(TOPK):
                got = self.got[j][t][:, :]
                pool.tensor_scalar(got, got, k.wt[j][:, n:n + 1], None, ALU.mult).then_inc(self.scaled, 1)
            for j, added in enumerate((self.part, self.whole)):
                pool.wait_ge(self.scaled, TOPK * (n - self.EARLY * TPB) + j + 1)
                pool.tensor_tensor(k.xt(n), k.xt(n), self.got[j][t][:, :], ALU.add).then_inc(added, 1)
                pool.wait_ge(added, n + 1)

    def statistics(self, dve, b):
        for t in range(TPB):
            n = b * TPB + t
            dve.wait_ge(self.whole, n + 1)
            self.norm.statistics(dve, n)
        self.norm.moments(dve, b)


ATT_LOADS = 8


def load_attention(eng, k, L):
    for c in "qkvo":
        eng.dma_start(k.att_w[c][:, :, :], k.a[f"L{L}_xcond_W{c}"]).then_inc(k.att_in, 16)
    for c, t in zip("qkvo", k.att_b):
        src = k.a[f"L{L}_xcond_b{c}"]
        eng.dma_start(t[:, :], src if c in "qk" else src.partition_broadcast(P)).then_inc(k.att_in, 16)


def attention(nc, k, L):
    ctx, sb, ps, sem = scoped(k)
    a = k.a
    nm = f"a{L}_"
    W = HPC * S
    with ctx:
        w, (bq, bk, bv, bo) = k.att_w, k.att_b
        bqt = sb(nm + "bqt", [P, DC, NB])
        cx = [sb(f"{nm}cx{s}", [P, DC, 2, S]) for s in range(2)]
        z = [sb(f"{nm}z{s}", [P, TPB, D]) for s in range(2)]
        zT = sb(nm + "zT", [P, DC, SEQ])
        qT = [sb(f"{nm}qT{s}", [P, DC, SEQ]) for s in range(2)]
        kb = [sb(f"{nm}kb{s}", [P, H * S]) for s in range(2)]
        va = [sb(f"{nm}va{s}", [P, H // 2, 2, VW]) for s in range(2)]
        pr = [sb(f"{nm}pr{s}", [P, H * S]) for s in range(2)]
        pT = [sb(f"{nm}pT{s}", [P, H // 2, P]) for s in range(2)]
        mx = [sb(f"{nm}mx{s}", [P, HPC]) for s in range(2)]
        rec = [sb(f"{nm}rec{s}", [P, H]) for s in range(2)]
        on = [sb(f"{nm}on{s}", [P, D]) for s in range(2)]
        oT = [sb(f"{nm}oT{s}", [P, DC, P]) for s in range(2)]
        sc_b = [ps(f"{nm}sc{c}", [P, W]) for c in range(2)]
        tr_b = [ps(f"{nm}tr{c}", [P, HPC // 2, P]) for c in range(2)]
        val_b = ps(nm + "val", [P, 512])
        out_b = ps(nm + "out", [P, 512])
        pr0, pr1 = ps(nm + "pr0", [P, 512]), ps(nm + "pr1", [P, 512])

        k.att_loads += ATT_LOADS
        cx_in = [sem(f"{nm}cx_in{s}") for s in range(2)]
        va_zero, va_init, bq_done = sem(nm + "va_zero"), sem(nm + "va_init"), sem(nm + "bq_done")
        z_done, xb_done = sem(nm + "z_done"), sem(nm + "xb_done")
        prep_ps, pr0_read, pr1_read, k_done, v_done = (
            sem(nm + c) for c in ("prep_ps", "pr0_read", "pr1_read", "k_done", "v_done"))
        s_ps, s_read, s_max, s_sub, exp_done = (
            sem(nm + c) for c in ("s_ps", "s_read", "s_max", "s_sub", "exp_done"))
        t_ps, t_evac, o_ps, o_rec, o_norm = (sem(nm + c) for c in ("t_ps", "t_evac", "o_ps", "o_rec", "o_norm"))
        oT_ps, oT_copied, y_ps, x_added = (sem(nm + c) for c in ("oT_ps", "oT_copied", "y_ps", "x_added"))

        arrival = Arrival(k, sb, sem, nm + "ar_") if k.arriving else None
        k.arriving = False
        out_norm = Norm(k, sem, nm + "out")

        FILLS = 6

        with nc.Block() as block:
            @block.sync
            def _(sp):
                def step(b, s, first, last):
                    wait_pos(sp, prep_ps, FILLS * (b - 1))
                    for j in range(2):
                        sp.dma_start(cx[s][:, :, j, :],
                                     a["ctxT"][bass.ds(b, 1)].rearrange("b p c l -> p (b c) l")).then_inc(cx_in[s], 16)
                over_batches(sp, step)

            @block.gpsimd
            def _(pool):
                for s in range(2):
                    pool.memset(va[s][:, :, :, :], 0.0).then_inc(va_zero, 1)
                pool.wait_ge(va_zero, 2)
                for s in range(2):
                    pool.memset(va[s][0:S, :, 0, DK:VW], 1.0).then_inc(va_init, 1)
                    pool.memset(va[s][S:P, :, 1, DK:VW], 1.0).then_inc(va_init, 1)
                pool.wait_ge(k.att_in, 16 * k.att_loads)

                def bias(b):
                    pool.wait_ge(z_done, b + 1)
                    xs = k.x[:, bass.ds(b * (TPB * D), TPB * D)].rearrange("p (t d) -> p t d", t=TPB)
                    pool.tensor_tensor(xs, xs, bo[:, None, :].to_broadcast([P, TPB, D]), ALU.add).then_inc(xb_done, 1)

                if arrival:
                    for b in range(2):
                        arrival.fetch(pool, b)
                        arrival.norm.root(pool, b)
                    for b in range(NB):
                        bias(b)
                        if b + 2 < NB:
                            arrival.fetch(pool, b + 2)
                        if b > 0:
                            out_norm.root(pool, b - 1)
                        if b + 2 < NB:
                            arrival.add_later(pool, b + 2)
                            arrival.norm.root(pool, b + 2)
                else:
                    bias(0)
                    with pool.Fori(1, NB) as b:
                        bias(b)
                        out_norm.root(pool, b - 1)
                out_norm.root(pool, NB - 1)

            @block.tensor
            def _(pe):
                def piece(b, s, t):
                    if t == 0:
                        pe.wait_ge(z_done, b + 1)
                        for c, (bank, done) in enumerate(((pr0, k_done), (pr1, v_done))):
                            wait_pos(pe, done, b)
                            for i in range(TPB):
                                mm = pe.transpose(bank[:, i * P:(i + 1) * P], z[s][:, i, c * P:(c + 1) * P], k.ident)
                            mm.then_inc(prep_ps, 1)
                    elif t == 1:
                        pe.wait_ge(pr0_read, 2 * b + 1)
                        pe.wait_ge(pr1_read, 2 * b + 1)
                        for c, bank in enumerate((pr0, pr1)):
                            for kk in range(DC):
                                mm = pe.matmul(bank[:, :], w["q"][:, kk, c * P:(c + 1) * P], zT[:, kk, :],
                                               start=(kk == 0), stop=(kk == DC - 1))
                            mm.then_inc(prep_ps, 1)
                    else:
                        pe.wait_ge(cx_in[s], 16 * b + (16 if s else 32))
                        pe.wait_ge(pr0_read, 2 * b + 2)
                        for c in range(DC):
                            for kk in range(DC):
                                mm = pe.matmul(pr0[:, c * S:(c + 1) * S], w["k"][:, kk, c * P:(c + 1) * P],
                                               cx[s][:, kk, 0, :], start=(kk == 0), stop=(kk == DC - 1))
                        mm.then_inc(prep_ps, 1)
                        pe.wait_ge(pr1_read, 2 * b + 2)
                        for kk in range(DC):
                            mm = pe.matmul(pr1[:, 0:D], cx[s][:, kk, :, :].rearrange("p j l -> p (j l)"),
                                           w["v"][:, kk, :], start=(kk == 0), stop=(kk == DC - 1))
                        mm.then_inc(prep_ps, 1)

                def scores(n, s, t, c):
                    wait_pos(pe, s_read, 2 * n + c - 1)
                    pe.matmul(sc_b[c][:, :], qT[s][:, c, t * P:(t + 1) * P], kb[s][:, c * W:(c + 1) * W],
                              start=True, stop=True).then_inc(s_ps, 1)

                def project_turn(n, t):
                    pe.wait_ge(o_norm, n + 1)
                    wait_pos(pe, x_added, n)
                    for c in range(DC):
                        mm = pe.transpose(out_b[:, c * P:(c + 1) * P], on[t % 2][:, c * P:(c + 1) * P], k.ident)
                    mm.then_inc(oT_ps, 1)

                def project(n, t):
                    pe.wait_ge(oT_copied, n + 1)
                    for c in range(DC):
                        mm = pe.matmul(out_b[:, D:2 * D], oT[t % 2][:, c, :], w["o"][:, c, :],
                                       start=(c == 0), stop=(c == DC - 1))
                    mm.then_inc(y_ps, 1)

                def step(b, s, first, last):
                    for t in range(TPB):
                        n = b * TPB + t
                        ends, begins = last and t == TPB - 1, first and t == 0
                        nxt = (n + 1, s, t + 1) if t < TPB - 1 else (n + 1, 1 - s, 0)
                        if t < TPB - 1:
                            scores(*nxt, 0)
                        if not begins:
                            project_turn(n - 1, t - 1)
                        for c in range(2):
                            pe.wait_ge(exp_done, 2 * n + c + 1)
                            wait_pos(pe, t_evac, 2 * n + c - 1)
                            for i in range(HPC // 2):
                                at = (c * HPC // 2 + i) * P
                                mm = pe.transpose(tr_b[c][:, i, :], pr[t % 2][:, at:at + P], k.ident)
                            mm.then_inc(t_ps, 1)
                        if t == TPB - 1 and not last:
                            pe.wait_ge(pr1_read, 2 * b + 4)
                            pe.wait_ge(k_done, b + 2)
                            scores(*nxt, 0)
                        if not ends:
                            scores(*nxt, 1)
                        if not begins:
                            project(n - 1, t - 1)
                        pe.wait_ge(t_evac, 2 * n + 2)
                        wait_pos(pe, o_norm, n)
                        if t == 0:
                            pe.wait_ge(v_done, b + 1)
                        for c in range(H // 2):
                            mm = pe.matmul(val_b[:, c * 2 * VW:(c + 1) * 2 * VW], pT[t % 2][:, c, :],
                                           va[s][:, c, :, :].rearrange("p j v -> p (j v)"), start=True, stop=True)
                        mm.then_inc(o_ps, 1)
                        if t < 3 and not last:
                            piece(b + 1, 1 - s, t)

                pe.wait_ge(k.att_in, 16 * k.att_loads)
                for t in range(3):
                    piece(0, 0, t)
                pe.wait_ge(k_done, 1)
                for c in range(2):
                    scores(0, 0, 0, c)
                over_batches(pe, step)
                project_turn(NT - 1, TPB - 1)
                project(NT - 1, TPB - 1)

            @block.scalar
            def _(act):
                def drain(b, s, t):
                    for c, (bank, read) in enumerate(((pr0, pr0_read), (pr1, pr1_read))):
                        act.wait_ge(prep_ps, FILLS * b + 2 * t + c + 1)
                        if t == 0:
                            act.activation(zT[:, c, :], bank[:, :], ACT.Copy).then_inc(read, 1)
                        else:
                            act.activation(qT[s][:, c, :], bank[:, :], ACT.Identity, bias=bqt[:, c, bass.ds(b, 1)],
                                           scale=k.tau[:, bass.ds(b, 1)]).then_inc(read, 1)

                def exponentials(n, t, c):
                    act.wait_ge(s_sub, 2 * n + c + 1)
                    half = pr[t % 2][:, c * W:(c + 1) * W]
                    act.activation(half, half, ACT.Exp).then_inc(exp_done, 1)

                def project_copy(n, t):
                    act.wait_ge(oT_ps, n + 1)
                    act.activation(oT[t % 2][:, :, :], out_b[:, 0:D].rearrange("p (c q) -> p c q", c=DC),
                                   ACT.Copy).then_inc(oT_copied, 1)

                def step(b, s, first, last):
                    for t in range(TPB):
                        n = b * TPB + t
                        if not (first and t == 0):
                            project_copy(n - 1, t - 1)
                        for c in range(2):
                            act.wait_ge(t_ps, 2 * n + c + 1)
                            act.activation(pT[t % 2][:, c * HPC // 2:(c + 1) * HPC // 2, :], tr_b[c][:, :, :],
                                           ACT.Copy).then_inc(t_evac, 1)
                        if not (last and t == TPB - 1):
                            for c in range(2):
                                exponentials(n + 1, t + 1, c)
                        if t < 2 and not last:
                            drain(b + 1, 1 - s, t)

                drain(0, 0, 0)
                k.ahead(act)
                act.wait_ge(bq_done, 1)
                drain(0, 0, 1)
                for c in range(2):
                    exponentials(0, 0, c)
                over_batches(act, step)
                project_copy(NT - 1, TPB - 1)

            @block.vector
            def _(dve):
                def normalise(b, s):
                    if arrival:
                        dve.wait_ge(arrival.norm.done, b + 1)
                    wait_pos(dve, prep_ps, FILLS * (b - 1))
                    for t in range(TPB):
                        n = b * TPB + t
                        v = dve.tensor_scalar(z[s][:, t, :], k.xt(n), k.mean[:, bass.ds(n, 1)],
                                              k.rstd[:, bass.ds(n, 1)], ALU.subtract, ALU.mult)
                    v.then_inc(z_done, 1)

                def drain(b, s):
                    dve.wait_ge(prep_ps, FILLS * b + 5)
                    for c in range(DC):
                        v = dve.scalar_tensor_tensor(
                            kb[s][:, c * W:(c + 1) * W].rearrange("p (h l) -> p h l", h=HPC),
                            pr0[:, None, c * S:(c + 1) * S].to_broadcast([P, HPC, S]), bk[:, c:c + 1],
                            k.cst[:, C_HM:C_HM + HPC, None].to_broadcast([P, HPC, S]), ALU.add, ALU.mult)
                    v.then_inc(k_done, 1)
                    dve.wait_ge(prep_ps, FILLS * b + 6)
                    for j in range(2):
                        h = slice(j * S, (j + 1) * S)
                        v = dve.tensor_tensor(
                            va[s][h, :, j, 0:DK],
                            pr1[h, 0:D].rearrange("p (c j e) -> p c j e", c=H // 2, j=2)[:, :, j, :],
                            bv[h, :].rearrange("p (c j e) -> p c j e", c=H // 2, j=2)[:, :, j, :], ALU.add)
                    v.then_inc(v_done, 1)

                def softmax(n, b, t, c):
                    p3 = pr[t % 2][:, c * W:(c + 1) * W].rearrange("p (h l) -> p h l", h=HPC)
                    dve.wait_ge(s_ps, 2 * n + c + 1)
                    dve.tensor_tensor(p3, sc_b[c][:, :].rearrange("p (h l) -> p h l", h=HPC),
                                      k.delta[:, None, bass.ds(b * S, S)].to_broadcast([P, HPC, S]),
                                      ALU.add).then_inc(s_read, 1)
                    dve.wait_ge(s_read, 2 * n + c + 1)
                    dve.tensor_reduce(mx[c][:, :], p3, AX.X, ALU.max).then_inc(s_max, 1)
                    dve.wait_ge(s_max, 2 * n + c + 1)
                    dve.tensor_tensor(p3, p3, mx[c][:, :, None].to_broadcast([P, HPC, S]),
                                      ALU.subtract).then_inc(s_sub, 1)

                def divide(n, t):
                    o3 = val_b[:, 0:H * VW].rearrange("p (h v) -> p h v", h=H)
                    dve.wait_ge(o_ps, n + 1)
                    dve.reciprocal(rec[t % 2][:, :], o3[:, :, DK]).then_inc(o_rec, 1)
                    dve.wait_ge(o_rec, n + 1)
                    dve.tensor_tensor(on[t % 2][:, :].rearrange("p (h e) -> p h e", h=H), o3[:, :, 0:DK],
                                      rec[t % 2][:, :, None].to_broadcast([P, H, DK]), ALU.mult).then_inc(o_norm, 1)

                def residual(n):
                    dve.wait_ge(y_ps, n + 1)
                    dve.tensor_tensor(k.xt(n), out_b[:, D:2 * D], k.xt(n), ALU.add).then_inc(x_added, 1)

                def statistics(n):
                    dve.wait_ge(x_added, n + 1)
                    out_norm.statistics(dve, n)

                def step(b, s, after):
                    for t in range(TPB):
                        n = b * TPB + t
                        ends, begins = t == TPB - 1 and not after(1), t == 0 and is_first(b)
                        nxt = (n + 1, b, t + 1) if t < TPB - 1 else (n + 1, b + 1, 0)
                        if not ends:
                            softmax(*nxt, 0)
                        if t == 0 and after(1):
                            normalise(b + 1, 1 - s)
                        if not ends:
                            softmax(*nxt, 1)
                        if not begins:
                            if t == 1:
                                dve.wait_ge(xb_done, b + 1)
                            residual(n - 1)
                        divide(n, t)
                        if not begins:
                            statistics(n - 1)
                        if t == 2 and after(1):
                            drain(b + 1, 1 - s)
                        if arrival and t == TPB - 1 and after(2):
                            arrival.statistics(dve, b + 2)
                        if t == 1 and not is_first(b):
                            out_norm.moments(dve, b - 1)

                dve.wait_ge(k.att_in, 16 * k.att_loads)
                for c in range(DC):
                    v = dve.tensor_scalar(bqt[:, c, :], k.tau[:, :], bq[:, c:c + 1], None, ALU.mult)
                v.then_inc(bq_done, 1)
                dve.wait_ge(va_init, 4)
                if arrival:
                    for b in range(2):
                        arrival.add(dve, b)
                        arrival.statistics(dve, b)
                normalise(0, 0)
                drain(0, 0)
                for c in range(2):
                    softmax(0, 0, 0, c)
                over_batches_ahead(dve, step)
                residual(NT - 1)
                statistics(NT - 1)
                out_norm.moments(dve, NB - 1)


def dispatch(nc, k, L):
    ctx, sb, ps, sem = scoped(k)
    nm = f"r{L}_"
    with ctx:
        gate = sb(nm + "gate", [P, DC, E])
        z = [sb(f"{nm}z{s}", [P, TPB * D]) for s in range(2)]
        if L:
            zk = [sb(f"{nm}zk{s}", [P, TPB * D]) for s in range(2)]
        else:
            zk = [k.z[:, b * (TPB * D):(b + 1) * (TPB * D)] for b in range(NB)]
        zT = sb(nm + "zT", [P, DC, SEQ])
        t3 = lambda n: sb(nm + n, [P, TPB, E])
        t2 = lambda n: sb(nm + n, [P, TPB])
        lgt, eq, cand, rest, place, prod = (t3(n) for n in ("lgt", "eq", "cand", "rest", "place", "prod"))
        hot = [sb(f"{nm}hot{j}", [P, NT, E]) for j in range(TOPK)]
        pf = [sb(f"{nm}pf{j}", [P, NT]) for j in range(TOPK)]
        sent_to = [sb(f"{nm}to{j}", [P, NT], U32) for j in range(TOPK)]
        shift, moved = sb(nm + "shift", [P, E]), sb(nm + "moved", [P, NT, E])
        chosen, before = ([t3(f"{n}{s}") for s in range(2)] for n in ("chosen", "before"))
        code = t2("code")
        top = [sb(f"{nm}top{j}", [P, NT]) for j in range(TOPK)]
        gap, den = sb(nm + "gap", [P, NT]), sb(nm + "den", [P, NT])
        pad, zero = sb(nm + "pad", [P, E], U32), sb(nm + "zero", [P, D])
        cnt = [sb(f"{nm}cnt{j}", [P, E]) for j in range(4)]
        base = sb(nm + "base", [1, E])
        tile2 = sb(nm + "tiles", [1, NTILES])
        bank = [ps(f"{nm}b{s}", [P, DC, SEQ]) for s in range(2)]
        lg = [ps(f"{nm}lg{s}", [P, 512]) for s in range(2)]
        pp = [ps(f"{nm}pp{s}", [P, 512]) for s in range(2)]
        (w_in, z_done, zT_ps, zT_copied, lg_ps, lg_read, v, chosen_done, place_ps, pos_done, gap_done, gap_exp,
         cnt_ps, pad_done, zero_set, z_kept) = (
            sem(nm + c) for c in ("w_in", "z_done", "zT_ps", "zT_copied", "lg_ps", "lg_read", "v", "chosen",
                                  "place_ps", "pos", "gap", "gap_exp", "cnt_ps", "pad", "zero_set", "z_kept"))
        sent = 16 * NT * k.mixtures
        padded = 16 * E * k.mixtures
        bc = lambda t: t.to_broadcast([P, TPB, E])
        code_e = bc(k.cst[:, None, C_E:C_E + E])
        region = bc(k.cst[:, None, C_REGION:C_REGION + E])
        with nc.Block() as block:
            @block.sync
            def _(sp):
                sp.dma_start(gate[:, :, :], k.a[f"L{L}_gate"]).then_inc(w_in, 16)
                k.late(sp)

            @block.tensor
            def _(pe):
                def turn(b, s):
                    pe.wait_ge(z_done, b + 1)
                    wait_pos(pe, zT_copied, b - 1)
                    for c in range(DC):
                        for t in range(TPB):
                            at = z[s][:, t * D + c * P:t * D + (c + 1) * P]
                            mm = pe.transpose(bank[s][:, c, t * P:(t + 1) * P], at, k.ident)
                    mm.then_inc(zT_ps, 1)

                def logits(b, s):
                    pe.wait_ge(zT_copied, b + 1)
                    wait_pos(pe, lg_read, b - 1)
                    for t in range(TPB):
                        for c in range(DC):
                            mm = pe.matmul(lg[s][:, t * E:(t + 1) * E], zT[:, c, t * P:(t + 1) * P],
                                           gate[:, c, :], start=(c == 0), stop=(c == DC - 1))
                    mm.then_inc(lg_ps, 1)

                def step(b, s, after):
                    pe.wait_ge(chosen_done, b + 1)
                    flat = lambda t: t[:, :, :].rearrange("p t e -> p (t e)")
                    pe.matmul(pp[s][:, 0:TPB * E], k.cst[:, C_TRI:C_TRI + P], flat(chosen[s]), start=True, stop=False)
                    pe.matmul(pp[s][:, 0:TPB * E], k.cst[:, C_ONE:C_ONE + P], flat(before[s]),
                              start=False, stop=True).then_inc(place_ps, 1)
                    if after(2):
                        turn(b + 2, s)
                        logits(b + 2, s)

                pe.wait_ge(w_in, 16)
                for b in range(2):
                    turn(b, b)
                    logits(b, b)
                over_batches_ahead(pe, step)
                pe.wait_ge(v, ROUTE_STEPS * NB + 1)
                pe.matmul(pp[0][:, 0:E], k.cst[:, C_ONE:C_ONE + P], cnt[3][:, :],
                          start=True, stop=True).then_inc(cnt_ps, 1)

            @block.scalar
            def _(act):
                def step(b, s, first, last):
                    act.wait_ge(zT_ps, b + 1)
                    wait_pos(act, lg_ps, b)
                    act.activation(zT[:, :, :], bank[s][:, :, :], ACT.Copy).then_inc(zT_copied, 1)
                    if L and (not isinstance(b, int) or b >= 2):
                        act.wait_ge(k.scattered[s], b * (8 * SCATTERS) + (sent - 8 * SCATTERS * s))
                    kept = zk[s][:, :] if L else k.z[:, bass.ds(b * (TPB * D), TPB * D)]
                    act.activation(kept, z[s][:, :], ACT.Copy).then_inc(z_kept, 1)
                over_batches(act, step)
                act.wait_ge(gap_done, 1)
                act.activation(k.wt[1][:, :], gap[:, :], ACT.Exp).then_inc(gap_exp, 1)

            @block.vector
            def _(dve):
                def normalise(b, s):
                    wait_pos(dve, z_kept, b - 1)
                    wait_pos(dve, zT_ps, b - 1)
                    for t in range(TPB):
                        n = b * TPB + t
                        o = dve.tensor_scalar(z[s][:, t * D:(t + 1) * D], k.xt(n), k.mean[:, bass.ds(n, 1)],
                                              k.rstd[:, bass.ds(n, 1)], ALU.subtract, ALU.mult)
                    o.then_inc(z_done, 1)

                def then(n, op):
                    op.then_inc(v, 1)
                    dve.wait_ge(v, n + 1)
                    return n + 1

                def route(b, s, first):
                    n = b * ROUTE_STEPS
                    tiles = bass.ds(b * TPB, TPB)
                    dve.wait_ge(lg_ps, b + 1)
                    dve.tensor_copy(lgt[:, :, :], lg[s][:, 0:TPB * E].rearrange("p (t e) -> p t e", t=TPB)
                                    ).then_inc(lg_read, 1)
                    dve.wait_ge(lg_read, b + 1)
                    src = lgt
                    for j in range(TOPK):
                        largest = top[j][:, tiles]
                        n = then(n, dve.tensor_reduce(largest, src[:, :, :], AX.X, ALU.max))
                        n = then(n, dve.tensor_tensor(eq[:, :, :], src[:, :, :], bc(largest[:, :, None]), ALU.is_equal))
                        n = then(n, dve.tensor_tensor(cand[:, :, :], eq[:, :, :], code_e, ALU.mult))
                        n = then(n, dve.tensor_reduce(code[:, :], cand[:, :, :], AX.X, ALU.max))
                        n = then(n, dve.tensor_tensor(hot[j][:, tiles, :], cand[:, :, :], bc(code[:, :, None]), ALU.is_equal))
                        if j == 0:
                            n = then(n, dve.scalar_tensor_tensor(rest[:, :, :], hot[0][:, tiles, :], -3e38, src[:, :, :],
                                                                 ALU.mult, ALU.add))
                            src = rest
                    n = then(n, dve.tensor_tensor(chosen[s][:, :, :], hot[0][:, tiles, :], hot[1][:, tiles, :], ALU.add))
                    if first:
                        n = then(n, dve.tensor_scalar(before[s][:, 0, :], chosen[s][:, 0, :], 0.0, None, ALU.mult))
                    else:
                        n = then(n, dve.tensor_tensor(before[s][:, 0, :], before[1 - s][:, TPB - 1, :],
                                                      chosen[1 - s][:, TPB - 1, :], ALU.add))
                    for t in range(1, TPB):
                        o = dve.tensor_tensor(before[s][:, t, :], before[s][:, t - 1, :], chosen[s][:, t - 1, :], ALU.add)
                        if t < TPB - 1:
                            n = then(n, o)
                    o.then_inc(chosen_done, 1)
                    dve.wait_ge(place_ps, b + 1)
                    n = then(n, dve.tensor_tensor(place[:, :, :], pp[s][:, 0:TPB * E].rearrange("p (t e) -> p t e", t=TPB),
                                                  region, ALU.add))
                    for j in range(TOPK):
                        n = then(n, dve.tensor_tensor(prod[:, :, :], place[:, :, :], hot[j][:, tiles, :], ALU.mult))
                        n = then(n, dve.tensor_reduce(pf[j][:, tiles], prod[:, :, :], AX.X, ALU.add))
                        o = dve.tensor_copy(sent_to[j][:, tiles], pf[j][:, tiles])
                        if j == 0:
                            n = then(n, o)
                    o.then_inc(pos_done, 1)
                    dve.wait_ge(pos_done, b + 1)
                    if isinstance(b, int):
                        assert n == (b + 1) * ROUTE_STEPS, n

                normalise(0, 0)
                normalise(1, 1)

                def ahead_step(b, s, after):
                    route(b, s, is_first(b))
                    if after(2):
                        normalise(b + 2, s)
                over_batches_ahead(dve, ahead_step)

                n = NB * ROUTE_STEPS
                last = (NB - 1) % 2
                n = then(n, dve.tensor_tensor(cnt[3][:, :], before[last][:, TPB - 1, :], chosen[last][:, TPB - 1, :], ALU.add))
                dve.tensor_tensor(gap[:, :], top[1][:, :], top[0][:, :], ALU.subtract).then_inc(gap_done, 1)
                dve.wait_ge(cnt_ps, 1)
                total = cnt[3]
                n = then(n, dve.tensor_copy(total[:, :], pp[0][:, 0:E]))
                n = then(n, dve.tensor_tensor(cnt[0][:, :], total[:, :], k.cst[:, C_REGION:C_REGION + E], ALU.add))
                dve.tensor_scalar(pad[:, :], cnt[0][:, :], k.cst[:, C_PART:C_PART + 1], None, ALU.add).then_inc(pad_done, 1)
                dve.wait_ge(pad_done, 1)
                n = then(n, dve.tensor_scalar(total[:, :], total[:, :], P - 1.0, 1.0 / P, ALU.add, ALU.mult))
                n = then(n, dve.tensor_scalar(total[:, :], total[:, :], -(0.5 - 0.5 / P), MAGIC, ALU.add, ALU.add))
                n = then(n, dve.tensor_scalar(total[:, :], total[:, :], MAGIC, None, ALU.subtract))
                n = then(n, dve.tensor_copy(cnt[1][:, :], total[:, :]))
                c = 1
                for sh in (1, 2, 4):
                    a, b = cnt[c], cnt[3 - c]
                    dve.tensor_copy(b[:, 0:sh], a[:, 0:sh])
                    n = then(n, dve.tensor_tensor(b[:, sh:E], a[:, sh:E], a[:, 0:E - sh], ALU.add))
                    c = 3 - c
                end, start = cnt[c], cnt[3 - c]
                n = then(n, dve.tensor_tensor(start[:, :], end[:, :], total[:, :], ALU.subtract))
                wide = lambda t: t.to_broadcast([1, NTILES, E])
                j_col = wide(k.cst[0:1, C_J:C_J + NTILES, None])
                member, ended = (t[0:1, 0:NTILES * E].rearrange("p (j e) -> p j e", j=NTILES) for t in z)
                dve.wait_ge(zT_ps, NB)
                dve.wait_ge(z_kept, NB)
                n = then(n, dve.tensor_tensor(member[:, :, :], j_col, wide(start[0:1, None, :]), ALU.is_ge))
                n = then(n, dve.tensor_tensor(ended[:, :, :], j_col, wide(end[0:1, None, :]), ALU.is_ge))
                n = then(n, dve.tensor_tensor(member[:, :, :], member[:, :, :], ended[:, :, :], ALU.subtract))
                n = then(n, dve.tensor_reduce(tile2[:, :], ended[:, :, :], AX.X, ALU.add))
                n = then(n, dve.tensor_scalar(k.owner[:, :], tile2[:, :], E - 1.0, None, ALU.min))
                n = then(n, dve.scalar_tensor_tensor(base[:, :], start[0:1, :], -float(P),
                                                     k.cst[0:1, C_REGION:C_REGION + E], ALU.mult, ALU.add))
                n = then(n, dve.tensor_scalar(base[:, :], base[:, :], float(E * CAP), None, ALU.subtract))
                n = then(n, dve.scalar_tensor_tensor(ended[:, :, :], j_col, float(P), wide(base[0:1, None, :]),
                                                     ALU.mult, ALU.add))
                n = then(n, dve.tensor_tensor(ended[:, :, :], ended[:, :, :], member[:, :, :], ALU.mult))
                n = then(n, dve.tensor_reduce(tile2[:, :], ended[:, :, :], AX.X, ALU.add))
                n = then(n, dve.tensor_scalar(k.rows[:, :], tile2[:, :], float(E * CAP), None, ALU.add))
                dve.wait_ge(gap_exp, 1)
                n = then(n, dve.scalar_tensor_tensor(shift[:, :], start[:, :], float(P),
                                                     k.cst[:, C_REGION:C_REGION + E], ALU.mult, ALU.subtract))
                for j in range(TOPK):
                    n = then(n, dve.tensor_tensor(moved[:, :, :], hot[j][:, :, :],
                                                  shift[:, None, :].to_broadcast([P, NT, E]), ALU.mult))
                    n = then(n, dve.tensor_reduce(gap[:, :], moved[:, :, :], AX.X, ALU.add))
                    n = then(n, dve.tensor_tensor(k.pos[j][:, :], pf[j][:, :], gap[:, :], ALU.add))
                n = then(n, dve.tensor_scalar(den[:, :], k.wt[1][:, :], 1.0, None, ALU.add))
                n = then(n, dve.reciprocal(k.wt[0][:, :], den[:, :]))
                n = then(n, dve.tensor_tensor(k.wt[1][:, :], k.wt[1][:, :], k.wt[0][:, :], ALU.mult))

            @block.gpsimd
            def _(pool):
                pool.memset(zero[:, :], 0.0).then_inc(zero_set, 1)
                for b in range(NB):
                    pool.wait_ge(pos_done, b + 1)
                    pool.wait_ge(z_kept, b + 1)
                    for t in range(TPB):
                        n = b * TPB + t
                        for j in range(TOPK):
                            pool.indirect_dma_start(
                                out=k.xs[:, :], out_offset=bass.IndirectOffsetOnAxis(ap=sent_to[j][:, n:n + 1], axis=0),
                                in_=zk[b % len(zk)][:, t * D:(t + 1) * D], in_offset=None).then_inc(k.scattered[b % 2], 16)
                pool.wait_ge(zero_set, 1)
                pool.wait_ge(pad_done, 1)
                for e in range(E):
                    pool.indirect_dma_start(
                        out=k.xs[:, :], out_offset=bass.IndirectOffsetOnAxis(ap=pad[:, e:e + 1], axis=0),
                        in_=zero[:, :], in_offset=None).then_inc(k.padded, 16)
                for s in range(2):
                    pool.wait_ge(k.scattered[s], sent + 16 * NT)
                pool.wait_ge(k.padded, padded + 16 * E)


ROUTE_STEPS = 21
SCATTERS = TOPK * TPB


def over_tiles(eng, step, ahead):
    loop = (NTILES - ahead) // 2
    step(0, 0, True, lambda d: True)
    step(1, 1, True, lambda d: True)
    with eng.Fori(1, loop) as i:
        step(i * 2, 0, False, lambda d: True)
        step(i * 2 + 1, 1, False, lambda d: True)
    for j in range(2 * loop, NTILES):
        step(j, j % 2, False, lambda d, j=j: j + d < NTILES)


def load_second_layers(sp, k, L):
    n2 = (F0 if L == 0 else F2) // P * D
    for e in range(E):
        sp.dma_start(k.w2[:, e * n2:(e + 1) * n2], k.a[f"L{L}_ffn_w2"][:, e, :]).then_inc(k.w_in, 16)


def load_first_layers(sp, k, L, es):
    n1 = DC * (F0 if L == 0 else F2)
    for e in es:
        sp.dma_start(k.w1[:, e * n1:(e + 1) * n1], k.a[f"L{L}_ffn_w1"][:, e, :]).then_inc(k.w_in, 16)


def experts(nc, k, L):
    ctx, sb, ps, sem = scoped(k)
    a = k.a
    nm = f"e{L}_"
    F = F0 if L == 0 else F2
    FC = F // P
    norm = L == 0
    A = 2 if norm else 1
    with ctx:
        w1, w2 = k.w1, k.w2
        b2 = sb(nm + "b2", [P, E * D])
        bt = sb(nm + "bt", [P, E * FC])
        if norm:
            b1 = sb(nm + "b1", [P, E * F])
            gt = sb(nm + "gt", [P, E * FC])
            post_b = sb(nm + "post_b", [P, D])
            st = [sb(f"{nm}st{s}", [P, 6]) for s in range(2)]
            mv = [sb(f"{nm}mv{s}", [P, 2]) for s in range(2)]
            ve = [sb(f"{nm}ve{s}", [P, 1]) for s in range(2)]
            rs = [sb(f"{nm}rs{s}", [P, 1]) for s in range(2)]
        xin = [sb(f"{nm}x{s}", [P, D]) for s in range(2)]
        xT = [sb(f"{nm}xT{s}", [P, DC, P]) for s in range(2)]
        h = [sb(f"{nm}h{s}", [P, F]) for s in range(A)]
        h = [h[0], h[A - 1]]
        hT = [sb(f"{nm}hT{s}", [P, FC, P]) for s in range(2)]
        y = [sb(f"{nm}y{s}", [P, D]) for s in range(2)]
        xT_b = ps(nm + "pxT", [P, 512])
        h_b = [ps(f"{nm}ph{s}", [P, F]) for s in range(2)]
        hT_b = ps(nm + "phT", [P, FC, P])
        y_b = ps(nm + "py", [P, 512])
        c_in = sem(nm + "c_in")
        x_in = [sem(f"{nm}x_in{s}") for s in range(2)]
        y_out = [sem(f"{nm}y_out{s}") for s in range(2)]
        xT_ps, xT_copied, h_ps, h_read, h_ready, hT_ps, gelu_done, y_ps, y_done = (
            sem(nm + c) for c in ("xT_ps", "xT_copied", "h_ps", "h_read", "h_ready", "hT_ps", "gelu_done",
                                  "y_ps", "y_done"))
        aggr, var, rsq = (sem(nm + c) for c in ("aggr", "var", "rsq"))
        if not norm:
            h_read = h_ready
        with nc.Block() as block:
            @block.sync
            def _(sp):
                sp.dma_start(b2[:, :], a[f"L{L}_ffn_b2"].partition_broadcast(P)).then_inc(c_in, 16)
                sp.dma_start(bt[:, :], a[f"L{L}_ffn_bt"]).then_inc(c_in, 16)
                if norm:
                    sp.dma_start(b1[:, :], a[f"L{L}_ffn_b1"].partition_broadcast(P)).then_inc(c_in, 16)
                    sp.dma_start(gt[:, :], a[f"L{L}_ffn_gt"]).then_inc(c_in, 16)
                    sp.dma_start(post_b[:, :], a["L0_ffn_ln_b"].partition_broadcast(P)).then_inc(c_in, 16)
                if k.next_att is not None:
                    load_attention(sp, k, k.next_att)

                def step(j, s, first, more):
                    wait_pos(sp, xT_ps, j - 1)
                    row = sp.value_load(k.rows[0:1, bass.ds(j, 1)], min_val=0, max_val=E * CAP)
                    sp.dma_start(xin[s][:, :], k.xs[bass.ds(row, P), :]).then_inc(x_in[s], 16)
                over_tiles(sp, step, 0)
                for s in range(2):
                    sp.wait_ge(y_out[s], 16 * (NTILES // 2))

            @block.tensor
            def _(pe):
                def turn(j, s):
                    pe.wait_ge(x_in[s], 8 * j + (8 if s else 16))
                    wait_pos(pe, xT_copied, j)
                    for c in range(DC):
                        mm = pe.transpose(xT_b[:, c * P:(c + 1) * P], xin[s][:, c * P:(c + 1) * P], k.ident)
                    mm.then_inc(xT_ps, 1)

                def layer1(j, s):
                    e = pe.value_load(k.owner[0:1, bass.ds(j, 1)], min_val=0, max_val=E - 1)
                    pe.wait_ge(xT_copied, j + 1)
                    wait_pos(pe, h_read, j - 1)
                    for c in range(F // 512):
                        for kk in range(DC):
                            mm = pe.matmul(h_b[s][:, c * 512:(c + 1) * 512], xT[s][:, kk, :],
                                           w1[:, bass.ds(e * (DC * F) + (kk * F + c * 512), 512)],
                                           start=(kk == 0), stop=(kk == DC - 1))
                    mm.then_inc(h_ps, 1)

                def step(j, s, first, more):
                    sa = (s + A) % 2
                    if more(A):
                        turn(j + A, sa)
                    pe.wait_ge(h_ready, j + 1)
                    wait_pos(pe, gelu_done, j)
                    for f in range(FC):
                        mm = pe.transpose(hT_b[:, f, :], h[s][:, f * P:(f + 1) * P], k.ident)
                    mm.then_inc(hT_ps, 1)
                    if more(A):
                        layer1(j + A, sa)
                    e = pe.value_load(k.owner[0:1, bass.ds(j, 1)], min_val=0, max_val=E - 1)
                    pe.wait_ge(gelu_done, j + 1)
                    wait_pos(pe, y_done, j)
                    for f in range(FC):
                        mm = pe.matmul(y_b[:, 0:D], hT[s][:, f, :], w2[:, bass.ds(e * (FC * D) + f * D, D)],
                                       start=(f == 0), stop=(f == FC - 1))
                    mm.then_inc(y_ps, 1)

                pe.wait_ge(k.w_in, k.w_count)
                for j in range(A):
                    turn(j, j)
                    layer1(j, j)
                over_tiles(pe, step, A)

            @block.scalar
            def _(act):
                def copy(j, s):
                    act.wait_ge(xT_ps, j + 1)
                    act.activation(xT[s][:, :, :], xT_b[:, 0:D].rearrange("p (c q) -> p c q", c=DC),
                                   ACT.Copy).then_inc(xT_copied, 1)

                def store(j, s):
                    act.wait_ge(y_done, j + 1)
                    act.dma_start(k.ys[bass.ds(j * P, P), :], y[s][:, :]).then_inc(y_out[s], 16)

                def step(j, s, first, more):
                    if more(A):
                        copy(j + A, (s + A) % 2)
                    e = act.value_load(k.owner[0:1, bass.ds(j, 1)], min_val=0, max_val=E - 1)
                    act.wait_ge(hT_ps, j + 1)
                    for f in range(FC):
                        col = bass.ds(e * FC + f, 1)
                        g = act.activation(hT[s][:, f, :], hT_b[:, f, :], ACT.Gelu, bias=bt[:, col],
                                           scale=gt[:, col] if norm else 1.0)
                    g.then_inc(gelu_done, 1)
                    if not (isinstance(j, int) and j == 0):
                        store(j - 1, 1 - s)

                act.wait_ge(c_in, 80 if norm else 32)
                for j in range(A):
                    copy(j, j)
                over_tiles(act, step, A)
                store(NTILES - 1, 1)

            @block.vector
            def _(dve):
                def hidden(j, s):
                    if not norm:
                        dve.wait_ge(h_ps, j + 1)
                        dve.tensor_copy(h[s][:, :], h_b[s][:, :]).then_inc(h_ready, 1)
                        return
                    e = dve.value_load(k.owner[0:1, bass.ds(j, 1)], min_val=0, max_val=E - 1)
                    dve.wait_ge(h_ps, j + 1)
                    dve.tensor_tensor(h[s][:, :], h_b[s][:, :], b1[:, bass.ds(e * F, F)], ALU.add).then_inc(h_read, 1)
                    dve.wait_ge(h_read, j + 1)
                    dve.bn_stats(st[s][:, :], h[s][:, :])
                    dve.drain()
                    dve.bn_aggr(mv[s][:, :], st[s][:, :]).then_inc(aggr, 1)
                    dve.wait_ge(aggr, j + 1)
                    dve.tensor_scalar(ve[s][:, :], mv[s][:, 1:2], EPS, None, ALU.add).then_inc(var, 1)

                def centre(j, s):
                    dve.wait_ge(rsq, j + 1)
                    dve.tensor_scalar(h[s][:, :], h[s][:, :], mv[s][:, 0:1], rs[s][:, :],
                                      ALU.subtract, ALU.mult).then_inc(h_ready, 1)

                def step(j, s, first, more):
                    if more(A):
                        hidden(j + A, (s + A) % 2)
                    e = dve.value_load(k.owner[0:1, bass.ds(j, 1)], min_val=0, max_val=E - 1)
                    dve.wait_ge(y_ps, j + 1)
                    if not first:
                        wait_pos(dve, y_out[s], 8 * j - (8 if s else 0))
                    dve.tensor_tensor(y[s][:, :], y_b[:, 0:D], b2[:, bass.ds(e * D, D)], ALU.add).then_inc(y_done, 1)
                    if norm and more(A):
                        centre(j + A, (s + A) % 2)

                dve.wait_ge(c_in, 80 if norm else 32)
                for j in range(A):
                    hidden(j, j)
                    if norm:
                        centre(j, j)
                over_tiles(dve, step, A)

            if norm:
                @block.gpsimd
                def _(pool):
                    def root(j, s):
                        pool.wait_ge(var, j + 1)
                        pool.tensor_tensor(rs[s][:, :], ve[s][:, :], k.half[:, 0:1], ALU.pow).then_inc(rsq, 1)

                    pool.wait_ge(c_in, 80)
                    with pool.Fori(0, NT // 2) as i:
                        root(i * 2, 0)
                        root(i * 2 + 1, 1)
                        xs = k.x[:, bass.ds(i * (2 * D), 2 * D)].rearrange("p (t d) -> p t d", t=2)
                        pool.tensor_tensor(xs, xs, post_b[:, None, :].to_broadcast([P, 2, D]), ALU.add)
                    with pool.Fori(NT // 2, NTILES // 2) as i:
                        root(i * 2, 0)
                        root(i * 2 + 1, 1)


def experts_gelu(nc, k):
    ctx, sb, ps, sem = scoped(k)
    a = k.a
    nm = "e2_"
    F, FC = F2, F2 // P
    N1 = DC * F
    with ctx:
        b2 = sb(nm + "b2", [P, E * D])
        bt = sb(nm + "bt", [P, E * FC])
        w1 = sb(nm + "w1", [P, DC, F])
        xin = [sb(f"{nm}x{s}", [P, D]) for s in range(2)]
        xT = [sb(f"{nm}xT{s}", [P, DC, P]) for s in range(2)]
        hT = [sb(f"{nm}hT{s}", [P, FC, P]) for s in range(2)]
        y = [sb(f"{nm}y{s}", [P, D]) for s in range(2)]
        xT_b = ps(nm + "pxT", [P, 512])
        h_b = [ps(f"{nm}ph{s}", [P, FC, P]) for s in range(2)]
        y_b = [ps(f"{nm}py{s}", [P, 512]) for s in range(2)]
        c_in = sem(nm + "c_in")
        x_in = [sem(f"{nm}x_in{s}") for s in range(2)]
        y_out = [sem(f"{nm}y_out{s}") for s in range(2)]
        xT_ps, xT_copied, w_copied, h_ps, gelu_done, y_ps, y_done = (
            sem(nm + c) for c in ("xT_ps", "xT_copied", "w_copied", "h_ps", "gelu_done", "y_ps", "y_done"))
        owner = lambda eng, j: eng.value_load(k.owner[0:1, bass.ds(j, 1)], min_val=0, max_val=E - 1)
        with nc.Block() as block:
            @block.sync
            def _(sp):
                sp.dma_start(b2[:, :], a["L2_ffn_b2"].partition_broadcast(P)).then_inc(c_in, 16)
                sp.dma_start(bt[:, :], a["L2_ffn_bt"]).then_inc(c_in, 16)
                if k.next_att is not None:
                    load_attention(sp, k, k.next_att)

                def step(j, s, first, more):
                    wait_pos(sp, xT_ps, j - 1)
                    row = sp.value_load(k.rows[0:1, bass.ds(j, 1)], min_val=0, max_val=E * CAP)
                    sp.dma_start(xin[s][:, :], k.xs[bass.ds(row, P), :]).then_inc(x_in[s], 16)
                over_tiles(sp, step, 0)
                for s in range(2):
                    sp.wait_ge(y_out[s], 16 * (NTILES // 2))

            @block.tensor
            def _(pe):
                def turn(j, s):
                    pe.wait_ge(x_in[s], 8 * j + (8 if s else 16))
                    wait_pos(pe, xT_copied, j)
                    for c in range(DC):
                        mm = pe.transpose(xT_b[:, c * P:(c + 1) * P], xin[s][:, c * P:(c + 1) * P], k.ident)
                    mm.then_inc(xT_ps, 1)

                def layer1(j, s):
                    pe.wait_ge(xT_copied, j + 1)
                    wait_pos(pe, gelu_done, j - 1)
                    pe.wait_ge(w_copied, j + 1)
                    for f in range(FC):
                        for kk in range(DC):
                            mm = pe.matmul(h_b[s][:, f, :], w1[:, kk, f * P:(f + 1) * P], xT[s][:, kk, :],
                                           start=(kk == 0), stop=(kk == DC - 1))
                    mm.then_inc(h_ps, 1)

                def layer2(j, s):
                    e = owner(pe, j)
                    pe.wait_ge(gelu_done, j + 1)
                    wait_pos(pe, y_done, j - 1)
                    for f in range(FC):
                        mm = pe.matmul(y_b[s][:, 0:D], hT[s][:, f, :], k.w2[:, bass.ds(e * (FC * D) + f * D, D)],
                                       start=(f == 0), stop=(f == FC - 1))
                    mm.then_inc(y_ps, 1)

                def step(j, s, first, more):
                    if more(1):
                        layer1(j + 1, 1 - s)
                    if more(2):
                        turn(j + 2, s)
                    layer2(j, s)

                pe.wait_ge(k.w_in, k.w_count)
                turn(0, 0)
                layer1(0, 0)
                turn(1, 1)
                over_tiles(pe, step, 2)

            @block.scalar
            def _(act):
                def copy(j, s):
                    act.wait_ge(xT_ps, j + 1)
                    act.activation(xT[s][:, :, :], xT_b[:, 0:D].rearrange("p (c q) -> p c q", c=DC),
                                   ACT.Copy).then_inc(xT_copied, 1)

                def gelu(j, s):
                    e = owner(act, j)
                    act.wait_ge(h_ps, j + 1)
                    for f in range(FC):
                        g = act.activation(hT[s][:, f, :], h_b[s][:, f, :], ACT.Gelu,
                                           bias=bt[:, bass.ds(e * FC + f, 1)])
                    g.then_inc(gelu_done, 1)

                def store(j, s):
                    act.wait_ge(y_done, j + 1)
                    act.dma_start(k.ys[bass.ds(j * P, P), :], y[s][:, :]).then_inc(y_out[s], 16)

                def step(j, s, first, more):
                    if more(1):
                        gelu(j + 1, 1 - s)
                    if more(2):
                        copy(j + 2, s)
                    if not first or s:
                        store(j - 1, 1 - s)

                act.wait_ge(c_in, 32)
                copy(0, 0)
                gelu(0, 0)
                copy(1, 1)
                over_tiles(act, step, 2)
                store(NTILES - 1, 1)

            @block.vector
            def _(dve):
                def weights(j):
                    e = owner(dve, j)
                    wait_pos(dve, h_ps, j)
                    dve.tensor_copy(w1[:, :, :].rearrange("p c f -> p (c f)"),
                                    k.w1[:, bass.ds(e * N1, N1)]).then_inc(w_copied, 1)

                def step(j, s, first, more):
                    if more(2):
                        weights(j + 2)
                    e = owner(dve, j)
                    dve.wait_ge(y_ps, j + 1)
                    if not first:
                        wait_pos(dve, y_out[s], 8 * j - (8 if s else 0))
                    dve.tensor_tensor(y[s][:, :], y_b[s][:, 0:D], b2[:, bass.ds(e * D, D)], ALU.add).then_inc(y_done, 1)

                dve.wait_ge(c_in, 32)
                dve.wait_ge(k.w_in, k.w_count)
                weights(0)
                weights(1)
                over_tiles(dve, step, 2)


def combine(nc, k):
    ctx, sb, ps, sem = scoped(k)
    nm = "c2_"
    with ctx:
        got = [[sb(f"{nm}g{j}_{r}", [P, D]) for r in range(RING)] for j in range(TOPK)]
        before = 32 * (NT // RING) * k.gathers
        k.gathers += 1
        part, whole = sem(nm + "part"), sem(nm + "whole")
        with nc.Block() as block:
            @block.gpsimd
            def _(pool):
                for n in range(NT):
                    wait_pos(pool, whole, n - RING + 1)
                    for j in range(TOPK):
                        pool.indirect_dma_start(
                            out=got[j][n % RING][:, :], out_offset=None, in_=k.ys[:, :],
                            in_offset=bass.IndirectOffsetOnAxis(ap=k.pos[j][:, n:n + 1], axis=0)
                        ).then_inc(k.g_in[n % RING], 16)

            @block.vector
            def _(dve):
                with dve.Fori(0, NT // RING) as i:
                    for r in range(RING):
                        n = i * RING + r
                        at = k.xt(n)
                        dve.wait_ge(k.g_in[r], i * 32 + (32 + before))
                        dve.scalar_tensor_tensor(at, got[0][r][:, :], k.wt[0][:, bass.ds(n, 1)], at,
                                                 ALU.mult, ALU.add).then_inc(part, 1)
                        dve.wait_ge(part, n + 1)
                        dve.scalar_tensor_tensor(at, got[1][r][:, :], k.wt[1][:, bass.ds(n, 1)], at,
                                                 ALU.mult, ALU.add).then_inc(whole, 1)
                        dve.wait_ge(whole, n + 1)
                        dve.bn_stats(k.stats[:, bass.ds(n, 1), :], at)


def combine_norm(nc, k):
    ctx, sb, ps, sem = scoped(k)
    nm = "c0_"
    with ctx:
        g = sb(nm + "g", [P, D])
        got = [[sb(f"{nm}g{j}_{r}", [P, D]) for r in range(RING)] for j in range(TOPK)]
        before = 32 * (NT // RING) * k.gathers
        k.gathers += 1
        w_in, scaled, part, whole, u_done, m_done, x_done = (sem(nm + c) for c in ("w_in", "scaled", "part", "whole", "u", "m", "x"))
        z_norm, x_norm = Norm(k, sem, nm + "z"), Norm(k, sem, nm + "x")
        span = lambda t, b: t[:, bass.ds(b * (TPB * D), TPB * D)].rearrange("p (t d) -> p t d", t=TPB)
        with nc.Block() as block:
            @block.sync
            def _(sp):
                sp.dma_start(g[:, :], k.a["L0_ffn_ln_g"].partition_broadcast(P)).then_inc(w_in, 16)

            @block.gpsimd
            def _(pool):
                def fetch(b):
                    for t in range(TPB):
                        n = b * TPB + t
                        wait_pos(pool, whole, n - RING + 1)
                        for j in range(TOPK):
                            pool.indirect_dma_start(
                                out=got[j][t][:, :], out_offset=None, in_=k.ys[:, :],
                                in_offset=bass.IndirectOffsetOnAxis(ap=k.pos[j][:, n:n + 1], axis=0)
                            ).then_inc(k.g_in[t], 16)

                def add_first(b):
                    for t in range(TPB):
                        n = b * TPB + t
                        at = k.z[:, n * D:(n + 1) * D]
                        pool.wait_ge(scaled, n + 1)
                        pool.tensor_tensor(at, at, got[0][t][:, :], ALU.add).then_inc(part, 1)

                fetch(0)
                add_first(0)
                for b in range(NB):
                    if b + 1 < NB:
                        fetch(b + 1)
                        add_first(b + 1)
                    z_norm.root(pool, b)
                    if b > 0:
                        x_norm.root(pool, b - 1)
                x_norm.root(pool, NB - 1)

            @block.scalar
            def _(act):
                with act.Fori(0, NB) as b:
                    for t in range(TPB):
                        act.wait_ge(k.g_in[t], b * 32 + (32 + before))
                        act.activation(got[0][t][:, :], got[0][t][:, :], ACT.Copy,
                                       scale=k.wt[0][:, bass.ds(b * TPB + t, 1)]).then_inc(scaled, 1)

            @block.vector
            def _(dve):
                def add(b):
                    tiles = [(b * TPB + t, k.z[:, bass.ds((b * TPB + t) * D, D)]) for t in range(TPB)]
                    for t, (n, at) in enumerate(tiles):
                        dve.wait_ge(part, n + 1)
                        dve.scalar_tensor_tensor(at, got[1][t][:, :], k.wt[1][:, bass.ds(n, 1)], at,
                                                 ALU.mult, ALU.add).then_inc(whole, 1)
                    for n, at in tiles:
                        dve.wait_ge(whole, n + 1)
                        z_norm.statistics(dve, n, at)
                    z_norm.moments(dve, b)

                def normalise(b):
                    dve.wait_ge(z_norm.done, b + 1)
                    for t in range(TPB):
                        n = b * TPB + t
                        at = k.z[:, bass.ds(n * D, D)]
                        v = dve.tensor_scalar(at, at, k.mean[:, bass.ds(n, 1)], k.rstd[:, bass.ds(n, 1)],
                                              ALU.subtract, ALU.mult)
                    v.then_inc(u_done, 1)
                    dve.wait_ge(u_done, b + 1)
                    dve.tensor_tensor(span(k.z, b), span(k.z, b), g[:, None, :].to_broadcast([P, TPB, D]),
                                      ALU.mult).then_inc(m_done, 1)
                    dve.wait_ge(m_done, b + 1)
                    dve.tensor_tensor(span(k.x, b), span(k.x, b), span(k.z, b), ALU.add).then_inc(x_done, 1)
                    dve.wait_ge(x_done, b + 1)
                    for t in range(TPB):
                        x_norm.statistics(dve, b * TPB + t)
                    x_norm.moments(dve, b)

                dve.wait_ge(w_in, 16)
                add(0)
                with dve.Fori(0, NB - 1) as b:
                    add(b + 1)
                    normalise(b)
                normalise(NB - 1)


def mixture(nc, k, L):
    ctx, sb, ps, sem = scoped(k)
    with ctx:
        k.owner, k.rows = (sb(f"x{L}_{n}", [1, NTILES], I32) for n in ("owner", "rows"))
        if L == 0:
            k.z = sb("x0_z", [P, NT * D])
        dispatch(nc, k, L)
        if L == 0:
            experts(nc, k, L)
        else:
            experts_gelu(nc, k)
        k.mixtures += 1
        k.arriving = L == 2 and k.next_att is not None
        if L == 0:
            combine_norm(nc, k)
        elif not k.arriving:
            combine(nc, k)


def load_quantum(eng, k):
    for t, src in zip(k.f1, ("L1_ffn_W1", "L1_ffn_W2", "L1_ffn_par")):
        eng.dma_start(t[:, :, :], k.a[src]).then_inc(k.f1_in, 16)
    eng.dma_start(k.f1[3][:, :], k.a["L1_ffn_b2"].partition_broadcast(P)).then_inc(k.f1_in, 16)


def load_window(eng, k):
    wa, wc, pt, ln = k.win
    for t, src in ((wa, "L2_Wa"), (wc, "L2_Wc")):
        eng.dma_start(t[:, :, :], k.a[src]).then_inc(k.win_in, 16)
    for t, src in ((pt, "pt"), (ln, "len")):
        eng.dma_start(t[:, :], k.a[src].partition_broadcast(P)).then_inc(k.win_in, 16)


def load_ternary(eng, k):
    for t, c in zip(k.f3_raw, ("gate", "up", "down")):
        eng.dma_start(t[:, :], k.a[f"L3_ffn_w_{c}"]).then_inc(k.f3_in, 16)


def quantum_ffn(nc, k):
    ctx, sb, ps, sem = scoped(k)
    nm = "f1_"
    a = k.a
    HS = 4
    FC = F1 // P
    with ctx:
        w1, w2, par, b2 = k.f1
        turn_t, half_t, cs, c_ = (sb(nm + n, [P, 2, FC]) for n in ("turn", "near", "cs", "c"))
        z = [sb(f"{nm}z{s}", [P, TPB, D]) for s in range(2)]
        zT = [sb(f"{nm}zT{s}", [P, DC, SEQ]) for s in range(2)]
        u = [sb(f"{nm}u{s}", [P, SEQ]) for s in range(HS)]
        near = [sb(f"{nm}near{s}", [P, SEQ]) for s in range(2)]
        q = [sb(f"{nm}q{s}", [P, FC, SEQ]) for s in range(2)]
        bank = ps(nm + "bank", [P, DC, SEQ])
        hb = [ps(f"{nm}h{i}", [P, SEQ]) for i in range(HS)]
        yb = [ps(f"{nm}y{s}", [P, 512]) for s in range(2)]
        norm = Norm(k, sem, nm + "out")
        w_in, v, sc = k.f1_in, sem(nm + "v"), sem(nm + "sc")
        z_done, b_done, zT_ps, zT_copied, h_ps, u_done, near_done, frac, sine, mixed, q_done, y_ps, x_added = (
            sem(nm + n) for n in ("z", "b", "zT_ps", "zT_copied", "h_ps", "u", "near", "frac", "sine",
                                  "mixed", "q", "y_ps", "x"))
        with nc.Block() as block:
            @block.gpsimd
            def _(pool):
                pool.wait_ge(w_in, 64)

                def bias(b):
                    pool.wait_ge(z_done, b + 1)
                    xs = k.x[:, bass.ds(b * (TPB * D), TPB * D)].rearrange("p (t d) -> p t d", t=TPB)
                    pool.tensor_tensor(xs, xs, b2[:, None, :].to_broadcast([P, TPB, D]), ALU.add).then_inc(b_done, 1)

                bias(0)
                with pool.Fori(1, NB) as b:
                    bias(b)
                    norm.root(pool, b - 1)
                norm.root(pool, NB - 1)

            @block.vector
            def _(dve):
                dve.wait_ge(w_in, 64)
                b1, th, wr, wi = (par[:, j, :] for j in range(4))
                tn, tc = turn_t[:, 0, :], turn_t[:, 1, :]
                n = [0]

                def then(op):
                    n[0] += 1
                    op.then_inc(v, 1)
                    dve.wait_ge(v, n[0])

                parts, rest = [], TWO_PI
                for _i in range(2):
                    hi = float(np.float32(np.round(rest * 2 ** (9 + 11 * _i)) / 2 ** (9 + 11 * _i)))
                    parts.append(hi)
                    rest -= hi
                parts.append(float(np.float32(rest)))
                kt = half_t[:, 0, :]
                then(dve.tensor_scalar(kt, th, 1.0 / TWO_PI, MAGIC, ALU.mult, ALU.add))
                then(dve.tensor_scalar(kt, kt, MAGIC, None, ALU.subtract))
                red = half_t[:, 1, :]
                then(dve.scalar_tensor_tensor(red, kt, -parts[0], th, ALU.mult, ALU.add))
                then(dve.scalar_tensor_tensor(red, kt, -parts[1], red, ALU.mult, ALU.add))
                then(dve.scalar_tensor_tensor(red, kt, -parts[2], red, ALU.mult, ALU.add))
                then(dve.tensor_scalar(tn, red, 1.0 / TWO_PI, None, ALU.mult))
                then(dve.tensor_scalar(tc, tn, 0.25, None, ALU.add))
                for j in range(2):
                    then(dve.tensor_scalar(half_t[:, j, :], turn_t[:, j, :], MAGIC, None, ALU.add))
                    then(dve.tensor_scalar(half_t[:, j, :], half_t[:, j, :], MAGIC, None, ALU.subtract))
                    then(dve.tensor_tensor(half_t[:, j, :], turn_t[:, j, :], half_t[:, j, :], ALU.subtract))
                dve.wait_ge(sc, 1)
                then(dve.tensor_tensor(c_[:, 0, :], cs[:, 1, :], wr, ALU.mult))
                then(dve.tensor_tensor(c_[:, 1, :], cs[:, 0, :], wi, ALU.mult))
                then(dve.tensor_tensor(c_[:, 0, :], c_[:, 0, :], c_[:, 1, :], ALU.add))
                then(dve.scalar_tensor_tensor(c_[:, 0, :], c_[:, 0, :], 0.1, wi, ALU.mult, ALU.mult))
                then(dve.scalar_tensor_tensor(c_[:, 1, :], b1, 0.1 / TWO_PI, tn, ALU.mult, ALU.add))
                assert n[0] == F1_CHAIN

                def normalise(b, s, t):
                    m = b * TPB + t
                    if t == 0:
                        wait_pos(dve, zT_ps, b - 1)
                    o = dve.tensor_scalar(z[s][:, t, :], k.xt(m), k.mean[:, bass.ds(m, 1)],
                                          k.rstd[:, bass.ds(m, 1)], ALU.subtract, ALU.mult)
                    if t == TPB - 1:
                        o.then_inc(z_done, 1)

                def fraction(m, f):
                    r = f % HS
                    dve.wait_ge(u_done, m + 1)
                    dve.tensor_scalar(near[f % 2][:, :], u[r][:, :], MAGIC, MAGIC, ALU.add,
                                      ALU.subtract).then_inc(near_done, 1)
                    dve.wait_ge(near_done, m + 1)
                    dve.tensor_tensor(u[r][:, :], u[r][:, :], near[f % 2][:, :], ALU.subtract).then_inc(frac, 1)

                def mix(m, f, s):
                    r = f % HS
                    dve.wait_ge(sine, m + 1)
                    dve.scalar_tensor_tensor(q[s][:, f, :], u[r][:, :], c_[:, 0, f:f + 1],
                                             hb[r][:, :], ALU.mult, ALU.add).then_inc(mixed, 1)
                    dve.wait_ge(mixed, m + 1)
                    dve.tensor_scalar(q[s][:, f, :], q[s][:, f, :], par[:, 0, f:f + 1], 0.0,
                                      ALU.add, ALU.max).then_inc(q_done, 1)

                def hidden(b, s, between=lambda f: None):
                    for f in range(FC):
                        fraction(b * FC + f, f)
                        if f > 0:
                            mix(b * FC + f - 1, f - 1, s)
                        between(f)
                    mix(b * FC + FC - 1, FC - 1, s)

                def residual(b, t):
                    m = b * TPB + t
                    dve.wait_ge(y_ps, m + 1)
                    dve.tensor_tensor(k.xt(m), yb[t % 2][:, 0:D], k.xt(m), ALU.add).then_inc(x_added, 1)

                def statistics(b, t):
                    m = b * TPB + t
                    dve.wait_ge(x_added, m + 1)
                    norm.statistics(dve, m)

                def step(b, s, after):
                    dve.wait_ge(b_done, b + 1)

                    def between(f):
                        if f < TPB and after(2):
                            normalise(b + 2, s, f)
                        if f % 2 == 1:
                            residual(b, f // 2)
                        elif f > 0:
                            statistics(b, f // 2 - 1)
                    if after(1):
                        hidden(b + 1, 1 - s, between)
                    else:
                        for f in range(FC):
                            between(f)
                    statistics(b, TPB - 1)
                    norm.moments(dve, b)

                for b in range(2):
                    for t in range(TPB):
                        normalise(b, b, t)
                hidden(0, 0)
                over_batches_ahead(dve, step)

            @block.scalar
            def _(act):
                act.wait_ge(v, F1_CHAIN - 5)
                act.activation(cs[:, :, :], half_t[:, :, :], ACT.Sin, scale=TWO_PI).then_inc(sc, 1)
                act.wait_ge(v, F1_CHAIN)

                def copy(b, s):
                    act.wait_ge(zT_ps, b + 1)
                    act.activation(zT[s][:, :, :], bank[:, :, :], ACT.Copy).then_inc(zT_copied, 1)

                def turns(m, f):
                    act.wait_ge(h_ps, m + 1)
                    act.activation(u[f % HS][:, :], hb[f % HS][:, :], ACT.Identity, bias=c_[:, 1, f:f + 1],
                                   scale=0.1 / TWO_PI).then_inc(u_done, 1)

                def sines(m, f):
                    act.wait_ge(frac, m + 1)
                    act.activation(u[f % HS][:, :], u[f % HS][:, :], ACT.Sin, scale=TWO_PI).then_inc(sine, 1)

                def hidden(b, between=lambda f: None):
                    for f in range(FC):
                        turns(b * FC + f, f)
                        if f > 0:
                            sines(b * FC + f - 1, f - 1)
                        between(f)
                    sines(b * FC + FC - 1, FC - 1)

                copy(0, 0)
                copy(1, 1)
                k.ahead(act)
                hidden(0)

                def step(b, s, after):
                    if after(1):
                        hidden(b + 1, lambda f: copy(b + 2, s) if f == 6 and after(2) else None)
                over_batches_ahead(act, step)

            @block.tensor
            def _(pe):
                pe.wait_ge(w_in, 64)

                def turn(b, s):
                    pe.wait_ge(z_done, b + 1)
                    wait_pos(pe, zT_copied, b)
                    for c in range(DC):
                        for t in range(TPB):
                            mm = pe.transpose(bank[:, c, t * P:(t + 1) * P], z[s][:, t, c * P:(c + 1) * P], k.ident)
                    mm.then_inc(zT_ps, 1)

                def hidden(b, s, f):
                    m = b * FC + f
                    wait_pos(pe, mixed, m - HS + 1)
                    for kk in range(DC):
                        mm = pe.matmul(hb[f % HS][:, :], w1[:, kk, f * P:(f + 1) * P], zT[s][:, kk, :],
                                       start=(kk == 0), stop=(kk == DC - 1))
                    mm.then_inc(h_ps, 1)

                def second(b, s, f):
                    t, half = f // 2, f % 2
                    m = b * TPB + t
                    if half == 0:
                        if f == 0:
                            pe.wait_ge(q_done, (b + 1) * FC)
                        wait_pos(pe, x_added, m - 1)
                    for g in range(half * FC // 2, (half + 1) * FC // 2):
                        mm = pe.matmul(yb[t % 2][:, 0:D], q[s][:, g, t * P:(t + 1) * P], w2[:, g, :],
                                       start=(g == 0), stop=(g == FC - 1))
                    if half:
                        mm.then_inc(y_ps, 1)

                turn(0, 0)
                turn(1, 1)
                pe.wait_ge(zT_copied, 1)
                for f in range(FC):
                    hidden(0, 0, f)

                def step(b, s, after):
                    if after(1):
                        pe.wait_ge(zT_copied, b + 2)
                    for f in range(FC):
                        if after(1):
                            hidden(b + 1, 1 - s, f)
                        second(b, s, f)
                        if f == 5 and after(2):
                            turn(b + 2, s)
                over_batches_ahead(pe, step)


F1_CHAIN = 18


def window_attention(nc, k):
    ctx, sb, ps, sem = scoped(k)
    nm = "a2_"
    a = k.a
    with ctx:
        wa, wc, pt, ln = k.win
        lo, hi, lf = sb(nm + "lo", [P, NB]), sb(nm + "hi", [P, NB]), sb(nm + "lf", [P, NB])
        keep, k2, neg = (sb(nm + n, [P, NB, S]) for n in ("keep", "k2", "neg"))
        dist, gauss = sb(nm + "dist", [P, NB]), sb(nm + "gauss", [P, NB])
        cx = [sb(f"{nm}cx{s}", [P, DC, 2, S]) for s in range(2)]
        z = [sb(f"{nm}z{s}", [P, TPB, D]) for s in range(2)]
        zT = [sb(f"{nm}zT{s}", [P, DC, SEQ]) for s in range(2)]
        ac = [sb(f"{nm}ac{s}", [P, DC, S]) for s in range(2)]
        cc = [sb(f"{nm}cc{s}", [P, D]) for s in range(2)]
        pr = [sb(f"{nm}pr{s}", [P, TPB, S]) for s in range(2)]
        mx, sm, rc = (sb(nm + n, [P, TPB]) for n in ("mx", "sm", "rc"))
        pT = sb(nm + "pT", [P, TPB // 2 * P])
        th = [sb(f"{nm}th{s}", [P, TPB, D]) for s in range(2)]
        bank = ps(nm + "bank", [P, DC, SEQ])
        cb, sbk, tb = ps(nm + "cb", [P, 512]), ps(nm + "sb", [P, 512]), ps(nm + "tb", [P, 512])
        yb = [ps(f"{nm}yb{s}", [P, 512]) for s in range(2)]
        norm = Norm(k, sem, nm + "out")
        w_in, v, ga = k.win_in, sem(nm + "v"), sem(nm + "ga")
        cx_in = [sem(f"{nm}cx_in{s}") for s in range(2)]
        (z_done, zT_ps, zT_copied, c_ps, c_read, s_ps, s_read, s_masked, s_max, s_sub, e_done, s_sum, s_rec,
         p_done, t_ps, t_copied, y_ps, t_done, x_added) = (
            sem(nm + n) for n in ("z", "zT_ps", "zT_copied", "c_ps", "c_read", "s_ps", "s_read", "s_masked",
                                  "s_max", "s_sub", "e", "s_sum", "s_rec", "p", "t_ps", "t_copied", "y_ps",
                                  "tanh", "x"))
        with nc.Block() as block:
            @block.sync
            def _(sp):
                def step(b, s, first, last):
                    wait_pos(sp, c_ps, b - 1)
                    for j in range(2):
                        sp.dma_start(cx[s][:, :, j, :],
                                     a["ctxT"][bass.ds(b, 1)].rearrange("b p c l -> p (b c) l")).then_inc(cx_in[s], 16)
                over_batches(sp, step)

            @block.vector
            def _(dve):
                n = [0]

                def then(op):
                    n[0] += 1
                    op.then_inc(v, 1)
                    dve.wait_ge(v, n[0])

                dve.wait_ge(w_in, 64)
                idx = k.cst[:, None, C_L:C_L + S].to_broadcast([P, NB, S])
                bc = lambda t: t[:, :, None].to_broadcast([P, NB, S])
                then(dve.tensor_copy(lf[:, :], ln[:, :]))
                then(dve.tensor_scalar(lo[:, :], pt[:, :], WINDOW, 0.0, ALU.subtract, ALU.max))
                then(dve.scalar_tensor_tensor(hi[:, :], pt[:, :], WINDOW, lf[:, :], ALU.add, ALU.min))
                then(dve.tensor_tensor(keep[:, :, :], idx, bc(lo), ALU.is_ge))
                then(dve.tensor_tensor(k2[:, :, :], idx, bc(hi), ALU.is_le))
                then(dve.tensor_tensor(keep[:, :, :], keep[:, :, :], k2[:, :, :], ALU.mult))
                then(dve.tensor_scalar(neg[:, :, :], keep[:, :, :], 1.0, 1e9, ALU.subtract, ALU.mult))
                then(dve.tensor_scalar(dist[:, :], pt[:, :], k.cst[:, C_P:C_P + 1], None, ALU.subtract))
                then(dve.tensor_tensor(dist[:, :], dist[:, :], dist[:, :], ALU.mult))
                dve.wait_ge(ga, 1)

                def normalise(b, s):
                    wait_pos(dve, zT_ps, b - 1)
                    for t in range(TPB):
                        m = b * TPB + t
                        o = dve.tensor_scalar(z[s][:, t, :], k.xt(m), k.mean[:, bass.ds(m, 1)],
                                              k.rstd[:, bass.ds(m, 1)], ALU.subtract, ALU.mult)
                    o.then_inc(z_done, 1)

                def prepare(b, s):
                    dve.wait_ge(c_ps, b + 1)
                    dve.tensor_copy(ac[s][:, :, :], cb[:, 0:DC * S].rearrange("p (c l) -> p c l", c=DC))
                    dve.tensor_scalar(cc[s][:, :], cb[:, D:2 * D], gauss[:, bass.ds(b, 1)], None,
                                      ALU.mult).then_inc(c_read, 1)

                def softmax(b, s, between):
                    p = pr[s][:, :, :]
                    at = lambda t: t[:, bass.ds(b, 1), :].to_broadcast([P, TPB, S])
                    bt = lambda t: t[:, :, None].to_broadcast([P, TPB, S])
                    dve.wait_ge(s_ps, b + 1)
                    dve.tensor_tensor(p, sbk[:, 0:TPB * S].rearrange("p (t l) -> p t l", t=TPB), at(keep),
                                      ALU.mult).then_inc(s_read, 1)
                    dve.wait_ge(s_read, b + 1)
                    dve.tensor_tensor(p, p, at(neg), ALU.add).then_inc(s_masked, 1)
                    dve.wait_ge(s_masked, b + 1)
                    dve.tensor_reduce(mx[:, :], p, AX.X, ALU.max).then_inc(s_max, 1)
                    dve.wait_ge(s_max, b + 1)
                    dve.tensor_tensor(p, p, bt(mx), ALU.subtract).then_inc(s_sub, 1)
                    between()
                    dve.wait_ge(e_done, b + 1)
                    dve.tensor_reduce(sm[:, :], p, AX.X, ALU.add).then_inc(s_sum, 1)
                    dve.wait_ge(s_sum, b + 1)
                    dve.reciprocal(rc[:, :], sm[:, :]).then_inc(s_rec, 1)
                    dve.wait_ge(s_rec, b + 1)
                    dve.tensor_tensor(p, p, bt(rc), ALU.mult).then_inc(p_done, 1)

                def residual(b, s):
                    dve.wait_ge(t_done, (b + 1) * TPB)
                    xs = k.x[:, bass.ds(b * (TPB * D), TPB * D)].rearrange("p (t d) -> p t d", t=TPB)
                    dve.tensor_tensor(xs, th[s][:, :, :], xs, ALU.add).then_inc(x_added, 1)

                def statistics(b):
                    dve.wait_ge(x_added, b + 1)
                    for t in range(TPB):
                        norm.statistics(dve, b * TPB + t)
                    norm.moments(dve, b)

                def step(b, s, after):
                    softmax(b, s, lambda: None if is_first(b) else residual(b - 1, 1 - s))
                    if after(1):
                        prepare(b + 1, 1 - s)
                    if after(2):
                        normalise(b + 2, s)
                    if not is_first(b):
                        statistics(b - 1)

                normalise(0, 0)
                normalise(1, 1)
                prepare(0, 0)
                over_batches_ahead(dve, step)
                residual(NB - 1, 1)
                statistics(NB - 1)

            @block.gpsimd
            def _(pool):
                with pool.Fori(0, NB) as b:
                    norm.root(pool, b)

            @block.scalar
            def _(act):
                act.wait_ge(v, 9)
                act.activation(gauss[:, :], dist[:, :], ACT.Exp, scale=-1.0 / DEV_POW).then_inc(ga, 1)

                def copy(b, s):
                    act.wait_ge(zT_ps, b + 1)
                    wait_pos(act, y_ps, (b - 1) * TPB)
                    act.activation(zT[s][:, :, :], bank[:, :, :], ACT.Copy).then_inc(zT_copied, 1)

                def step(b, s, after):
                    act.wait_ge(s_sub, b + 1)
                    act.activation(pr[s][:, :, :], pr[s][:, :, :], ACT.Exp).then_inc(e_done, 1)
                    if after(1):
                        copy(b + 1, 1 - s)
                    act.wait_ge(t_ps, b + 1)
                    act.activation(pT[:, :], tb[:, 0:TPB // 2 * P], ACT.Copy).then_inc(t_copied, 1)
                    wait_pos(act, x_added, b - 1)
                    for t in range(TPB):
                        m = b * TPB + t
                        act.wait_ge(y_ps, m + 1)
                        act.activation(th[s][:, t, :], yb[t % 2][:, 0:D], ACT.Tanh).then_inc(t_done, 1)

                copy(0, 0)
                k.ahead(act)
                over_batches_ahead(act, step)

            @block.tensor
            def _(pe):
                pe.wait_ge(w_in, 64)

                def turn(b, s):
                    pe.wait_ge(z_done, b + 1)
                    wait_pos(pe, zT_copied, b)
                    for c in range(DC):
                        for t in range(TPB):
                            mm = pe.transpose(bank[:, c, t * P:(t + 1) * P], z[s][:, t, c * P:(c + 1) * P], k.ident)
                    mm.then_inc(zT_ps, 1)

                def prepare(b, s):
                    pe.wait_ge(cx_in[s], 16 * b + (16 if s else 32))
                    wait_pos(pe, c_read, b)
                    for c in range(DC):
                        for kk in range(DC):
                            pe.matmul(cb[:, c * S:(c + 1) * S], wa[:, kk, c * P:(c + 1) * P], cx[s][:, kk, 0, :],
                                      start=(kk == 0), stop=(kk == DC - 1))
                    for kk in range(DC):
                        mm = pe.matmul(cb[:, D:2 * D], cx[s][:, kk, :, :].rearrange("p j l -> p (j l)"), wc[:, kk, :],
                                       start=(kk == 0), stop=(kk == DC - 1))
                    mm.then_inc(c_ps, 1)

                def scores(b, s):
                    pe.wait_ge(zT_copied, b + 1)
                    pe.wait_ge(c_read, b + 1)
                    wait_pos(pe, s_read, b)
                    for t in range(TPB):
                        for kk in range(DC):
                            mm = pe.matmul(sbk[:, t * S:(t + 1) * S], zT[s][:, kk, t * P:(t + 1) * P], ac[s][:, kk, :],
                                           start=(kk == 0), stop=(kk == DC - 1))
                    mm.then_inc(s_ps, 1)

                def step(b, s, after):
                    if after(1):
                        turn(b + 1, 1 - s)
                        prepare(b + 1, 1 - s)
                    pe.wait_ge(p_done, b + 1)
                    for g in range(TPB // 2):
                        mm = pe.transpose(tb[:, g * P:(g + 1) * P],
                                          pr[s][:, 2 * g:2 * g + 2, :].rearrange("p t l -> p (t l)"), k.ident)
                    mm.then_inc(t_ps, 1)
                    if after(1):
                        scores(b + 1, 1 - s)
                    pe.wait_ge(t_copied, b + 1)
                    for t in range(TPB):
                        m = b * TPB + t
                        wait_pos(pe, t_done, m - 1)
                        for kk in range(DC):
                            pe.matmul(yb[t % 2][:, 0:D], zT[s][:, kk, t * P:(t + 1) * P], wc[:, DC + kk, :],
                                      start=(kk == 0), stop=False)
                        half = slice(t % 2 * S, (t % 2 + 1) * S)
                        pe.matmul(yb[t % 2][:, 0:D], pT[half, t // 2 * P:(t // 2 + 1) * P], cc[s][half, :],
                                  start=False, stop=True).then_inc(y_ps, 1)

                turn(0, 0)
                prepare(0, 0)
                scores(0, 0)
                over_batches_ahead(pe, step)


def ternary_ffn(nc, k, out):
    ctx, sb, ps, sem = scoped(k)
    nm = "f3_"
    a = k.a
    FC = F3 // P
    with ctx:
        z = [sb(f"{nm}z{s}", [P, TPB, D]) for s in range(2)]
        xq = [sb(f"{nm}xq{s}", [P, TPB, D], BF16) for s in range(2)]
        xT = [sb(f"{nm}xT{s}", [P, DC, SEQ], BF16) for s in range(2)]
        am, sc, rc = (sb(nm + n, [P, TPB]) for n in ("am", "sc", "rc"))
        sg = [sb(f"{nm}sg{s}", [P, TPB]) for s in range(2)]
        su = [sb(f"{nm}su{s}", [P, TPB]) for s in range(2)]
        g_ = [sb(f"{nm}g{s}", [P, F3]) for s in range(2)]
        h = [sb(f"{nm}h{s}", [P, F3]) for s in range(2)]
        hq = [sb(f"{nm}hq{s}", [P, F3], BF16) for s in range(2)]
        hm, hr, hs, hd = ([sb(f"{nm}{n}{s}", [P, 1]) for s in range(2)] for n in ("hm", "hr", "hs", "hd"))
        hT = [sb(f"{nm}hT{s}", [P, FC, P], BF16) for s in range(2)]
        ident = sb(nm + "ident", [P, P], BF16)
        wq = {c: sb(nm + "wq" + c, [P, 2 * F3], BF16) for c in "gud"}
        wsum, wmean, wscale = (sb(nm + n, [P, 3]) for n in ("wsum", "wmean", "wscale"))
        xb = ps(nm + "xb", [P, DC, SEQ], BF16)
        gb, ub = ps(nm + "gb", [P, F3]), ps(nm + "ub", [P, F3])
        hb = ps(nm + "hb", [P, FC, P], BF16)
        yb = [ps(f"{nm}yb{s}", [P, 512]) for s in range(2)]
        w_in, v, tot_ps = k.f3_in, sem(nm + "v"), sem(nm + "tot")
        (z_done, z_max, z_clip, z_rec, z_scale, z_mul, xq_done, x_ps, x_copied, g_ps, g_done, h_done, h_max,
         h_clip, h_rec, h_scale, h_mul, hq_done, h_tp, h_copied, y_ps, x_added) = (
            sem(nm + n) for n in ("z", "z_max", "z_clip", "z_rec", "z_scale", "z_mul", "xq", "x_ps", "x_copied",
                                  "g_ps", "g_done", "h", "h_max", "h_clip", "h_rec", "h_scale", "h_mul", "hq",
                                  "h_tp", "h_copied", "y_ps", "x"))
        stored, u_ps = sem(nm + "stored"), sem(nm + "u_ps")
        N3 = 2 * F3
        with ExitStack() as wctx:
            raw = k.f3_raw
            tb = yb[0]
            with nc.Block() as block:
                @block.vector
                def _(dve):
                    n = [0]

                    def then(op):
                        n[0] += 1
                        op.then_inc(v, 1)
                        dve.wait_ge(v, n[0])

                    dve.wait_ge(w_in, 48)
                    for j in range(3):
                        dve.tensor_reduce(wsum[:, j:j + 1], raw[j][:, :], AX.X, ALU.add,
                                          apply_absolute_value=True).then_inc(v, 1)
                    n[0] = 3
                    dve.wait_ge(tot_ps, 1)
                    then(dve.tensor_scalar(wmean[:, :], tb[:, 0:3], 1.0 / (D * F3), 1e-5, ALU.mult, ALU.max))
                    then(dve.reciprocal(wscale[:, :], wmean[:, :]))
                    for j, c in enumerate("gud"):
                        then(dve.tensor_scalar(raw[j][:, :], raw[j][:, :], wscale[:, j:j + 1], MAGIC,
                                               ALU.mult, ALU.add))
                        then(dve.tensor_scalar(raw[j][:, :], raw[j][:, :], MAGIC, 1.0, ALU.subtract, ALU.min))
                        dve.tensor_scalar(wq[c][:, :], raw[j][:, :], -1.0, None, ALU.max)
                    dve.tensor_copy(ident[:, :], k.ident)

                @block.tensor
                def _(pe):
                    pe.wait_ge(v, 3)
                    pe.matmul(tb[:, 0:3], k.cst[:, C_ONE:C_ONE + P], wsum[:, :], start=True, stop=True).then_inc(tot_ps, 1)

        wg = wq["g"][:, :].rearrange("p (c f) -> p c f", c=DC)
        wu = wq["u"][:, :].rearrange("p (c f) -> p c f", c=DC)
        wd = wq["d"][:, :].rearrange("p (c f) -> p c f", c=FC)
        with nc.Block() as block:
            @block.vector
            def _(dve):
                def quantise(b, s):
                    wait_pos(dve, x_ps, b - 1)
                    for t in range(TPB):
                        m = b * TPB + t
                        o = dve.tensor_scalar(z[s][:, t, :], k.xt(m), k.mean[:, bass.ds(m, 1)],
                                              k.rstd[:, bass.ds(m, 1)], ALU.subtract, ALU.mult)
                    o.then_inc(z_done, 1)
                    dve.wait_ge(z_done, b + 1)
                    dve.tensor_reduce(am[:, :], z[s][:, :, :], AX.X, ALU.max, apply_absolute_value=True).then_inc(z_max, 1)
                    dve.wait_ge(z_max, b + 1)
                    dve.tensor_scalar(am[:, :], am[:, :], 1e-5, None, ALU.max).then_inc(z_clip, 1)
                    dve.wait_ge(z_clip, b + 1)
                    dve.reciprocal(rc[:, :], am[:, :]).then_inc(z_rec, 1)
                    dve.tensor_scalar(sg[s][:, :], am[:, :], 1.0 / 127.0, wmean[:, 0:1], ALU.mult, ALU.mult)
                    dve.tensor_scalar(su[s][:, :], am[:, :], 1.0 / 127.0, wmean[:, 1:2], ALU.mult, ALU.mult)
                    dve.wait_ge(z_rec, b + 1)
                    dve.tensor_scalar(sc[:, :], rc[:, :], 127.0, None, ALU.mult).then_inc(z_scale, 1)
                    dve.wait_ge(z_scale, b + 1)
                    for t in range(TPB):
                        o = dve.tensor_scalar(z[s][:, t, :], z[s][:, t, :], sc[:, t:t + 1], MAGIC, ALU.mult, ALU.add)
                    o.then_inc(z_mul, 1)
                    dve.wait_ge(z_mul, b + 1)
                    dve.tensor_scalar(xq[s][:, :, :], z[s][:, :, :], MAGIC, 127.0, ALU.subtract, ALU.min).then_inc(xq_done, 1)

                def hidden(m, t, s):
                    u = t % 2
                    dve.wait_ge(g_done, m + 1)
                    dve.wait_ge(u_ps, m + 1)
                    dve.scalar_tensor_tensor(h[u][:, :], ub[:, :], su[s][:, t:t + 1], g_[u][:, :],
                                             ALU.mult, ALU.mult).then_inc(h_done, 1)
                    dve.wait_ge(h_done, m + 1)
                    dve.tensor_reduce(hm[u][:, :], h[u][:, :], AX.X, ALU.max, apply_absolute_value=True).then_inc(h_max, 1)
                    dve.wait_ge(h_max, m + 1)
                    dve.tensor_scalar(hm[u][:, :], hm[u][:, :], 1e-5, None, ALU.max).then_inc(h_clip, 1)
                    dve.wait_ge(h_clip, m + 1)
                    dve.reciprocal(hr[u][:, :], hm[u][:, :]).then_inc(h_rec, 1)
                    dve.tensor_scalar(hd[u][:, :], hm[u][:, :], 1.0 / 127.0, wmean[:, 2:3], ALU.mult, ALU.mult)
                    dve.wait_ge(h_rec, m + 1)
                    dve.tensor_scalar(hs[u][:, :], hr[u][:, :], 127.0, None, ALU.mult).then_inc(h_scale, 1)
                    dve.wait_ge(h_scale, m + 1)
                    dve.tensor_scalar(h[u][:, :], h[u][:, :], hs[u][:, :], MAGIC, ALU.mult, ALU.add).then_inc(h_mul, 1)
                    dve.wait_ge(h_mul, m + 1)
                    dve.tensor_scalar(hq[u][:, :], h[u][:, :], MAGIC, 127.0, ALU.subtract, ALU.min).then_inc(hq_done, 1)

                def residual(m, t):
                    dve.wait_ge(y_ps, m + 1)
                    dve.scalar_tensor_tensor(k.xt(m), yb[t % 2][:, 0:D], hd[t % 2][:, :], k.xt(m),
                                             ALU.mult, ALU.add).then_inc(x_added, 1)

                def step(b, s, first, last):
                    for t in range(TPB):
                        m = b * TPB + t
                        if t == 0 and not last:
                            quantise(b + 1, 1 - s)
                        hidden(m, t, s)
                        if not (first and t == 0):
                            residual(m - 1, t - 1)

                quantise(0, 0)
                over_batches(dve, step)
                residual(NT - 1, TPB - 1)

            @block.scalar
            def _(act):
                def copy(b, s):
                    act.wait_ge(x_ps, b + 1)
                    act.activation(xT[s][:, :, :], xb[:, :, :], ACT.Copy).then_inc(x_copied, 1)

                def silu(m, t, s):
                    act.wait_ge(g_ps, m + 1)
                    act.activation(g_[t % 2][:, :], gb[:, :], ACT.Silu, scale=sg[s][:, t:t + 1]).then_inc(g_done, 1)

                def step(b, s, first, last):
                    for t in range(TPB):
                        m = b * TPB + t
                        act.wait_ge(h_tp, m + 1)
                        act.activation(hT[t % 2][:, :, :], hb[:, :, :], ACT.Copy).then_inc(h_copied, 1)
                        if t < TPB - 2:
                            silu(m + 2, t + 2, s)
                        elif not last:
                            silu(m + 2, t + 2 - TPB, 1 - s)
                        if t == 1 and not last:
                            copy(b + 1, 1 - s)

                copy(0, 0)
                silu(0, 0, 0)
                silu(1, 1, 0)
                over_batches(act, step)

            @block.tensor
            def _(pe):
                def turn(b, s):
                    pe.wait_ge(xq_done, b + 1)
                    wait_pos(pe, x_copied, b)
                    for c in range(DC):
                        for t in range(TPB):
                            mm = pe.transpose(xb[:, c, t * P:(t + 1) * P], xq[s][:, t, c * P:(c + 1) * P], ident[:, :])
                    mm.then_inc(x_ps, 1)

                def first_layers(m, t, s):
                    for w, dst, left, filled in ((wg, gb, g_done, g_ps), (wu, ub, h_done, u_ps)):
                        wait_pos(pe, left, m)
                        for j in range(F3 // 512):
                            for c in range(DC):
                                mm = pe.matmul(dst[:, j * 512:(j + 1) * 512], xT[s][:, c, t * P:(t + 1) * P],
                                               w[:, c, j * 512:(j + 1) * 512], start=(c == 0), stop=(c == DC - 1))
                        mm.then_inc(filled, 1)

                def step(b, s, first, last):
                    for t in range(TPB):
                        m = b * TPB + t
                        pe.wait_ge(hq_done, m + 1)
                        wait_pos(pe, h_copied, m)
                        for f in range(FC):
                            mm = pe.transpose(hb[:, f, :], hq[t % 2][:, f * P:(f + 1) * P], ident[:, :])
                        mm.then_inc(h_tp, 1)
                        if t < TPB - 2:
                            first_layers(m + 2, t + 2, s)
                        elif not last:
                            if t == 2:
                                pe.wait_ge(x_copied, b + 2)
                            first_layers(m + 2, t + 2 - TPB, 1 - s)
                        if t == 1 and not last:
                            turn(b + 1, 1 - s)
                        pe.wait_ge(h_copied, m + 1)
                        wait_pos(pe, x_added, m - 1)
                        for f in range(FC):
                            mm = pe.matmul(yb[t % 2][:, 0:D], hT[t % 2][:, f, :], wd[:, f, :],
                                           start=(f == 0), stop=(f == FC - 1))
                        mm.then_inc(y_ps, 1)

                turn(0, 0)
                pe.wait_ge(x_copied, 1)
                first_layers(0, 0, 0)
                first_layers(1, 1, 0)
                over_batches(pe, step)

            @block.sync
            def _(sp):
                def step(b, s, first, last):
                    sp.wait_ge(x_added, b * TPB + TPB)
                    xs = k.x[:, bass.ds(b * (TPB * D), TPB * D)].rearrange("p (t d) -> p t d", t=TPB)
                    sp.dma_start(out[bass.ds(b, 1)].rearrange("b (t p) d -> p (b t) d", p=P), xs).then_inc(stored, 16)
                over_batches(sp, step)
                sp.wait_ge(stored, 16 * NB)


def load_early(nc, k, load):
    with nc.Block() as block:
        @block.sync
        def _(sp):
            load(sp, k)


def store_stage(nc, k, out):
    ctx, sb, ps, sem = scoped(k)
    with ctx:
        stored = sem("stored")
        with nc.Block() as block:
            @block.sync
            def _(sp):
                for b in range(NB):
                    sp.dma_start(out[b].rearrange("(t p) d -> p t d", p=P),
                                 k.x[:, b * TPB * D:(b + 1) * TPB * D].rearrange("p (t d) -> p t d", t=TPB)
                                 ).then_inc(stored, 16)
                sp.wait_ge(stored, 16 * NB)


def build(nc, a, out, stages="a0 m0 a1 f1 w2 m2 a3 f3"):
    nothing = lambda sp: None
    with ExitStack() as ctx:
        k = Core(nc, ctx, a)
        todo = stages.split()
        layers = [int(st[1]) for st in todo if st[0] == "a"]
        k.first_att = layers[0] if layers else None
        load_stage(nc, k)
        weights = ExitStack()
        room = lambda n, words: weights.enter_context(nc.sbuf_tensor(n, [P, words], F32))

        def run(st, ahead=nothing):
            k.ahead = ahead
            if k.normed or k.arriving:
                clean_stage(nc, k)
            else:
                ln_scalars(nc, k, st)
            k.normed = st != "m2"
            if st[0] == "a":
                attention(nc, k, int(st[1]))
            elif st[0] == "m":
                after = [L for L in layers if L > int(st[1])]
                k.next_att = after[0] if after and layers[0] <= int(st[1]) else None
                mixture(nc, k, int(st[1]))
            elif st == "f1":
                quantum_ffn(nc, k)
            elif st == "w2":
                window_attention(nc, k)
            elif st == "f3":
                ternary_ffn(nc, k, out)

        def m0_weights(eng):
            load_first_layers(eng, k, 0, range(E))
            load_second_layers(eng, k, 0)

        def first_stage(st):
            return todo[0] == st

        if "m0" in todo:
            k.w1, k.w2 = room("m0_w1", E * DC * F0), room("m0_w2", E * F0 // P * D)
            k.w_count = 16 * 2 * E
            k.late = m0_weights if first_stage("m0") else nothing
        if "a0" in todo:
            run("a0", m0_weights if "m0" in todo else nothing)
        if "m0" in todo:
            run("m0")
            weights.close()
        if "m2" in todo:
            before = k.w_count if "m0" in todo else 0
            k.w_count = before + 16 * 2 * E
            k.w2 = room("m2_w2", E * F2 // P * D)
        with ExitStack() as small:
            sb = lambda n, s, d=F32: small.enter_context(nc.sbuf_tensor(n, s, d))
            k.f1 = (sb("f1_w1", [P, DC, F1]), sb("f1_w2", [P, F1 // P, D]), sb("f1_par", [P, 4, F1 // P]),
                    sb("f1_b2", [P, D]))
            k.win = (sb("a2_wa", [P, DC, D]), sb("a2_wc", [P, 2 * DC, D]), sb("a2_pt", [P, NB]),
                     sb("a2_ln", [P, NB], I32))
            if todo[0] in ("f1", "w2"):
                load_early(nc, k, (load_quantum if todo[0] == "f1" else load_window))

            def a1_ahead(eng):
                load_quantum(eng, k)
                if "m2" in todo:
                    load_second_layers(eng, k, 2)
            if "a1" in todo:
                run("a1", a1_ahead)
            if "f1" in todo:
                run("f1", (lambda eng: load_window(eng, k)) if "w2" in todo else nothing)
            if "w2" in todo:
                run("w2")
        if "m2" in todo:
            k.w1 = room("m2_w1", E * DC * F2)

            def m2_late(eng):
                if "a1" not in todo:
                    load_second_layers(eng, k, 2)
                load_first_layers(eng, k, 2, range(E))
            k.late = m2_late
            run("m2")
            weights.close()
        with ExitStack() as small:
            k.f3_raw = [small.enter_context(nc.sbuf_tensor("f3_raw" + c, [P, 2 * F3], F32)) for c in "gud"]
            if todo[0] == "f3":
                load_early(nc, k, load_ternary)
            if "a3" in todo:
                run("a3", (lambda eng: load_ternary(eng, k)) if "f3" in todo else nothing)
            if "f3" in todo:
                run("f3")
        if "f3" not in todo:
            store_stage(nc, k, out)


def chunked(w):
    return np.ascontiguousarray(np.asarray(w).reshape(-1, P, w.shape[-1]).transpose(1, 0, 2))


def layout(inputs):
    i = {n: np.asarray(v) for n, v in inputs.items()}
    a = {"x": i["x"], "cst": constants(), "tau": i["condB_tau"], "delta": i["fside_BxS2_0"].reshape(-1)}
    a["ctxT"] = np.ascontiguousarray(i["ctx_1024"].reshape(NB, S, DC, P).transpose(0, 3, 2, 1))
    for L in (0, 1, 3):
        for c in "qkvo":
            a[f"L{L}_xcond_W{c}"] = chunked(i[f"L{L}_xcond_W{c}"].T)
        for c in "qk":
            a[f"L{L}_xcond_b{c}"] = np.ascontiguousarray(i[f"L{L}_xcond_b{c}"].reshape(DC, P).T)
        for c in "vo":
            a[f"L{L}_xcond_b{c}"] = i[f"L{L}_xcond_b{c}"]
    a["L0_gate"], a["L2_gate"] = chunked(i["L0_ffn_gate_w"]), chunked(i["L2_ffn_router_w"].T)
    for L, w1, w2 in ((0, i["L0_ffn_w1"], i["L0_ffn_w2"]),
                      (2, i["L2_ffn_w1"].transpose(0, 2, 1), i["L2_ffn_w2"].transpose(0, 2, 1))):
        for n, w in (("w1", w1), ("w2", w2)):
            w = w.reshape(E, -1, P, w.shape[-1]).transpose(2, 0, 1, 3)
            a[f"L{L}_ffn_{n}"] = np.ascontiguousarray(w.reshape(P, E, -1))
        a[f"L{L}_ffn_b2"] = i[f"L{L}_ffn_b2"].reshape(-1)
    for n, v in (("L0_ffn_bt", i["L0_ffn_ln1_b"]), ("L0_ffn_gt", i["L0_ffn_ln1_g"]), ("L2_ffn_bt", i["L2_ffn_b1"])):
        a[n] = np.ascontiguousarray(v.reshape(-1, P).T)
    a["L0_ffn_b1"] = i["L0_ffn_b1"].reshape(-1)
    a["L1_ffn_W1"], a["L1_ffn_W2"] = chunked(i["L1_ffn_W1"]), chunked(i["L1_ffn_W2"])
    a["L1_ffn_par"] = np.ascontiguousarray(np.stack([
        i["L1_ffn_" + n].reshape(-1, P) for n in ("b1", "quantum_phases", "quantum_weights_real",
                                                  "quantum_weights_imag")]).transpose(2, 0, 1))
    a["L1_ffn_b2"] = i["L1_ffn_b2"]
    a["L2_Wa"], a["L2_Wc"] = chunked(i["L2_xcond_W_a"].T), chunked(i["L2_xcond_W_c"].T)
    a["pt"], a["len"] = i["condB_pt"], i["_lenS2"]
    for n in ("gate", "up", "down"):
        a["L3_ffn_w_" + n] = chunked(i["L3_ffn_w_" + n].T).reshape(P, -1)
    a["L0_ffn_ln_g"], a["L0_ffn_ln_b"] = i["L0_ffn_ln_g"], i["L0_ffn_ln_b"]
    return a


def kernel(**inputs):
    import concourse.bacc as bacc
    from concourse.bass_utils import run_bass_kernel_spmd

    nc = bacc.Bacc("TRN2", target_bir_lowering=False, num_devices=1)
    arrays = {f"in_{n}": v for n, v in layout(inputs).items()}
    a = {n[3:]: nc.dram_tensor(n, v.shape, mybir.dt.from_np(v.dtype), kind="ExternalInput").ap()
         for n, v in arrays.items()}
    out = nc.dram_tensor("out_x", (NB, SEQ, D), F32, kind="ExternalOutput").ap()
    build(nc, a, out)
    r = run_bass_kernel_spmd(nc, [arrays], core_ids=[0])
    return r.results[0]["out_x"]
```
